# Optimizing a Trainium2 kernel written in Bass

```python
import numpy as np
import jax
import jax.numpy as jnp

def _softmax(x, axis=-1):
    return jax.nn.softmax(x, axis=axis)

def _gelu(x):
    return jax.nn.gelu(x, approximate=True)

def _silu(x):
    return jax.nn.silu(x)

def _sigmoid(x):
    return jax.nn.sigmoid(x)

def _layernorm(x, axis=-1, eps=1e-05):
    m = jnp.mean(x, axis=axis, keepdims=True)
    v = jnp.var(x, axis=axis, keepdims=True)
    return (x - m) / jnp.sqrt(v + eps)

def _scatter_add(tgt, idx, src, axis=0):
    return tgt.at[idx].add(src)

def _segment_sum(src, seg, n):
    return jax.ops.segment_sum(src, seg, n)
kernel_name = 'mk_prb_d2_jaxref_r8_04f8fb'

def setup_inputs(seed: int=0):
    np.random.seed(seed)
    _w = jnp.asarray

    def _L0_attn_setup():
        import jax, jax.numpy as jnp
        import numpy as np
        BSZ, SEQ, EMBED = (2, 512, 128)
        NUM_HEADS = 16
        HEAD_DIM = EMBED // NUM_HEADS
        WINDOW = 32

        def _blocks3(x, nb, w):
            b = x.shape[0]
            xb = x.reshape(b, nb + 2, w, NUM_HEADS, HEAD_DIM)
            return jnp.concatenate([xb[:, i:i + nb] for i in range(3)], axis=2)
        key = jax.random.key(seed)
        ks = jax.random.split(key, 7)
        s = 1.0 / np.sqrt(EMBED)
        return {'hidden_states': jax.random.normal(ks[0], (BSZ, SEQ, EMBED), jnp.float32), 'Wq': jax.random.normal(ks[1], (EMBED, EMBED), jnp.float32) * s, 'bq': jnp.zeros((EMBED,), jnp.float32), 'Wk': jax.random.normal(ks[2], (EMBED, EMBED), jnp.float32) * s, 'bk': jnp.zeros((EMBED,), jnp.float32), 'Wv': jax.random.normal(ks[3], (EMBED, EMBED), jnp.float32) * s, 'bv': jnp.zeros((EMBED,), jnp.float32)}
    _L0_attn_in = _L0_attn_setup()

    def _L0_ffn_setup():
        import jax, jax.numpy as jnp
        import numpy as np
        DIM = 128
        HIDDEN = 512
        E = 8
        B, S = (2, 512)
        key = jax.random.key(seed)
        ks = jax.random.split(key, 8)
        sd = 1.0 / np.sqrt(DIM)
        sh = 1.0 / np.sqrt(HIDDEN)
        return {'x': jax.random.normal(ks[0], (B, S, DIM), dtype=jnp.float32), 'router_w': jax.random.uniform(ks[1], (DIM, E), jnp.float32, -sd, sd), 'router_b': jax.random.uniform(ks[2], (E,), jnp.float32, -sd, sd), 'w1': jax.random.uniform(ks[3], (E, DIM, 2 * HIDDEN), jnp.float32, -sd, sd), 'b1': jax.random.uniform(ks[4], (E, 2 * HIDDEN), jnp.float32, -sd, sd), 'w2': jax.random.uniform(ks[5], (E, HIDDEN, DIM), jnp.float32, -sh, sh), 'b2': jax.random.uniform(ks[6], (E, DIM), jnp.float32, -sh, sh)}
    _L0_ffn_in = _L0_ffn_setup()

    def _L1_attn_setup():
        import jax, jax.numpy as jnp
        import numpy as np
        EMBED_DIM = 128
        NUM_HEADS = 16
        DEPTH = 12
        HEAD_DIM = EMBED_DIM // NUM_HEADS // 2
        LAMBDA_INIT = float(0.8 - 0.6 * np.exp(-0.3 * DEPTH))
        B, T = (2, 256)
        key = jax.random.key(seed)
        ks = jax.random.split(key, 10)
        s = 0.02
        return {'query': jax.random.normal(ks[0], (B, T, EMBED_DIM), jnp.float32), 'Wq': jax.random.normal(ks[1], (EMBED_DIM, EMBED_DIM), jnp.float32) * s, 'Wk': jax.random.normal(ks[2], (EMBED_DIM, EMBED_DIM), jnp.float32) * s, 'Wv': jax.random.normal(ks[3], (EMBED_DIM, EMBED_DIM), jnp.float32) * s, 'Wo': jax.random.normal(ks[4], (EMBED_DIM, EMBED_DIM), jnp.float32) * s, 'lambda_q1': jax.random.normal(ks[5], (HEAD_DIM,), jnp.float32) * 0.1, 'lambda_k1': jax.random.normal(ks[6], (HEAD_DIM,), jnp.float32) * 0.1, 'lambda_q2': jax.random.normal(ks[7], (HEAD_DIM,), jnp.float32) * 0.1, 'lambda_k2': jax.random.normal(ks[8], (HEAD_DIM,), jnp.float32) * 0.1, 'subln_w': jnp.ones((2 * HEAD_DIM,), jnp.float32)}
    _L1_attn_in = _L1_attn_setup()

    def _L1_ffn_setup():
        import jax, jax.numpy as jnp
        import numpy as np
        NUM_EXPERTS = 8
        NUM_SELECTED = 2
        EXPERT_CAPACITY = 64
        NUM_GROUPS = 8

        def _routing(xg, w_router):
            G, T, H = xg.shape
            logits = jnp.einsum('gth,he->gte', xg, w_router)
            probs = jax.nn.softmax(logits, axis=-1)
            _gate, idx = jax.lax.top_k(probs, NUM_SELECTED)
            idx_kt = jnp.swapaxes(idx, 1, 2).reshape(G, -1)
            expert_mask = jax.nn.one_hot(idx_kt, NUM_EXPERTS, dtype=jnp.int32)
            priority = jnp.cumsum(expert_mask, axis=1) * expert_mask - 1
            priority = priority.reshape(G, NUM_SELECTED, T, NUM_EXPERTS)
            priority = jnp.swapaxes(priority, 1, 2).max(axis=2)
            dispatch = jax.nn.one_hot(priority, EXPERT_CAPACITY, dtype=xg.dtype)
            combine = probs[..., None] * dispatch
            return (dispatch, combine)
        key = jax.random.key(seed)
        k1, k2, k3, k4 = jax.random.split(key, 4)
        B, S, H, F = (8, 256, 128, 512)
        return {'x': jax.random.normal(k1, (B, S, H), jnp.float32), 'w_router': jax.random.normal(k2, (H, NUM_EXPERTS), jnp.float32) * 0.02, 'wi': jax.random.normal(k3, (NUM_EXPERTS, H, F), jnp.float32) * 0.02, 'wo': jax.random.normal(k4, (NUM_EXPERTS, F, H), jnp.float32) * 0.02}
    _L1_ffn_in = _L1_ffn_setup()
    _d = {'L0_attn_hidden_states': _L0_attn_in['hidden_states'], 'L0_attn_Wq': _L0_attn_in['Wq'], 'L0_attn_bq': _L0_attn_in['bq'], 'L0_attn_Wk': _L0_attn_in['Wk'], 'L0_attn_bk': _L0_attn_in['bk'], 'L0_attn_Wv': _L0_attn_in['Wv'], 'L0_attn_bv': _L0_attn_in['bv'], 'L0_ffn_router_w': _L0_ffn_in['router_w'], 'L0_ffn_router_b': _L0_ffn_in['router_b'], 'L0_ffn_w1': _L0_ffn_in['w1'], 'L0_ffn_b1': _L0_ffn_in['b1'], 'L0_ffn_w2': _L0_ffn_in['w2'], 'L0_ffn_b2': _L0_ffn_in['b2'], 'L1_attn_Wq': _L1_attn_in['Wq'], 'L1_attn_Wk': _L1_attn_in['Wk'], 'L1_attn_Wv': _L1_attn_in['Wv'], 'L1_attn_Wo': _L1_attn_in['Wo'], 'L1_attn_lambda_q1': _L1_attn_in['lambda_q1'], 'L1_attn_lambda_k1': _L1_attn_in['lambda_k1'], 'L1_attn_lambda_q2': _L1_attn_in['lambda_q2'], 'L1_attn_lambda_k2': _L1_attn_in['lambda_k2'], 'L1_attn_subln_w': _L1_attn_in['subln_w'], 'L1_ffn_w_router': _L1_ffn_in['w_router'], 'L1_ffn_wi': _L1_ffn_in['wi'], 'L1_ffn_wo': _L1_ffn_in['wo']}
    _x0 = _d['L0_attn_hidden_states']
    _d['L0_attn_hidden_states'] = jax.random.normal(jax.random.fold_in(jax.random.key(seed), 1), (8, 256, 128), dtype=_x0.dtype)
    del _x0
    return _d

def reference(L0_attn_hidden_states, L0_attn_Wq, L0_attn_bq, L0_attn_Wk, L0_attn_bk, L0_attn_Wv, L0_attn_bv, L0_ffn_router_w, L0_ffn_router_b, L0_ffn_w1, L0_ffn_b1, L0_ffn_w2, L0_ffn_b2, L1_attn_Wq, L1_attn_Wk, L1_attn_Wv, L1_attn_Wo, L1_attn_lambda_q1, L1_attn_lambda_k1, L1_attn_lambda_q2, L1_attn_lambda_k2, L1_attn_subln_w, L1_ffn_w_router, L1_ffn_wi, L1_ffn_wo):

    def _L0_attn_ref(hidden_states, Wq, bq, Wk, bk, Wv, bv):
        import jax, jax.numpy as jnp
        import numpy as np
        BSZ, SEQ, EMBED = (2, 512, 128)
        NUM_HEADS = 16
        HEAD_DIM = EMBED // NUM_HEADS
        WINDOW = 32

        def _blocks3(x, nb, w):
            b = x.shape[0]
            xb = x.reshape(b, nb + 2, w, NUM_HEADS, HEAD_DIM)
            return jnp.concatenate([xb[:, i:i + nb] for i in range(3)], axis=2)
        b, s, e = hidden_states.shape
        w = WINDOW
        nb = s // w
        q = (hidden_states @ Wq + bq) * (1.0 / np.sqrt(HEAD_DIM))
        k = hidden_states @ Wk + bk
        v = hidden_states @ Wv + bv
        q = q.reshape(b, nb, w, NUM_HEADS, HEAD_DIM)
        k = k.reshape(b, s, NUM_HEADS, HEAD_DIM)
        v = v.reshape(b, s, NUM_HEADS, HEAD_DIM)
        pad = ((0, 0), (w, w), (0, 0), (0, 0))
        kb = _blocks3(jnp.pad(k, pad), nb, w)
        vb = _blocks3(jnp.pad(v, pad), nb, w)
        scores = jnp.einsum('bnxhd,bnyhd->bnhxy', q, kb)
        x_idx = jnp.arange(w)
        y_idx = jnp.arange(3 * w)
        band = jnp.abs(y_idx[None, :] - x_idx[:, None] - w) <= w
        kpos = jnp.arange(nb)[:, None] * w - w + y_idx[None, :]
        inb = (kpos >= 0) & (kpos < s)
        mask = band[None, :, :] & inb[:, None, :]
        scores = jnp.where(mask[None, :, None, :, :], scores, -jnp.inf)
        probs = jax.nn.softmax(scores.astype(jnp.float32), axis=-1).astype(v.dtype)
        attn = jnp.einsum('bnhxy,bnyhd->bnxhd', probs, vb)
        return attn.reshape(b, s, e)

    def _L0_ffn_ref(x, router_w, router_b, w1, b1, w2, b2):
        import jax, jax.numpy as jnp
        import numpy as np
        DIM = 128
        HIDDEN = 512
        E = 8
        B, S = (2, 512)
        logits = jnp.einsum('bsd,de->bse', x, router_w) + router_b
        probs = jax.nn.softmax(logits, axis=-1)
        top1 = jnp.argmax(probs, axis=-1)
        out = jnp.zeros_like(x)
        for i in range(E):
            h = jnp.einsum('bsd,df->bsf', x, w1[i]) + b1[i]
            a, g = jnp.split(h, 2, axis=-1)
            y = jnp.einsum('bsh,hd->bsd', a * jax.nn.sigmoid(g), w2[i]) + b2[i]
            out = out + jnp.where((top1 == i)[..., None], y, 0.0)
        return out

    def _L1_attn_ref(query, Wq, Wk, Wv, Wo, lambda_q1, lambda_k1, lambda_q2, lambda_k2, subln_w):
        import jax, jax.numpy as jnp
        import numpy as np
        EMBED_DIM = 128
        NUM_HEADS = 16
        DEPTH = 12
        HEAD_DIM = EMBED_DIM // NUM_HEADS // 2
        LAMBDA_INIT = float(0.8 - 0.6 * np.exp(-0.3 * DEPTH))
        B, T = (2, 256)
        Bsz, Tt, E = query.shape
        H, hd = (NUM_HEADS, HEAD_DIM)
        scaling = hd ** (-0.5)
        q = jnp.einsum('bte,fe->btf', query, Wq).reshape(Bsz, Tt, 2 * H, hd).transpose(0, 2, 1, 3)
        k = jnp.einsum('bse,fe->bsf', query, Wk).reshape(Bsz, Tt, 2 * H, hd).transpose(0, 2, 1, 3)
        v = jnp.einsum('bse,fe->bsf', query, Wv).reshape(Bsz, Tt, H, 2 * hd).transpose(0, 2, 1, 3)
        q = q * scaling
        scores = jnp.einsum('bhtd,bhsd->bhts', q, k)
        attn_w = jax.nn.softmax(scores.astype(jnp.float32), axis=-1).astype(q.dtype)
        lam1 = jnp.exp(jnp.sum(lambda_q1 * lambda_k1))
        lam2 = jnp.exp(jnp.sum(lambda_q2 * lambda_k2))
        lam = lam1 - lam2 + LAMBDA_INIT
        aw = attn_w.reshape(Bsz, H, 2, Tt, Tt)
        aw = aw[:, :, 0] - lam * aw[:, :, 1]
        attn = jnp.einsum('bhts,bhsd->bhtd', aw, v)
        x32 = attn.astype(jnp.float32)
        normed = (x32 * jax.lax.rsqrt(jnp.mean(x32 * x32, axis=-1, keepdims=True) + 1e-05)).astype(attn.dtype)
        attn = normed * subln_w
        attn = attn * (1.0 - LAMBDA_INIT)
        out = attn.transpose(0, 2, 1, 3).reshape(Bsz, Tt, H * 2 * hd)
        return jnp.einsum('bte,fe->btf', out, Wo)

    def _L1_ffn_ref(x, w_router, wi, wo):
        import jax, jax.numpy as jnp
        import numpy as np
        NUM_EXPERTS = 8
        NUM_SELECTED = 2
        EXPERT_CAPACITY = 64
        NUM_GROUPS = 8

        def _routing(xg, w_router):
            G, T, H = xg.shape
            logits = jnp.einsum('gth,he->gte', xg, w_router)
            probs = jax.nn.softmax(logits, axis=-1)
            _gate, idx = jax.lax.top_k(probs, NUM_SELECTED)
            idx_kt = jnp.swapaxes(idx, 1, 2).reshape(G, -1)
            expert_mask = jax.nn.one_hot(idx_kt, NUM_EXPERTS, dtype=jnp.int32)
            priority = jnp.cumsum(expert_mask, axis=1) * expert_mask - 1
            priority = priority.reshape(G, NUM_SELECTED, T, NUM_EXPERTS)
            priority = jnp.swapaxes(priority, 1, 2).max(axis=2)
            dispatch = jax.nn.one_hot(priority, EXPERT_CAPACITY, dtype=xg.dtype)
            combine = probs[..., None] * dispatch
            return (dispatch, combine)
        B, S, H = x.shape
        T = B * S // NUM_GROUPS
        xg = x.reshape(NUM_GROUPS, T, H)
        dispatch, combine = _routing(xg, w_router)
        expert_in = jnp.einsum('gth,gtec->gech', xg, dispatch)
        h = jax.nn.gelu(jnp.einsum('gech,ehf->gecf', expert_in, wi))
        expert_out = jnp.einsum('gecf,efh->gech', h, wo)
        out = jnp.einsum('gech,gtec->gth', expert_out, combine)
        return out.reshape(B, S, H)
    x = L0_attn_hidden_states
    xn = _layernorm(x, axis=-1)
    x = x + _L0_attn_ref(xn, L0_attn_Wq, L0_attn_bq, L0_attn_Wk, L0_attn_bk, L0_attn_Wv, L0_attn_bv) + _L0_ffn_ref(xn, L0_ffn_router_w, L0_ffn_router_b, L0_ffn_w1, L0_ffn_b1, L0_ffn_w2, L0_ffn_b2)
    xn = _layernorm(x, axis=-1)
    x = x + _L1_attn_ref(xn, L1_attn_Wq, L1_attn_Wk, L1_attn_Wv, L1_attn_Wo, L1_attn_lambda_q1, L1_attn_lambda_k1, L1_attn_lambda_q2, L1_attn_lambda_k2, L1_attn_subln_w) + _L1_ffn_ref(xn, L1_ffn_w_router, L1_ffn_wi, L1_ffn_wo)
    return x

_drawn_inputs = setup_inputs


def setup_inputs(seed=0):
    import zlib

    import numpy as np

    out = dict(_drawn_inputs(seed))
    spreads = {'L0_attn_bq': (0.0, 0.427),
     'L0_attn_bk': (0.0, 0.8),
     'L0_attn_bv': (0.0, 0.1),
     'L1_attn_subln_w': (1.0, 0.6)}
    factors = {'L0_ffn_b1': 3.772,
     'L1_attn_Wq': 5.956,
     'L1_attn_Wk': 5.886,
     'L1_attn_lambda_q1': 8.0,
     'L1_attn_lambda_k1': 8.0,
     'L1_attn_lambda_q2': 8.0,
     'L1_attn_lambda_k2': 8.0,
     'L1_ffn_w_router': 5.632,
     'L1_ffn_wi': 5.077,
     'L1_ffn_wo': 4.992}
    for name, (base, spread) in spreads.items():
        noise = np.random.default_rng([zlib.crc32(name.encode()), seed]).standard_normal(out[name].shape)
        drawn = base * np.exp(spread * noise) if base else spread * noise
        out[name] = jnp.asarray(drawn.astype(out[name].dtype))
    for name, factor in factors.items():
        out[name] = (out[name] * factor).astype(out[name].dtype)
    return out
```

```python
import numpy as np
import concourse.bass as bass
from concourse import mybir
from contextlib import ExitStack

F32 = mybir.dt.float32
BF16 = mybir.dt.bfloat16
I32 = mybir.dt.int32
ALU = mybir.AluOpType
ACT = mybir.ActivationFunctionType
AX = mybir.AxisListType

P = 128
NB, SEQ, D = 8, 256, 128
NT = NB * SEQ // P
TPB = SEQ // P
H = 16
HD0 = D // H
HD1 = HD0 // 2
WINDOW = 32
NX = P + WINDOW
E, FF = 8, 512
FC = FF // P
CAP = 64
MT = NT + E - 1
EPS = 1e-5
LAMBDA_INIT = float(0.8 - 0.6 * np.exp(-0.3 * 12))
TERMS = 6
QPART = (0, 0, 0, 1, 1, 2)
KPART = (0, 1, 2, 0, 1, 0)
BIG = 1e30
VW = HD0 + 1
VROW = H * VW + 32 - VW
GELU_C = float(np.sqrt(2.0 / np.pi))
GELU_A = 0.044715


class Mark:

    def __init__(self, sem, value):
        self.sem, self.value = sem, value


class Queue:

    def __init__(self, sem):
        self.sem, self.count, self.steps, self.passed = sem, 0, [], {}

    def wait(self, *marks):
        for m in marks:
            if m is None:
                continue
            key = id(m.sem)
            if self.passed.get(key, 0) < m.value:
                self.passed[key] = m.value
                self.steps.append(lambda e, m=m: e.wait_ge(m.sem, m.value))

    def do(self, step):
        self.steps.append(step)

    def mark(self, step):
        self.count += 1
        self.steps.append(lambda e: step(e).then_inc(self.sem, 1))
        return Mark(self.sem, self.count)

    def dma(self, group, step):
        group.n += 16
        self.steps.append(lambda e: step(e).then_inc(group.sem, 16))

    def play(self, engine):
        for step in self.steps:
            step(engine)


class DmaGroup:

    def __init__(self, sem):
        self.sem, self.n = sem, 0

    def done(self):
        return Mark(self.sem, self.n)


class Buffer:

    def __init__(self, ap):
        self.ap, self.free = ap, []


def constants_f32():
    parts = [np.eye(P), np.tile(np.arange(CAP), (P, 1)), np.tile(np.arange(E, 0, -1), (P, 1)),
             np.tile(np.arange(NT) * P, (P, 1)),
             np.tile((np.arange(E)[None, :] <= np.arange(E)[:, None]).ravel(), (P, 1)),
             np.tile(np.arange(MT), (P, 1))]
    return np.concatenate(parts, axis=1).astype(np.float32)


def constants_masks():
    p = np.arange(P)[:, None]
    c = np.arange(NX)[None, :]
    mask = [np.where(np.abs(c - p) <= WINDOW, 0.0, -BIG), np.where(np.abs(c - WINDOW - p) <= WINDOW, 0.0, -BIG)]
    parts = [np.eye(P), (p < np.arange(P)[None, :]), np.ones((P, P))] + mask
    return np.concatenate(parts, axis=1).astype(np.float32)


def build(nc, d):
    ctx = ExitStack()
    with ctx:
        def sb(name, shape, dt=F32):
            return ctx.enter_context(nc.sbuf_tensor(name, shape, dt))

        def sem(name):
            return ctx.enter_context(nc.semaphore(name))

        groups = []

        def group(name):
            groups.append(DmaGroup(sem(name)))
            return groups[-1]

        pe, act, dve, pool, sp = (Queue(sem(f"done_{n}")) for n in ("pe", "act", "dve", "pool", "sp"))

        cf = sb("cf", [P, P + CAP + E + NT + E * E + MT])
        cb = sb("cb", [P, 3 * P + 2 * NX], BF16)
        at = 0
        names = {}
        for n, w in (("ident", P), ("iota", CAP), ("down", E), ("steps", NT), ("upto", E * E), ("tiles", MT)):
            names[n] = cf[:, at:at + w]
            at += w
        ident, iota, down, steps, upto, tilenr = (names[n] for n in ("ident", "iota", "down", "steps", "upto", "tiles"))
        identb, before, onesb, maskb = cb[:, 0:P], cb[:, P:2 * P], cb[:, 2 * P:3 * P], cb[:, 3 * P:]

        x_tok = sb("x_tok", [P, NT, D])
        xn_tok = sb("xn_tok", [P, NT, D])
        xnT = sb("xnT", [P, NT * P])
        attn_tok = sb("attn_tok", [P, NT, D])
        wsmall = sb("wsmall", [P, 7, D])
        wr = sb("wr", [P, 2, E])
        rb = sb("rb", [P, E])
        bqk = sb("bqk", [P, 2])
        bvb = sb("bvb", [P, D])
        lamv = sb("lamv", [P, 4, HD1])
        subln = sb("subln", [P, 1])
        regA = sb("regA", [P, E * 2 * FF + E * FC * D])
        w1 = regA[:, 0:E * 2 * FF].rearrange("p (e n) -> p e n", e=E)
        w2 = regA[:, E * 2 * FF:].rearrange("p (e c n) -> p e c n", e=E, c=FC)
        XE = regA[:, 0:4096].rearrange("p (g e c) -> p g e c", e=E, g=NB)
        G = regA[:, 4096:8192].rearrange("p (b f n) -> p b f n", b=2, f=FC)
        tmpA = regA[:, 8192:12288].rearrange("p (k n) -> p k n", k=8)
        regB = sb("regB", [P, 2 * E * FF])
        wi = regB[:, 0:E * FF].rearrange("p (e n) -> p e n", e=E)
        wo = regB[:, E * FF:].rearrange("p (e c n) -> p e c n", e=E, c=FC)
        b1r = regB[0:3, 0:4096].bitcast(BF16).rearrange("p (e n) -> p e n", e=E)
        b2r = regB[0:3, 4096:4608].bitcast(BF16).rearrange("p (e n) -> p e n", e=E)
        xs = [Buffer(regB[:, 4608 + P * i:4608 + P * (i + 1)]) for i in range(4)]
        xsT = [Buffer(regB[:, 5120 + P * i:5120 + P * (i + 1)]) for i in range(2)]
        tg = [Buffer(regB[:, 5376 + 512 * i:5376 + 512 * (i + 1)]) for i in range(1)]
        ga = [Buffer(regB[:, 5888:6400])]
        gaT = [Buffer(regB[:, 6400:6912])]
        ysb = [Buffer(regB[:, 6912 + P * i:6912 + P * (i + 1)]) for i in range(2)]
        ygat = [Buffer(regB[:, 7168 + P * i:7168 + P * (i + 1)]) for i in range(4)]
        bias3 = sb("bias3", [P, 3, 72], BF16)
        biasf = regB[:, 7992:7992 + 144].rearrange("p (k n) -> p k n", k=2)

        Qst = [sb(f"Qst{i}", [P, H, SEQ], BF16) for i in range(2)]
        Kst = [sb(f"Kst{i}", [P, H, SEQ], BF16) for i in range(2)]
        q32 = Buffer(sb("q32", [P, 512]))
        parts = Buffer(sb("parts", [P, 3, 512], BF16))
        V = sb("V", [P, NT, VROW])
        PT = [Buffer(sb(f"PT{i}", [P, 1024])) for i in range(5)]
        OT = [Buffer(sb(f"OT{i}", [P, 512])) for i in range(2)]
        Otok = [Buffer(sb(f"Otok{i}", [P, 2 * TPB, H, VW])) for i in range(2)]
        rec = sb("rec", [P, 2 * TPB * H])
        osc = sb("osc", [P, 2 * TPB * H * HD0])
        sq = sb("sq", [P, TPB * H * HD0])
        ms = sb("ms", [P, TPB * H])
        mbuf = [sb(f"mbuf{i}", [P, TPB, 2 * H]) for i in range(2)]
        M2 = [sb(f"M2{i}", [P, TPB, 2, 2 * H], BF16) for i in range(2)]
        MTs = [Buffer(sb(f"MTs{i}", [64, SEQ], BF16)) for i in range(2)]
        stats = sb("stats", [P, NT, 6])
        mv = sb("mv", [P, NT, 2])
        rstd = sb("rstd", [P, NT])
        halfneg = sb("halfneg", [P, TPB * H])
        lam = sb("lam", [P, 24])
        lg = sb("lg", [P, NT, E])
        pr = sb("pr", [P, NT, E])
        tmp8 = sb("tmp8", [P, NT, E])
        mx = sb("mx", [P, NT])
        ohf = [sb(f"ohf{k}", [P, NT, E]) for k in range(2)]
        ohb = [sb(f"ohb{k}", [P, NT + 1, E], BF16) for k in range(2)]
        rank = sb("rank", [P, 2 * NT, E])
        cnt = regB[:, 7680:7808].rearrange("p (e t) -> p e t", e=E)
        tiles_of = sb("tiles_of", [P, 2, E])
        posf = sb("posf", [P, NT])
        posi = sb("posi", [P, NT], I32)
        endsc = regB[:, 7808:7808 + MT * E].rearrange("p (t e) -> p t e", e=E)
        tef = sb("tef", [P, MT])
        tei = sb("tei", [P, MT], I32)
        posm = sb("posm", [P, NT, E])

        PS = ctx.enter_context(nc.psum_tensor("PS", [P, 8, 512], F32))
        bankA, bankB = Buffer(PS[:, 0:2, :]), Buffer(PS[:, 2:4, :])
        bankV, bankM, bank6, bank7 = (Buffer(PS[:, i, :]) for i in (4, 5, 6, 7))
        bankMb = PS[:, 5, :].bitcast(BF16)

        Q6 = [nc.dram_tensor(f"Q6_{L}", (NB, TERMS, D, SEQ), BF16, kind="Internal").ap() for L in range(2)]
        K6 = [nc.dram_tensor(f"K6_{L}", (NB, TERMS, D, SEQ), BF16, kind="Internal").ap() for L in range(2)]
        Mx = [nc.dram_tensor(f"Mx_{L}", (NB, 2, (1, 2)[L] * H, SEQ), BF16, kind="Internal").ap() for L in range(2)]
        B3 = nc.dram_tensor("B3", (3, P, 72), BF16, kind="Internal").ap()
        Xs = nc.dram_tensor("Xs", (MT * P, D), F32, kind="Internal").ap()
        Ys = nc.dram_tensor("Ys", (MT * P, D), F32, kind="Internal").ap()

        g_c, g_x, g_w, g_e0, g_e1 = (group(n) for n in ("ld_const", "ld_x", "ld_small", "ld_exp0", "ld_exp1"))
        xin = d["x"].rearrange("b (t p) c -> p (b t) c", p=P)
        for k in range(4):
            sp.dma(g_x, lambda e, k=k: e.dma_start(x_tok[:, 4 * k:4 * k + 4, :], xin[:, 4 * k:4 * k + 4, :]))
        sp.dma(g_c, lambda e: e.dma_start(cf[:, :], d["cf"]))
        sp.dma(g_c, lambda e: e.dma_start(PT[0].ap[:, 0:3 * P + 2 * NX], d["cb"]))
        for dst, name in ((wsmall[:, :, :], "wsmall"), (wr[:, :, :], "wr"), (rb[:, :], "rb"), (bqk[:, :], "bqk"),
                          (bvb[:, :], "bvb"), (lamv[:, :, :], "lamv"), (subln[:, :], "subln"),
                          (biasf[:, 0, :], "bias")):
            sp.dma(g_w, lambda e, dst=dst, name=name: e.dma_start(dst, d[name]))
        w1_d = d["w1"].rearrange("e p n -> p e n")
        w2_d = d["w2"].rearrange("e (c p) n -> p e c n", p=P)
        x_in, loaded, small = g_x.done(), g_c.done(), g_w.done()
        dve.wait(loaded)
        consts = dve.mark(lambda e: e.tensor_copy(cb[:, :], PT[0].ap[:, 0:3 * P + 2 * NX]))
        PT[0].free = [consts]

        m_set = []
        for i in range(2):
            pool.do(lambda e, i=i: e.memset(Kst[i][:, :, :], -1.0))
            m_set.append(dve.mark(lambda e, i=i: e.memset(Qst[i][:, :, :], 0.0)))
        dve.do(lambda e: e.memset(halfneg[:, :], -0.5))
        dve.do(lambda e: e.memset(V[:, :, :], 1.0))
        m_ohz = dve.mark(lambda e: e.memset(ohb[0][:, NT, :], 0.0))
        pool.do(lambda e: e.memset(xn_tok[:, 0:6, :], 0.0))
        m_kset = pool.mark(lambda e: e.memset(lam[:, :], 0.0))
        g_z = group("zero_xs")
        sp.wait(m_kset)
        xs_v = Xs.rearrange("(t p) c -> p t c", p=P)
        for k in range(0, MT, 6):
            n = min(6, MT - k)
            sp.dma(g_z, lambda e, k=k, n=n: e.dma_start(xs_v[:, k:k + n, :], xn_tok[:, 0:n, :]))
        for e_ in range(0, E, 2):
            sp.dma(g_e0, lambda e, e_=e_: e.dma_start(w1[:, e_:e_ + 2, :], w1_d[:, e_:e_ + 2, :]))
            sp.dma(g_e0, lambda e, e_=e_: e.dma_start(w2[:, e_:e_ + 2, :, :], w2_d[:, e_:e_ + 2, :, :]))
        w_e0 = g_e0.done()
        zeroed = g_z.done()

        dve.wait(small)
        dve.wait(m_kset)
        a = dve.mark(lambda e: e.tensor_tensor(lam[:, 0:8].rearrange("p (a b) -> p a b", a=2),
                                               lamv[:, 0::2, :], lamv[:, 1::2, :], ALU.mult))
        dve.wait(a)
        a = dve.mark(lambda e: e.tensor_reduce(lam[:, 8:10], lam[:, 0:8].rearrange("p (a b) -> p a b", a=2),
                                               AX.X, ALU.add))
        act.wait(a)
        a = act.mark(lambda e: e.activation(lam[:, 10:12], lam[:, 8:10], ACT.Exp))
        dve.wait(a)
        a = dve.mark(lambda e: e.tensor_tensor(lam[:, 12:13], lam[:, 11:12], lam[:, 10:11], ALU.subtract))
        dve.wait(a)
        dve.do(lambda e: e.tensor_scalar(lam[:, 13:14], lam[:, 12:13], -LAMBDA_INIT, None, ALU.add))
        m_wo = dve.mark(lambda e: e.tensor_scalar(wsmall[:, 6, :], wsmall[:, 6, :], subln[:, 0:1], 1.0 - LAMBDA_INIT,
                                                  ALU.mult, ALU.mult))
        a = dve.mark(lambda e: e.tensor_scalar(biasf[:, 0, 64:72], biasf[:, 0, 64:72], 2.0, None, ALU.mult))
        g_b = group("bias_rows")
        for k in range(3):
            src = k % 2
            dve.wait(a)
            a = dve.mark(lambda e, k=k, src=src: e.tensor_copy(bias3[:, k, :], biasf[:, src, :]))
            if k < 2:
                dve.wait(a)
                a = dve.mark(lambda e, k=k, src=src: e.tensor_tensor(biasf[:, 1 - src, :], biasf[:, src, :],
                                                                     bias3[:, k, :], ALU.subtract))
        sp.wait(a)
        sp.dma(g_b, lambda e: e.dma_start(B3.rearrange("k p n -> p k n"), bias3[:, :, :]))
        sp.wait(g_b.done())
        b1v = regB[0:3, 0:4096].bitcast(BF16).rearrange("k (q n) -> k q n", n=64)
        b2v = regB[0:3, 4096:4608].bitcast(BF16).rearrange("k (q n) -> k q n", n=8)
        sp.dma(g_b, lambda e: e.dma_start(b1v, B3[:, :, 0:64]))
        sp.dma(g_b, lambda e: e.dma_start(b2v, B3[:, :, 64:72]))
        bias_rows = g_b.done()

        def layer_norm(ready, xn_free, xnT_free):
            dve.wait(*ready)
            for i in range(NT):
                a = dve.mark(lambda e, i=i: e.bn_stats(stats[:, i, :], x_tok[:, i, :]))
            dve.wait(a)
            for i in range(NT):
                a = dve.mark(lambda e, i=i: e.bn_aggr(mv[:, i, :], stats[:, i, :]))
            dve.wait(a)
            a = dve.mark(lambda e: e.tensor_scalar(rstd[:, :], mv[:, :, 1], EPS, None, ALU.add))
            pool.wait(a)
            a = pool.mark(lambda e: e.tensor_tensor(rstd[:, :], rstd[:, :], halfneg[:, 0:NT], ALU.pow))
            dve.wait(a, *xn_free)
            tok, tr = [], []
            for i in range(NT):
                tok.append(dve.mark(lambda e, i=i: e.tensor_scalar(xn_tok[:, i, :], x_tok[:, i, :], mv[:, i, 0:1],
                                                                   rstd[:, i:i + 1], ALU.subtract, ALU.mult)))
            pe.wait(consts)
            act.wait(*xnT_free)
            for c in range(NT // 4):
                bank = (bankM, bank6, bank7, bankV)[c]
                pe.wait(tok[4 * c + 3], *bank.free)
                for i in range(4):
                    a = pe.mark(lambda e, i=i, c=c, bank=bank: e.transpose(bank.ap[:, P * i:P * (i + 1)],
                                                                         xn_tok[:, 4 * c + i, :], ident))
                act.wait(a)
                tr.append(act.mark(lambda e, c=c, bank=bank: e.copy(xnT[:, 512 * c:512 * (c + 1)], bank.ap)))
                bank.free = [tr[-1]]
            return tok, tr

        def pick_first_max(src, out_f, out_b, ready):
            def bc(t):
                return t.unsqueeze(2).to_broadcast([P, NT, E])
            dve.wait(ready)
            a = dve.mark(lambda e: e.tensor_reduce(mx[:, :], src, AX.X, ALU.max))
            dve.wait(a)
            a = dve.mark(lambda e: e.tensor_tensor(tmp8[:, :, :], src, bc(mx[:, :]), ALU.is_equal))
            dve.wait(a)
            dw = down.unsqueeze(1).to_broadcast([P, NT, E])
            a = dve.mark(lambda e: e.tensor_tensor(tmp8[:, :, :], tmp8[:, :, :], dw, ALU.mult))
            dve.wait(a)
            a = dve.mark(lambda e: e.tensor_reduce(posf[:, :], tmp8[:, :, :], AX.X, ALU.max))
            dve.wait(a)
            a = dve.mark(lambda e: e.tensor_tensor(out_f, dw, bc(posf[:, :]), ALU.is_equal))
            dve.wait(a)
            return dve.mark(lambda e: e.tensor_copy(out_b, out_f))

        def logits(L, xnT_done):
            pe.wait(small, *xnT_done)
            pe.wait(*bank6.free)
            for i in range(NT):
                a = pe.mark(lambda e, i=i: e.matmul(bank6.ap[:, E * i:E * (i + 1)], xnT[:, P * i:P * (i + 1)],
                                                    wr[:, L, :], start=True, stop=True))
            return a

        def route0(tok, xnT_done):
            a = logits(0, xnT_done)
            dve.wait(a)
            a = dve.mark(lambda e: e.tensor_tensor(lg[:, :, :], bank6.ap[:, 0:NT * E].rearrange("p (t e) -> p t e", e=E),
                                                   rb[:, :].unsqueeze(1).to_broadcast([P, NT, E]), ALU.add))
            bank6.free = [a]
            dve.wait(consts)
            a = pick_first_max(lg[:, :, :], ohf[0][:, :, :], ohb[0][:, 0:NT, :], a)
            pe.wait(a, m_ohz, *bank7.free)
            rk = bank7.ap[:, 0:(NT + 1) * E]
            pe.do(lambda e: e.matmul(rk, before, ohb[0][:, :, :], start=True, stop=False, skip_group_check=True))
            for k in range(1, NT + 1):
                a = pe.mark(lambda e, k=k: e.matmul(rk[:, E * k:], onesb, ohb[0][:, 0:NT + 1 - k, :], start=False,
                                                    stop=k == NT, skip_group_check=True))
            rv = rk.rearrange("p (t e) -> p t e", e=E)
            dve.wait(a)
            a = dve.mark(lambda e: e.tensor_copy(tiles_of[:, 0, :], rv[:, NT, :]))
            dve.wait(a)
            a = dve.mark(lambda e: e.tensor_tensor(cnt[:, :, :], tiles_of[:, 0, :].unsqueeze(2).to_broadcast([P, E, NT]),
                                                   steps.unsqueeze(1).to_broadcast([P, E, NT]), ALU.is_gt))
            dve.wait(a)
            a = dve.mark(lambda e: e.tensor_reduce(tiles_of[:, 0, :], cnt[:, :, :], AX.X, ALU.add))
            dve.wait(a)
            uv = upto.rearrange("p (a b) -> p a b", a=E)
            c8 = cnt[:, :, 0:E]
            a = dve.mark(lambda e: e.tensor_tensor(c8, uv, tiles_of[:, 0, :].unsqueeze(1).to_broadcast([P, E, E]),
                                                   ALU.mult))
            dve.wait(a)
            a = dve.mark(lambda e: e.tensor_reduce(tiles_of[:, 1, :], c8, AX.X, ALU.add))
            dve.wait(a)
            dve.do(lambda e: e.tensor_tensor(endsc[:, :, :], tilenr.unsqueeze(2).to_broadcast([P, MT, E]),
                                             tiles_of[:, 1, :].unsqueeze(1).to_broadcast([P, MT, E]), ALU.is_ge))
            a = dve.mark(lambda e: e.tensor_tensor(tiles_of[:, 0, :], tiles_of[:, 1, :], tiles_of[:, 0, :],
                                                   ALU.subtract))
            dve.wait(a)
            a = dve.mark(lambda e: e.tensor_reduce(tef[:, :], endsc[:, :, :], AX.X, ALU.add))
            a = dve.mark(lambda e: e.tensor_scalar(tiles_of[:, 0, :], tiles_of[:, 0, :], float(P), None, ALU.mult))
            dve.wait(a)
            te_m = dve.mark(lambda e: e.tensor_scalar(tei[:, :], tef[:, :], float(E - 1), None, ALU.min))
            a = dve.mark(lambda e: e.tensor_tensor(rank[:, 0:NT, :], rv[:, 0:NT, :],
                                                   tiles_of[:, 0, :].unsqueeze(1).to_broadcast([P, NT, E]), ALU.add))
            bank7.free = [a]
            dve.wait(a)
            a = dve.mark(lambda e: e.tensor_tensor(rank[:, 0:NT, :], rank[:, 0:NT, :], ohf[0][:, :, :], ALU.mult))
            dve.wait(a)
            a = dve.mark(lambda e: e.tensor_reduce(posf[:, :], rank[:, 0:NT, :], AX.X, ALU.add))
            dve.wait(a)
            a = dve.mark(lambda e: e.tensor_copy(posi[:, :], posf[:, :]))
            g = group("scatter_x")
            pool.wait(a, zeroed, *tok)
            for i in range(NT):
                pool.dma(g, lambda e, i=i: e.indirect_dma_start(
                    Xs, bass.IndirectOffsetOnAxis(ap=posi[:, i:i + 1], axis=0), xn_tok[:, i, :], None))
            return te_m, g.done()

        def experts0(te_m, scattered):
            pe.wait(te_m, w_e0, bias_rows, consts)
            g_y = group("store_y")
            loads = {}

            def load(j):
                if j < MT:
                    g = group(f"ld_xs{j % 4}") if j < 4 else loads[j - 4]
                    sp.wait(scattered, *xs[j % 4].free)
                    sp.dma(g, lambda e: e.dma_start(xs[j % 4].ap, Xs[P * j:P * (j + 1), :]))
                    loads[j] = g
                    loads[j, "done"] = g.done()

            for j in range(3):
                load(j)
            for j in range(MT):
                b = bankM
                pe.wait(loads[j, "done"], *b.free)
                a = pe.mark(lambda e, j=j: e.transpose(bankM.ap[:, 0:P], xs[j % 4].ap, ident))
                xs[j % 4].free = [a]
                load(j + 3)
                t = xsT[j % 2]
                act.wait(a, *t.free)
                xt = act.mark(lambda e, t=t: e.copy(t.ap, bankM.ap[:, 0:P]))
                bankM.free = [xt]
                yield
                pe.wait(xt, *bank6.free, *bank7.free)
                ev = {}

                def expert_of(e, j=j, ev=ev):
                    ev["e"] = e.value_load(tei[0:1, j:j + 1], min_val=0, max_val=E - 1)
                pe.do(expert_of)
                for half, bank in ((1, bank7), (0, bank6)):
                    pe.do(lambda e, half=half, bank=bank, t=t, ev=ev: e.matmul(
                        bank.ap, t.ap, w1[:, bass.ds(ev["e"], 1), FF * half:FF * (half + 1)], start=True, stop=False))
                    a = pe.mark(lambda e, half=half, bank=bank, ev=ev: e.matmul(
                        bank.ap, onesb[0:3, :], b1r[:, bass.ds(ev["e"], 1), FF * half:FF * (half + 1)],
                        start=False, stop=True))
                    if half:
                        act.wait(a, *tg[0].free)
                        th = act.mark(lambda e: e.activation(tg[0].ap, bank7.ap, ACT.Tanh, scale=0.5))
                        bank7.free = [th]
                t.free = [a]
                dve.wait(a, th, *ga[0].free)
                gm = dve.mark(lambda e: e.scalar_tensor_tensor(ga[0].ap, tg[0].ap, 1.0, bank6.ap, ALU.add, ALU.mult))
                bank6.free = [gm]
                tg[0].free = [gm]
                yield
                pe.wait(gm, *bank7.free)
                for c in range(FC):
                    a = pe.mark(lambda e, c=c: e.transpose(bank7.ap[:, P * c:P * (c + 1)],
                                                           ga[0].ap[:, P * c:P * (c + 1)], ident))
                ga[0].free = [a]
                dve.wait(a, *gaT[0].free)
                gt = dve.mark(lambda e: e.tensor_copy(gaT[0].ap, bank7.ap))
                bank7.free = [gt]
                yield
                pe.wait(gt, *bank6.free)
                for c in range(FC):
                    pe.do(lambda e, c=c, ev=ev: e.matmul(bank6.ap[:, 0:D], gaT[0].ap[:, P * c:P * (c + 1)],
                                                         w2[:, bass.ds(ev["e"], 1), c, :], start=c == 0, stop=False))
                a = pe.mark(lambda e, ev=ev: e.matmul(bank6.ap[:, 0:D], onesb[0:3, :], b2r[:, bass.ds(ev["e"], 1), :],
                                                      start=False, stop=True))
                gaT[0].free = [a]
                y = ysb[j % 2]
                act.wait(a, *y.free)
                a = act.mark(lambda e, y=y: e.mul(y.ap, bank6.ap[:, 0:D], 0.5))
                bank6.free = [a]
                sp.wait(a)
                if j < 2:
                    y.group = group(f"st_y{j}")
                sp.dma(y.group, lambda e, j=j, y=y: e.dma_start(Ys[P * j:P * (j + 1), :], y.ap))
                y.free = [y.group.done()]
                yield
            del g_y
            pool.wait(*ysb[0].free, *ysb[1].free)
            gg = [group(f"gather_y{k}") for k in range(4)]
            added = []
            for i in range(NT):
                b = ygat[i % 4]
                pool.wait(*b.free)
                pool.dma(gg[i % 4], lambda e, i=i, b=b: e.indirect_dma_start(
                    b.ap, None, Ys, bass.IndirectOffsetOnAxis(ap=posi[:, i:i + 1], axis=0)))
                dve.wait(gg[i % 4].done())
                a = dve.mark(lambda e, i=i, b=b: e.tensor_tensor(x_tok[:, i, :], x_tok[:, i, :], b.ap, ALU.add))
                b.free = [a]
                added.append(a)
                yield
            experts0.added = added

        def attention(L, xnT_done, heads_done, V_free):
            hd = (HD0, HD1)[L]
            halves = (1, 2)[L]
            scale = float(1.0 / np.sqrt(hd))
            rows = TERMS * hd
            kA = (66, 50)[L]
            W = (NX, SEQ)[L]
            hpu = (2, 1)[L]
            units = H // hpu
            stack_free = [list(m_set) + [m_kset], list(m_set) + [m_kset]]
            if L:
                stack_free = [list(heads_done.stacks[i]) for i in range(2)]
            state = {}

            def project(c):
                g = group(f"terms{L}_{c}")
                for which, (dst, part_of, wsel) in enumerate(((Q6[L], QPART, 0), (K6[L], KPART, 1))):
                    pe.wait(small, xnT_done[c], *bankM.free)
                    a = pe.mark(lambda e, c=c, wsel=wsel: e.matmul(bankM.ap, wsmall[:, 3 * L + wsel, :],
                                                                   xnT[:, 512 * c:512 * (c + 1)], start=True, stop=True))
                    dve.wait(a, small, *q32.free)
                    sc = scale if which == 0 else 1.0
                    if L == 0:
                        qm = dve.mark(lambda e, which=which, sc=sc: e.tensor_scalar(
                            q32.ap[:, :], bankM.ap, bqk[:, which:which + 1], sc, ALU.add, ALU.mult))
                    else:
                        qm = dve.mark(lambda e, sc=sc: e.tensor_scalar(q32.ap[:, :], bankM.ap, sc, None, ALU.mult))
                    bankM.free = [qm]
                    act.wait(qm, *parts.free)
                    a = act.mark(lambda e: e.copy(parts.ap[:, 0, :], q32.ap[:, :]))
                    dve.wait(a)
                    a = dve.mark(lambda e: e.tensor_tensor(q32.ap[:, :], q32.ap[:, :], parts.ap[:, 0, :], ALU.subtract))
                    act.wait(a)
                    a = act.mark(lambda e: e.copy(parts.ap[:, 1, :], q32.ap[:, :]))
                    dve.wait(a)
                    a = dve.mark(lambda e: e.tensor_tensor(parts.ap[:, 2, :], q32.ap[:, :], parts.ap[:, 1, :],
                                                           ALU.subtract))
                    q32.free = [a]
                    sp.wait(a)
                    for t in range(TERMS):
                        sp.dma(g, lambda e, t=t, c=c, dst=dst, part_of=part_of: e.dma_start(
                            dst[2 * c:2 * c + 2, t, :, :].rearrange("b f n -> f b n"),
                            parts.ap[:, part_of[t], :].rearrange("p (b n) -> p b n", b=2)))
                    parts.free = [g.done()]
                    yield
                state["terms", c] = g.done()
                pe.wait(*bankM.free)
                for i in range(4):
                    a = pe.mark(lambda e, c=c, i=i: e.matmul(bankM.ap[:, P * i:P * (i + 1)],
                                                             xnT[:, 512 * c + P * i:512 * c + P * (i + 1)],
                                                             wsmall[:, 3 * L + 2, :], start=True, stop=True))
                vo = V[:, 4 * c:4 * c + 4, 0:H * VW].rearrange("p t (h v) -> p t h v", v=VW)
                dve.wait(a, *V_free)
                for i in range(4):
                    vi = bankM.ap[:, P * i:P * (i + 1)].rearrange("p (h v) -> p h v", v=HD0)
                    if L == 0:
                        a = dve.mark(lambda e, i=i, vi=vi: e.tensor_tensor(
                            vo[:, i, :, 0:HD0], vi, bvb[:, :].rearrange("p (h v) -> p h v", v=HD0), ALU.add))
                    else:
                        a = dve.mark(lambda e, i=i, vi=vi: e.tensor_copy(vo[:, i, :, 0:HD0], vi))
                bankM.free = [a]
                state["V", c] = a
                yield

            def load_stack(b):
                i = b % 2
                g = state["ld_group", i] if b >= 2 else group(f"stack{L}_{i}")
                state["ld_group", i] = g
                sp.wait(state["terms", b // 2], *stack_free[i])
                for src, dst in ((Q6[L], Qst[i]), (K6[L], Kst[i])):
                    for r in range(halves):
                        v = src[b].rearrange("t (d r h) n -> (t d) r h n", r=halves, h=H)[:, r, :, :]
                        sp.dma(g, lambda e, r=r, dst=dst, v=v: e.dma_start(dst[64 * r:64 * r + rows, :, :], v))
                state["stack", b] = g.done()

            def first_pass(b):
                i = b % 2
                pe.wait(state["stack", b], consts)
                mo = mbuf[i][:, :, 0:halves * H].rearrange("p q (r h) -> p r q h", r=halves)
                dve.wait(*state.get(("mfree", i), []))
                for u in range(units):
                    pe.wait(*bankA.free)
                    if L == 0:
                        for s in range(hpu):
                            h = hpu * u + s
                            pe.do(lambda e, s=s: e.matmul(bankA.ap[:, s, 0:2 * NX], identb, maskb, start=True,
                                                          stop=False, skip_group_check=True))
                            for q in range(TPB):
                                k0 = q * (SEQ - NX)
                                a = pe.mark(lambda e, s=s, h=h, q=q, k0=k0, i=i: e.matmul(
                                    bankA.ap[:, s, NX * q:NX * (q + 1)], Qst[i][0:kA, h, P * q:P * (q + 1)],
                                    Kst[i][0:kA, h, k0:k0 + NX], start=False, stop=q == 1, skip_group_check=True))
                        dve.wait(a)
                        src = bankA.ap[:, :, 0:2 * NX].rearrange("p s (q n) -> p s q n", q=2)
                        a = dve.mark(lambda e, u=u, src=src, i=i: e.tensor_reduce(
                            mbuf[i][:, :, 2 * u:2 * u + 2].rearrange("p q s -> p s q"), src, AX.X, ALU.max))
                    else:
                        for q in range(TPB):
                            for r in range(2):
                                a = pe.mark(lambda e, r=r, u=u, q=q, i=i: e.matmul(
                                    bankA.ap[:, r, SEQ * q:SEQ * (q + 1)],
                                    Qst[i][64 * r:64 * r + kA, u, P * q:P * (q + 1)],
                                    Kst[i][64 * r:64 * r + kA, u, :], start=True, stop=True))
                        dve.wait(a)
                        src = bankA.ap.rearrange("p r (q n) -> p r q n", q=2)
                        a = dve.mark(lambda e, u=u, src=src, mo=mo: e.tensor_reduce(mo[:, :, :, u], src, AX.X, ALU.max))
                    bankA.free = [a]
                    yield
                hh = halves * H
                dve.wait(a)
                a = dve.mark(lambda e, i=i: e.tensor_copy(M2[i][:, :, 0, 0:hh], mbuf[i][:, :, 0:hh]))
                dve.wait(a)
                a = dve.mark(lambda e, i=i: e.tensor_tensor(M2[i][:, :, 1, 0:hh], mbuf[i][:, :, 0:hh],
                                                            M2[i][:, :, 0, 0:hh], ALU.subtract))
                state["mfree", i] = [a]
                yield
                pe.wait(a, *bankM.free)
                for k in range(2):
                    for q in range(TPB):
                        a = pe.mark(lambda e, k=k, q=q, i=i: e.transpose(
                            bankMb[32 * k:32 * k + hh, P * q:P * (q + 1)], M2[i][:, q, k, 0:hh], identb))
                t = MTs[i]
                dve.wait(a, *t.free)
                top = 32 + hh
                if hh == 32:
                    a = dve.mark(lambda e, t=t: e.tensor_copy(t.ap[:, :], bankMb[0:64, 0:SEQ]))
                else:
                    for k in range(2):
                        a = dve.mark(lambda e, t=t, k=k: e.tensor_copy(t.ap[32 * k:32 * k + hh, :],
                                                                       bankMb[32 * k:32 * k + hh, 0:SEQ]))
                del top
                bankM.free = [a]
                g = state["m_group", i] if b >= 2 else group(f"max{L}_{i}")
                state["m_group", i] = g
                sp.wait(a)
                for k in range(2):
                    sp.dma(g, lambda e, k=k, t=t, b=b: e.dma_start(Mx[L][b, k, :, :], t.ap[32 * k:32 * k + hh, :]))
                sp.wait(g.done())
                for r in range(halves):
                    sp.dma(g, lambda e, r=r, i=i, b=b: e.dma_start(
                        Qst[i][64 * r + kA:64 * r + kA + 2, :, :], Mx[L][b, :, H * r:H * (r + 1), :]))
                t.free = [g.done()]
                state["max", b] = g.done()
                yield

            def second_pass(b):
                i = b % 2
                kB = kA + 2
                o = Otok[i]
                pe.wait(state["max", b], state["V", b // 2])
                ups = 4 // hpu
                made = []
                for u in range(units):
                    n = state.get("unit", 0)
                    state["unit"] = n + 1
                    pt = PT[n % len(PT)]
                    pe.wait(*bankB.free)
                    if L == 0:
                        for s in range(hpu):
                            h = hpu * u + s
                            pe.do(lambda e, s=s: e.matmul(bankB.ap[:, s, 0:2 * NX], identb, maskb, start=True,
                                                          stop=False, skip_group_check=True))
                            for k in range(TPB):
                                q0 = k * (SEQ - NX)
                                a = pe.mark(lambda e, s=s, h=h, k=k, q0=q0, i=i: e.matmul(
                                    bankB.ap[:, s, NX * k:NX * (k + 1)], Kst[i][0:kB, h, P * k:P * (k + 1)],
                                    Qst[i][0:kB, h, q0:q0 + NX], start=False, stop=k == 1, skip_group_check=True))
                        act.wait(a, *pt.free)
                        a = act.mark(lambda e, pt=pt: e.activation(
                            pt.ap[:, 0:4 * NX].rearrange("p (s n) -> p s n", s=2), bankB.ap[:, :, 0:2 * NX], ACT.Exp))
                    else:
                        for k in range(TPB):
                            for r in range(2):
                                a = pe.mark(lambda e, r=r, u=u, k=k, i=i: e.matmul(
                                    bankB.ap[:, r, SEQ * k:SEQ * (k + 1)],
                                    Kst[i][64 * r:64 * r + kB, u, P * k:P * (k + 1)],
                                    Qst[i][64 * r:64 * r + kB, u, :], start=True, stop=True))
                        act.wait(a, *pt.free)
                        a = act.mark(lambda e, pt=pt: e.activation(
                            pt.ap[:, :].rearrange("p (s n) -> p s n", s=2), bankB.ap, ACT.Exp))
                    last_score = a
                    bankB.free = [a]
                    made.append((pt, a))
                    yield
                    if u % ups == ups - 1:
                        grp = u // ups
                        n_o = state.get("ot", 0)
                        state["ot"] = n_o + 1
                        ot = OT[n_o % 2]
                        pe.wait(*bankV.free, *(m for _, m in made))
                        width = SEQ * halves
                        for k in range(TPB):
                            for c in range(4):
                                pt, _ = made[c // hpu]
                                h = 4 * grp + c
                                if L == 0:
                                    q0 = k * (SEQ - NX)
                                    rhs = pt.ap[:, (c % 2) * 2 * NX + NX * k:(c % 2) * 2 * NX + NX * (k + 1)]
                                    out = bankV.ap[32 * c:32 * c + 32, q0:q0 + NX]
                                else:
                                    rhs = pt.ap[:, :].rearrange("p (r k n) -> p r k n", r=2, k=2)[:, :, k, :]
                                    out = bankV.ap[32 * c:32 * c + 32, :]
                                a = pe.mark(lambda e, k=k, h=h, rhs=rhs, out=out, b=b: e.matmul(
                                    out, V[:, TPB * b + k, VW * h:VW * h + 32], rhs, start=k == 0, stop=k == 1,
                                    skip_group_check=True))
                        for pt, _ in made:
                            pt.free = [a]
                        made = []
                        eng = act if L == 0 or grp % 2 else dve
                        eng.wait(a, *ot.free)
                        if eng is act:
                            a = act.mark(lambda e, ot=ot, width=width: e.copy(ot.ap[:, 0:width], bankV.ap[:, 0:width]))
                        else:
                            a = dve.mark(lambda e, ot=ot, width=width: e.tensor_copy(ot.ap[:, 0:width],
                                                                                     bankV.ap[:, 0:width]))
                        bankV.free = [a]
                        yield
                        nblk = halves * TPB
                        pe.wait(a, *bankM.free)
                        for k in range(nblk):
                            a = pe.mark(lambda e, k=k, ot=ot: e.transpose(bankM.ap[:, P * k:P * (k + 1)],
                                                                          ot.ap[:, P * k:P * (k + 1)], ident))
                        ot.free = [a]
                        act.wait(a, *o.free)
                        a = act.mark(lambda e, grp=grp, nblk=nblk, o=o: e.copy(
                            o.ap[:, 0:nblk, 4 * grp:4 * grp + 4, :],
                            bankM.ap[:, 0:P * nblk].rearrange("p (k c v) -> p k c v", k=nblk, c=4)[:, :, :, 0:VW]))
                        bankM.free = [a]
                        yield
                stack_free[i] = [last_score, state_last_first.get(b)]
                state["stack_free", i] = [last_score]
                if b + 2 < NB:
                    load_stack(b + 2)
                n = halves * TPB * H
                dve.wait(a)
                r = dve.mark(lambda e, o=o: e.reciprocal(rec[:, 0:n].rearrange("p (k h) -> p k h", h=H),
                                                         o.ap[:, 0:halves * TPB, :, HD0]))
                dve.wait(r)
                if L == 1:
                    r = dve.mark(lambda e: e.tensor_scalar(rec[:, n // 2:n], rec[:, n // 2:n], lam[:, 13:14], None,
                                                           ALU.mult))
                    dve.wait(r)
                num = o.ap[:, 0:halves * TPB, :, 0:HD0].rearrange("p k h v -> p (k h) v")
                rb_ = rec[:, 0:n].unsqueeze(2).to_broadcast([P, n, HD0])
                at_b = attn_tok[:, TPB * b:TPB * (b + 1), :].rearrange("p t f -> p (t f)")
                if L == 0:
                    r = dve.mark(lambda e: e.tensor_tensor(at_b.rearrange("p (k v) -> p k v", v=HD0), num, rb_, ALU.mult))
                    o.free = [r]
                    dve.wait(r)
                    xb = x_tok[:, TPB * b:TPB * (b + 1), :].rearrange("p t f -> p (t f)")
                    r = dve.mark(lambda e: e.tensor_tensor(xb, xb, at_b, ALU.add))
                    state["out", b] = r
                    yield
                else:
                    m = n // 2 * HD0
                    r = dve.mark(lambda e: e.tensor_tensor(osc[:, :].rearrange("p (k v) -> p k v", v=HD0), num, rb_,
                                                           ALU.mult))
                    o.free = [r]
                    dve.wait(r)
                    r = dve.mark(lambda e: e.tensor_tensor(osc[:, 0:m], osc[:, 0:m], osc[:, m:2 * m], ALU.add))
                    dve.wait(r)
                    r = dve.mark(lambda e: e.tensor_tensor(sq[:, :], osc[:, 0:m], osc[:, 0:m], ALU.mult))
                    dve.wait(r)
                    r = dve.mark(lambda e: e.tensor_reduce(ms[:, :], sq[:, :].rearrange("p (k v) -> p k v", v=HD0),
                                                           AX.X, ALU.add))
                    dve.wait(r)
                    r = dve.mark(lambda e: e.tensor_scalar(ms[:, :], ms[:, :], 1.0 / HD0, EPS, ALU.mult, ALU.add))
                    pool.wait(r)
                    r = pool.mark(lambda e: e.tensor_tensor(ms[:, :], ms[:, :], halfneg[:, :], ALU.pow))
                    yield
                    dve.wait(r)
                    r = dve.mark(lambda e: e.tensor_tensor(
                        sq[:, :].rearrange("p (k v) -> p k v", v=HD0), osc[:, 0:m].rearrange("p (k v) -> p k v", v=HD0),
                        ms[:, :].unsqueeze(2).to_broadcast([P, n // 2, HD0]), ALU.mult))
                    pe.wait(r, *bankM.free)
                    for q in range(TPB):
                        a = pe.mark(lambda e, q=q: e.transpose(bankM.ap[:, P * q:P * (q + 1)],
                                                               sq[:, P * q:P * (q + 1)], ident))
                    act.wait(a)
                    a = act.mark(lambda e: e.copy(at_b, bankM.ap[:, 0:SEQ]))
                    dve.wait(a)
                    bankM.free = [a]
                    state["out", b] = a
                    yield

            state_last_first = {}
            for c in range(2):
                yield from project(c)
            for b in range(2):
                load_stack(b)
            yield from first_pass(0)
            for b in range(NB):
                if b in (1, 3):
                    yield from project(b // 2 + 2)
                second = second_pass(b)
                first = first_pass(b + 1) if b + 1 < NB else iter(())
                while True:
                    one = next(first, "end")
                    two = next(second, "end")
                    if one is None:
                        yield
                    if two is None:
                        yield
                    if one == "end" and two == "end":
                        break
            attention.out = [state["out", b] for b in range(NB)]
            attention.stacks = [state["stack_free", 0], state["stack_free", 1]]

        def route1(xnT_done):
            a = logits(1, xnT_done)
            lv = bank6.ap[:, 0:NT * E].rearrange("p (t e) -> p t e", e=E)
            dve.wait(a)
            a = dve.mark(lambda e: e.tensor_copy(lg[:, :, :], lv))
            bank6.free = [a]
            dve.wait(a)
            a = dve.mark(lambda e: e.tensor_reduce(mx[:, :], lg[:, :, :], AX.X, ALU.max))
            dve.wait(a)
            mxb = mx[:, :].unsqueeze(2).to_broadcast([P, NT, E])
            a = dve.mark(lambda e: e.tensor_tensor(pr[:, :, :], lg[:, :, :], mxb, ALU.subtract))
            act.wait(a)
            a = act.mark(lambda e: e.activation(pr[:, :, :], pr[:, :, :], ACT.Exp))
            dve.wait(a)
            a = dve.mark(lambda e: e.tensor_reduce(mx[:, :], pr[:, :, :], AX.X, ALU.add))
            dve.wait(a)
            a = dve.mark(lambda e: e.reciprocal(mx[:, :], mx[:, :]))
            dve.wait(a)
            a = dve.mark(lambda e: e.tensor_tensor(pr[:, :, :], pr[:, :, :], mxb, ALU.mult))
            a = pick_first_max(lg[:, :, :], ohf[0][:, :, :], ohb[0][:, 0:NT, :], a)
            dve.wait(a)
            a = dve.mark(lambda e: e.tensor_scalar(tmp8[:, :, :], ohf[0][:, :, :], -BIG, None, ALU.mult))
            dve.wait(a)
            a = dve.mark(lambda e: e.tensor_tensor(lg[:, :, :], lg[:, :, :], tmp8[:, :, :], ALU.add))
            a = pick_first_max(lg[:, :, :], ohf[1][:, :, :], ohb[1][:, 0:NT, :], a)
            ov = [ohb[k][:, 0:NT, :].rearrange("p (g t) e -> p t g e", t=TPB) for k in range(2)]
            pe.wait(a, *bank7.free)
            queue = [(0, 0), (0, 1), (1, 0), (1, 1)]
            for n, (k, t) in enumerate(queue):
                out = bank7.ap[:, 64 * n:64 * n + 64].rearrange("p (g e) -> p g e", e=E)
                pe.do(lambda e, k=k, t=t, out=out, n=n: e.matmul(out, before, ov[k][:, t, :, :], start=True,
                                                               stop=n == 0, skip_group_check=True))
                for m, (k2, t2) in enumerate(queue[:n]):
                    a = pe.mark(lambda e, k2=k2, t2=t2, out=out, m=m, n=n: e.matmul(
                        out, onesb, ov[k2][:, t2, :, :], start=False, stop=m == n - 1, skip_group_check=True))
            dve.wait(a)
            r4 = bank7.ap[:, 0:256].rearrange("p (k t g e) -> p k g t e", k=2, t=TPB, e=E)
            for k in range(2):
                dst = rank[:, NT * k:NT * (k + 1), :]
                for t in range(TPB):
                    a = dve.mark(lambda e, k=k, t=t, dst=dst: e.tensor_scalar(
                        dst.rearrange("p (g t) e -> p t g e", t=TPB)[:, t, :, :], r4[:, k, :, t, :], 1.0, None, ALU.add))
                dve.wait(a)
                a = dve.mark(lambda e, k=k, dst=dst: e.tensor_tensor(dst, dst, ohf[k][:, :, :], ALU.mult))
            bank7.free = [a]
            dve.wait(a)
            a = dve.mark(lambda e: e.tensor_tensor(posm[:, :, :], rank[:, 0:NT, :], rank[:, NT:2 * NT, :], ALU.add))
            dve.wait(a)
            return dve.mark(lambda e: e.tensor_scalar(posm[:, :, :], posm[:, :, :], -1.0, None, ALU.add))

        Dm = [Buffer(tmpA[:, k, :]) for k in range(2)]
        CT = [Buffer(tmpA[:, 2 + k, :]) for k in range(2)]
        Yg = [Buffer(tmpA[:, 4, :])]
        gq = [Buffer(tmpA[:, 5 + k, :]) for k in range(2)]
        iob = iota.unsqueeze(1).to_broadcast([P, E, CAP])

        def one_hot(i, n, routed):
            b = Dm[n % 2]
            dve.wait(routed, *b.free)
            return b, dve.mark(lambda e, b=b, i=i: e.tensor_tensor(
                b.ap.rearrange("p (e c) -> p e c", e=E), iob,
                posm[:, i, :].unsqueeze(2).to_broadcast([P, E, CAP]), ALU.is_equal))

        def experts1(tok, routed, weights):
            banks = (bank6, bank7)
            n = 0
            for g in range(NB):
                bank = banks[g % 2]
                pe.wait(*bank.free, *tok)
                for t in range(TPB):
                    b, a = one_hot(TPB * g + t, n, routed)
                    n += 1
                    pe.wait(a)
                    a = pe.mark(lambda e, g=g, t=t, b=b, bank=bank: e.matmul(
                        bank.ap, xn_tok[:, TPB * g + t, :], b.ap, start=t == 0, stop=t == 1))
                    b.free = [a]
                act.wait(a)
                ex = act.mark(lambda e, g=g, bank=bank: e.copy(XE[:, g, :, :],
                                                              bank.ap.rearrange("p (e c) -> p e c", e=E)))
                bank.free = [ex]
                yield
            pe.wait(ex, *weights)
            gfree = [[], []]
            n = 0
            for e_ in range(E):
                gb = e_ % 2
                for f in range(FC):
                    bank, u = banks[n % 2], gq[n % 2]
                    n += 1
                    pe.wait(*bank.free)
                    a = pe.mark(lambda e, e_=e_, f=f, bank=bank: e.matmul(
                        bank.ap, wi[:, e_, P * f:P * (f + 1)], XE[:, :, e_, :],
                        start=True, stop=True))
                    act.wait(a, *u.free)
                    a = act.mark(lambda e, bank=bank, u=u: e.activation(u.ap, bank.ap, ACT.Square,
                                                                        scale=float(np.sqrt(GELU_A))))
                    dve.wait(a)
                    a = dve.mark(lambda e, bank=bank, u=u: e.scalar_tensor_tensor(u.ap, u.ap, 1.0, bank.ap, ALU.add,
                                                                                ALU.mult))
                    act.wait(a)
                    a = act.mark(lambda e, u=u: e.activation(u.ap, u.ap, ACT.Tanh, scale=GELU_C))
                    yield
                    dve.wait(a, *gfree[gb])
                    a = dve.mark(lambda e, gb=gb, f=f, bank=bank, u=u: e.scalar_tensor_tensor(
                        G[:, gb, f, :], u.ap, 1.0, bank.ap, ALU.add, ALU.mult))
                    bank.free, u.free = [a], [a]
                    yield
                bank = banks[n % 2]
                n += 1
                pe.wait(a, *bank.free)
                for f in range(FC):
                    a = pe.mark(lambda e, e_=e_, f=f, gb=gb, bank=bank: e.matmul(
                        bank.ap, wo[:, e_, f, :], G[:, gb, f, :], start=f == 0, stop=f == FC - 1))
                gfree[gb] = [a]
                act.wait(a)
                a = act.mark(lambda e, e_=e_, bank=bank: e.mul(XE[:, :, e_, :],
                                                               bank.ap.rearrange("p (g c) -> p g c", g=NB), 0.5))
                bank.free = [a]
                experts1.done = a
                yield

        def combine(b, routed, attn_out):
            g = b
            y = Yg[0]
            pe.wait(experts1.done, *bank6.free)
            for k in range(4):
                a = pe.mark(lambda e, k=k, g=g: e.transpose(bank6.ap[:, P * k:P * (k + 1)],
                                                           XE[:, g, 2 * k:2 * k + 2, :].rearrange("p e c -> p (e c)"), ident))
            act.wait(a, *y.free)
            ym = act.mark(lambda e, y=y: e.copy(y.ap, bank6.ap))
            bank6.free = [ym]
            yield
            pe.wait(*bankV.free)
            for t in range(TPB):
                i = TPB * b + t
                dm, a = one_hot(i, t, routed)
                dve.wait(a)
                a = dve.mark(lambda e, i=i, dm=dm: e.tensor_tensor(
                    dm.ap.rearrange("p (e c) -> p e c", e=E), dm.ap.rearrange("p (e c) -> p e c", e=E),
                    pr[:, i, :].unsqueeze(2).to_broadcast([P, E, CAP]), ALU.mult))
                pe.wait(a, *bank7.free)
                for k in range(4):
                    a = pe.mark(lambda e, k=k, dm=dm: e.transpose(bank7.ap[:, P * k:P * (k + 1)],
                                                                  dm.ap[:, P * k:P * (k + 1)], ident))
                dm.free = [a]
                ct = CT[t]
                act.wait(a, *ct.free)
                a = act.mark(lambda e, ct=ct: e.copy(ct.ap, bank7.ap))
                bank7.free = [a]
                yield
                pe.wait(a, ym, attn_out, m_wo)
                ob = bankV.ap[:, P * t:P * (t + 1)]
                pe.do(lambda e, i=i, ob=ob: e.matmul(ob, attn_tok[:, i, :], wsmall[:, 6, :], start=True, stop=False,
                                                     skip_group_check=True))
                for k in range(4):
                    a = pe.mark(lambda e, k=k, ct=ct, y=y, ob=ob: e.matmul(
                        ob, ct.ap[:, P * k:P * (k + 1)], y.ap[:, P * k:P * (k + 1)], start=False, stop=k == 3,
                        skip_group_check=True))
                ct.free = [a]
                yield
            y.free = [a]
            dve.wait(a)
            xb = x_tok[:, TPB * b:TPB * (b + 1), :]
            a = dve.mark(lambda e, xb=xb: e.tensor_tensor(xb, xb, bankV.ap[:, 0:SEQ].rearrange("p (t f) -> p t f", t=TPB),
                                                          ALU.add))
            bankV.free = [a]
            sp.wait(a)
            sp.dma(g_out, lambda e, b=b, xb=xb: e.dma_start(d["out"][b].rearrange("(t p) c -> p t c", p=P), xb))
            yield

        def run(*tasks):
            live = [[t, n] for t, n in tasks]
            while live:
                for entry in list(live):
                    for _ in range(entry[1]):
                        if next(entry[0], "end") == "end":
                            live.remove(entry)
                            break

        tok0, xnT0 = layer_norm([x_in, m_ohz], [zeroed], [])
        te_m, scattered = route0(tok0, xnT0)
        run((attention(0, xnT0, None, []), 3), (experts0(te_m, scattered), 1))
        out0, added = attention.out, experts0.added
        sp.wait(added[-1])
        sp.dma(g_e1, lambda e: e.dma_start(wi, d["wi"].rearrange("e p n -> p e n")))
        sp.dma(g_e1, lambda e: e.dma_start(wo, d["wo_e"].rearrange("e (c p) n -> p e c n", p=P)))
        w_e1 = g_e1.done()
        for i in range(2):
            dve.wait(*attention.stacks[i])
            pool.wait(*attention.stacks[i])
            a = dve.mark(lambda e, i=i: e.memset(Qst[i][:, :, :], 0.0))
            k = pool.mark(lambda e, i=i: e.memset(Kst[i][:, :, :], -1.0))
            attention.stacks[i] = [a, k]
        tok1, xnT1 = layer_norm([*out0, added[-1]], [], [])
        routed = route1(xnT1)
        g_out = group("store_out")
        run((attention(1, xnT1, attention, []), 3), (experts1(tok1, routed, [w_e1]), 1))
        out1 = attention.out
        for b in range(NB):
            run((combine(b, routed, out1[b]), 1))
        for g in groups:
            sp.wait(g.done())

        block = ctx.enter_context(nc.Block())

        @block.sync
        def _(e):
            sp.play(e)

        @block.gpsimd
        def _(e):
            pool.play(e)

        @block.vector
        def _(e):
            dve.play(e)

        @block.scalar
        def _(e):
            act.play(e)

        @block.tensor
        def _(e):
            pe.play(e)


def kernel(**inputs):
    import concourse.bacc as bacc
    from concourse.bass_utils import run_bass_kernel_spmd

    a = {k: np.asarray(v) for k, v in inputs.items()}
    o0 = np.arange(D).reshape(H, HD0).T.ravel()
    o1 = np.arange(D).reshape(H, 2, HD1).transpose(2, 1, 0).ravel()
    lay = {
        "x": a["L0_attn_hidden_states"],
        "cf": constants_f32(),
        "cb": constants_masks(),
        "wsmall": np.stack([a["L0_attn_Wq"][:, o0], a["L0_attn_Wk"][:, o0], a["L0_attn_Wv"],
                            a["L1_attn_Wq"].T[:, o1], a["L1_attn_Wk"].T[:, o1], a["L1_attn_Wv"].T, a["L1_attn_Wo"].T], axis=1),
        "wr": np.stack([a["L0_ffn_router_w"], a["L1_ffn_w_router"]], axis=1),
        "rb": np.tile(a["L0_ffn_router_b"][None, :], (P, 1)),
        "bqk": np.stack([a["L0_attn_bq"][o0], a["L0_attn_bk"][o0]], axis=1),
        "bvb": np.tile(a["L0_attn_bv"][None, :], (P, 1)),
        "lamv": np.tile(np.stack([a["L1_attn_lambda_q1"], a["L1_attn_lambda_k1"], a["L1_attn_lambda_q2"],
                                  a["L1_attn_lambda_k2"]])[None], (P, 1, 1)),
        "subln": np.tile(a["L1_attn_subln_w"], H)[:, None],
        "bias": np.concatenate([a["L0_ffn_b1"].reshape(P, 64), a["L0_ffn_b2"].reshape(P, 8)], axis=1),
        "w1": a["L0_ffn_w1"], "w2": a["L0_ffn_w2"], "wi": a["L1_ffn_wi"], "wo_e": a["L1_ffn_wo"],
    }
    lay = {k: np.ascontiguousarray(v) for k, v in lay.items()}
    nc = bacc.Bacc("TRN2", target_bir_lowering=False, num_devices=1)
    d = {k: nc.dram_tensor(f"in_{k}", v.shape, mybir.dt.from_np(v.dtype), kind="ExternalInput").ap()
         for k, v in lay.items()}
    d["out"] = nc.dram_tensor("out", (NB, SEQ, D), F32, kind="ExternalOutput").ap()
    build(nc, d)
    r = run_bass_kernel_spmd(nc, [{f"in_{k}": v for k, v in lay.items()}], core_ids=[0])
    return r.results[0]["out"]
```

```python
import numpy as np
import concourse.bass as bass
from concourse import mybir
from contextlib import ExitStack

F32 = mybir.dt.float32
BF16 = mybir.dt.bfloat16
I32 = mybir.dt.int32
ALU = mybir.AluOpType
ACT = mybir.ActivationFunctionType
AX = mybir.AxisListType

P = 128
NB, SEQ, D = 8, 256, 128
NT = NB * SEQ // P
TPB = SEQ // P
H = 16
HD0 = D // H
HD1 = HD0 // 2
WINDOW = 32
NX = P + WINDOW
E, FF = 8, 512
FC = FF // P
CAP = 64
MT = NT + E - 1
EPS = 1e-5
LAMBDA_INIT = float(0.8 - 0.6 * np.exp(-0.3 * 12))
TERMS = 6
QPART = (0, 0, 0, 1, 1, 2)
KPART = (0, 1, 2, 0, 1, 0)
BIG = 1e30
VW = HD0 + 1
VROW = H * VW + 32 - VW
GELU_C = float(np.sqrt(2.0 / np.pi))
GELU_A = 0.044715


class Mark:

    def __init__(self, sem, value):
        self.sem, self.value = sem, value


class Queue:

    def __init__(self, sem):
        self.sem, self.count, self.steps, self.passed = sem, 0, [], {}

    def wait(self, *marks):
        for m in marks:
            if m is None:
                continue
            key = id(m.sem)
            if self.passed.get(key, 0) < m.value:
                self.passed[key] = m.value
                self.steps.append(lambda e, m=m: e.wait_ge(m.sem, m.value))

    def do(self, step):
        self.steps.append(step)

    def mark(self, step):
        self.count += 1
        self.steps.append(lambda e: step(e).then_inc(self.sem, 1))
        return Mark(self.sem, self.count)

    def dma(self, group, step):
        group.n += 16
        self.steps.append(lambda e: step(e).then_inc(group.sem, 16))

    def play(self, engine):
        for step in self.steps:
            step(engine)


class DmaGroup:

    def __init__(self, sem):
        self.sem, self.n = sem, 0

    def done(self):
        return Mark(self.sem, self.n)


class Buffer:

    def __init__(self, ap):
        self.ap, self.free = ap, []


def constants_f32():
    parts = [np.eye(P), np.tile(np.arange(CAP), (P, 1)), np.tile(np.arange(E, 0, -1), (P, 1)),
             np.tile(np.arange(NT) * P, (P, 1)),
             np.tile((np.arange(E)[None, :] <= np.arange(E)[:, None]).ravel(), (P, 1)),
             np.tile(np.arange(MT), (P, 1))]
    return np.concatenate(parts, axis=1).astype(np.float32)


def constants_masks():
    p = np.arange(P)[:, None]
    c = np.arange(NX)[None, :]
    mask = [np.where(np.abs(c - p) <= WINDOW, 0.0, -BIG), np.where(np.abs(c - WINDOW - p) <= WINDOW, 0.0, -BIG)]
    parts = [np.eye(P), (p < np.arange(P)[None, :]), np.ones((P, P))] + mask
    return np.concatenate(parts, axis=1).astype(np.float32)


def build(nc, d):
    ctx = ExitStack()
    with ctx:
        def sb(name, shape, dt=F32):
            return ctx.enter_context(nc.sbuf_tensor(name, shape, dt))

        def sem(name):
            return ctx.enter_context(nc.semaphore(name))

        groups = []

        def group(name):
            groups.append(DmaGroup(sem(name)))
            return groups[-1]

        pe, act, dve, pool, sp = (Queue(sem(f"done_{n}")) for n in ("pe", "act", "dve", "pool", "sp"))

        cf = sb("cf", [P, P + CAP + E + NT + E * E + MT])
        cb = sb("cb", [P, 3 * P + 2 * NX], BF16)
        at = 0
        names = {}
        for n, w in (("ident", P), ("iota", CAP), ("down", E), ("steps", NT), ("upto", E * E), ("tiles", MT)):
            names[n] = cf[:, at:at + w]
            at += w
        ident, iota, down, steps, upto, tilenr = (names[n] for n in ("ident", "iota", "down", "steps", "upto", "tiles"))
        identb, before, onesb, maskb = cb[:, 0:P], cb[:, P:2 * P], cb[:, 2 * P:3 * P], cb[:, 3 * P:]

        x_tok = sb("x_tok", [P, NT, D])
        xn_tok = sb("xn_tok", [P, NT, D])
        xnT = sb("xnT", [P, NT * P])
        attn_tok = sb("attn_tok", [P, NT, D])
        wsmall = sb("wsmall", [P, 7, D])
        wr = sb("wr", [P, 2, E])
        rb = sb("rb", [P, E])
        bqk = sb("bqk", [P, 2])
        bvb = sb("bvb", [P, D])
        lamv = sb("lamv", [P, 4, HD1])
        subln = sb("subln", [P, 1])
        regA = sb("regA", [P, E * 2 * FF + E * FC * D])
        w1 = regA[:, 0:E * 2 * FF].rearrange("p (e n) -> p e n", e=E)
        w2 = regA[:, E * 2 * FF:].rearrange("p (e c n) -> p e c n", e=E, c=FC)
        XE = regA[:, 0:4096].rearrange("p (g e c) -> p g e c", e=E, g=NB)
        G = regA[:, 4096:8192].rearrange("p (b f n) -> p b f n", b=2, f=FC)
        xn1_tok = regA[:, 4096:6144].rearrange("p (t c) -> p t c", c=D)
        xnT1 = regA[:, 6144:8192]
        tmpA = regA[:, 8192:12288].rearrange("p (k n) -> p k n", k=8)
        regB = sb("regB", [P, 2 * E * FF])
        wi = regB[:, 0:E * FF].rearrange("p (e n) -> p e n", e=E)
        wo = regB[:, E * FF:].rearrange("p (e c n) -> p e c n", e=E, c=FC)
        b1r = regB[0:3, 0:4096].bitcast(BF16).rearrange("p (e n) -> p e n", e=E)
        b2r = regB[0:3, 4096:4608].bitcast(BF16).rearrange("p (e n) -> p e n", e=E)
        xs = [Buffer(regB[:, 4608 + P * i:4608 + P * (i + 1)]) for i in range(4)]
        xsT = [Buffer(regB[:, 5120 + P * i:5120 + P * (i + 1)]) for i in range(2)]
        tg = [Buffer(regB[:, 5376 + 512 * i:5376 + 512 * (i + 1)]) for i in range(1)]
        ga = [Buffer(regB[:, 5888:6400])]
        gaT = [Buffer(regB[:, 6400:6912])]
        ysb = [Buffer(regB[:, 6912 + P * i:6912 + P * (i + 1)]) for i in range(2)]
        ygat = [Buffer(regB[:, 7168 + P * i:7168 + P * (i + 1)]) for i in range(4)]
        bias3 = sb("bias3", [P, 3, 72], BF16)
        biasf = regB[:, 7992:7992 + 144].rearrange("p (k n) -> p k n", k=2)

        Qst = [sb(f"Qst{i}", [P, H, SEQ], BF16)[:, :, :] for i in range(2)]
        Kst = [sb(f"Kst{i}", [P, H, SEQ], BF16)[:, :, :] for i in range(2)]
        Qst.append(xnT[:, :].bitcast(BF16).rearrange("p (h n) -> p h n", h=H))
        Kst.append(xn_tok[:, :, :].bitcast(BF16).rearrange("p t c -> p (t c)").rearrange("p (h n) -> p h n", h=H))
        q32 = Buffer(sb("q32", [P, 512]))
        parts = Buffer(sb("parts", [P, 3, 512], BF16))
        V = sb("V", [P, NT, VROW])
        PT = [Buffer(sb(f"PT{i}", [P, 1024])) for i in range(5)]
        OT = [Buffer(sb(f"OT{i}", [P, 512])) for i in range(2)]
        Otok = [Buffer(sb(f"Otok{i}", [P, 2 * TPB, H, VW])) for i in range(2)]
        rec = sb("rec", [P, 2 * TPB * H])
        osc = sb("osc", [P, 2 * TPB * H * HD0])
        sq = sb("sq", [P, TPB * H * HD0])
        ms = sb("ms", [P, TPB * H])
        mbuf = [sb(f"mbuf{i}", [P, TPB, 2 * H]) for i in range(2)]
        M2 = [sb(f"M2{i}", [P, TPB, 2, 2 * H], BF16) for i in range(2)]
        MTs = [Buffer(sb(f"MTs{i}", [64, SEQ], BF16)) for i in range(2)]
        mfree = [[], []]
        stats = sb("stats", [P, NT, 6])
        mv = sb("mv", [P, NT, 2])
        rstd = sb("rstd", [P, NT])
        halfneg = sb("halfneg", [P, TPB * H])
        lam = sb("lam", [P, 24])
        lg = sb("lg", [P, NT, E])
        pr = sb("pr", [P, NT, E])
        tmp8 = sb("tmp8", [P, NT, E])
        mx = sb("mx", [P, NT])
        ohf = [sb(f"ohf{k}", [P, NT, E]) for k in range(2)]
        ohb = [sb(f"ohb{k}", [P, NT + 1, E], BF16) for k in range(2)]
        rank = sb("rank", [P, 2 * NT, E])
        cnt = regB[:, 7680:7808].rearrange("p (e t) -> p e t", e=E)
        tiles_of = sb("tiles_of", [P, 2, E])
        posf = sb("posf", [P, NT])
        posi = sb("posi", [P, NT], I32)
        endsc = regB[:, 7808:7808 + MT * E].rearrange("p (t e) -> p t e", e=E)
        tef = sb("tef", [P, MT])
        tei = sb("tei", [P, MT], I32)
        posm = sb("posm", [P, NT, E])

        PS = ctx.enter_context(nc.psum_tensor("PS", [P, 8, 512], F32))
        bankA, bankB = Buffer(PS[:, 0:2, :]), Buffer(PS[:, 2:4, :])
        bankV, bankM, bank6, bank7 = (Buffer(PS[:, i, :]) for i in (4, 5, 6, 7))
        bankMb = PS[:, 5, :].bitcast(BF16)
        bank_for_ln = [bankM, bank6, bank7, bankV]
        ln_done = {}

        Q6 = [nc.dram_tensor(f"Q6_{L}", (NB, TERMS, D, SEQ), BF16, kind="Internal").ap() for L in range(2)]
        K6 = [nc.dram_tensor(f"K6_{L}", (NB, TERMS, D, SEQ), BF16, kind="Internal").ap() for L in range(2)]
        Mx = [nc.dram_tensor(f"Mx_{L}", (NB, 2, (1, 2)[L] * H, SEQ), BF16, kind="Internal").ap() for L in range(2)]
        B3 = nc.dram_tensor("B3", (3, P, 72), BF16, kind="Internal").ap()
        Xs = nc.dram_tensor("Xs", (MT * P, D), F32, kind="Internal").ap()
        Ys = nc.dram_tensor("Ys", (MT * P, D), F32, kind="Internal").ap()

        g_c, g_w, g_e0, g_e1 = (group(n) for n in ("ld_const", "ld_small", "ld_exp0", "ld_exp1"))
        w_e1 = Mark(g_e1.sem, 32)
        xin = d["x"].rearrange("b (t p) c -> p (b t) c", p=P)
        x_in = []
        for k in range(4):
            g = group(f"ld_x{k}")
            sp.dma(g, lambda e, k=k: e.dma_start(x_tok[:, 4 * k:4 * k + 4, :], xin[:, 4 * k:4 * k + 4, :]))
            x_in.append(g.done())
        sp.dma(g_c, lambda e: e.dma_start(cf[:, :], d["cf"]))
        sp.dma(g_c, lambda e: e.dma_start(PT[0].ap[:, 0:3 * P + 2 * NX], d["cb"]))
        for dst, name in ((wsmall[:, :, :], "wsmall"), (wr[:, :, :], "wr"), (rb[:, :], "rb"), (bqk[:, :], "bqk"),
                          (bvb[:, :], "bvb"), (lamv[:, :, :], "lamv"), (subln[:, :], "subln"),
                          (biasf[:, 0, :], "bias")):
            sp.dma(g_w, lambda e, dst=dst, name=name: e.dma_start(dst, d[name]))
        w1_d = d["w1"].rearrange("e p n -> p e n")
        w2_d = d["w2"].rearrange("e (c p) n -> p e c n", p=P)
        loaded, small = g_c.done(), g_w.done()
        dve.wait(loaded)
        consts = dve.mark(lambda e: e.tensor_copy(cb[:, :], PT[0].ap[:, 0:3 * P + 2 * NX]))
        PT[0].free = [consts]

        m_set = []
        for i in range(2):
            pool.do(lambda e, i=i: e.memset(Kst[i][:, :, :], -1.0))
            m_set.append(dve.mark(lambda e, i=i: e.memset(Qst[i][:, :, :], 0.0)))
        m_half = dve.mark(lambda e: e.memset(halfneg[:, :], -0.5))
        dve.do(lambda e: e.memset(V[:, :, :], 1.0))
        m_ohz = dve.mark(lambda e: e.memset(ohb[0][:, NT, :], 0.0))
        pool.do(lambda e: e.memset(attn_tok[:, 0:6, :], 0.0))
        m_kset = pool.mark(lambda e: e.memset(lam[:, :], 0.0))
        g_z = group("zero_xs")
        sp.wait(m_kset)
        xs_v = Xs.rearrange("(t p) c -> p t c", p=P)
        for k in range(0, MT, 6):
            n = min(6, MT - k)
            sp.dma(g_z, lambda e, k=k, n=n: e.dma_start(xs_v[:, k:k + n, :], attn_tok[:, 0:n, :]))
        for e_ in range(0, E, 2):
            sp.dma(g_e0, lambda e, e_=e_: e.dma_start(w1[:, e_:e_ + 2, :], w1_d[:, e_:e_ + 2, :]))
            sp.dma(g_e0, lambda e, e_=e_: e.dma_start(w2[:, e_:e_ + 2, :, :], w2_d[:, e_:e_ + 2, :, :]))
        w_e0 = g_e0.done()
        zeroed = g_z.done()

        dve.wait(small)
        dve.wait(m_kset)
        a = dve.mark(lambda e: e.tensor_tensor(lam[:, 0:8].rearrange("p (a b) -> p a b", a=2),
                                               lamv[:, 0::2, :], lamv[:, 1::2, :], ALU.mult))
        dve.wait(a)
        a = dve.mark(lambda e: e.tensor_reduce(lam[:, 8:10], lam[:, 0:8].rearrange("p (a b) -> p a b", a=2),
                                               AX.X, ALU.add))
        act.wait(a)
        a = act.mark(lambda e: e.activation(lam[:, 10:12], lam[:, 8:10], ACT.Exp))
        dve.wait(a)
        a = dve.mark(lambda e: e.tensor_tensor(lam[:, 12:13], lam[:, 11:12], lam[:, 10:11], ALU.subtract))
        dve.wait(a)
        dve.do(lambda e: e.tensor_scalar(lam[:, 13:14], lam[:, 12:13], -LAMBDA_INIT, None, ALU.add))
        m_wo = dve.mark(lambda e: e.tensor_scalar(wsmall[:, 6, :], wsmall[:, 6, :], subln[:, 0:1], 1.0 - LAMBDA_INIT,
                                                  ALU.mult, ALU.mult))
        a = dve.mark(lambda e: e.tensor_scalar(biasf[:, 0, 64:72], biasf[:, 0, 64:72], 2.0, None, ALU.mult))
        g_b = group("bias_rows")
        for k in range(3):
            src = k % 2
            dve.wait(a)
            a = dve.mark(lambda e, k=k, src=src: e.tensor_copy(bias3[:, k, :], biasf[:, src, :]))
            if k < 2:
                dve.wait(a)
                a = dve.mark(lambda e, k=k, src=src: e.tensor_tensor(biasf[:, 1 - src, :], biasf[:, src, :],
                                                                     bias3[:, k, :], ALU.subtract))
        sp.wait(a)
        sp.dma(g_b, lambda e: e.dma_start(B3.rearrange("k p n -> p k n"), bias3[:, :, :]))
        sp.wait(g_b.done())
        b1v = regB[0:3, 0:4096].bitcast(BF16).rearrange("k (q n) -> k q n", n=64)
        b2v = regB[0:3, 4096:4608].bitcast(BF16).rearrange("k (q n) -> k q n", n=8)
        sp.dma(g_b, lambda e: e.dma_start(b1v, B3[:, :, 0:64]))
        sp.dma(g_b, lambda e: e.dma_start(b2v, B3[:, :, 64:72]))
        bias_rows = g_b.done()

        def layer_norm(c, ready, dst_tok, dstT):
            lo, hi = 4 * c, 4 * c + 4
            dve.wait(*ready)
            for i in range(lo, hi):
                a = dve.mark(lambda e, i=i: e.bn_stats(stats[:, i, :], x_tok[:, i, :]))
            dve.wait(a)
            for i in range(lo, hi):
                a = dve.mark(lambda e, i=i: e.bn_aggr(mv[:, i, :], stats[:, i, :]))
            dve.wait(a)
            a = dve.mark(lambda e: e.tensor_scalar(rstd[:, lo:hi], mv[:, lo:hi, 1], EPS, None, ALU.add))
            pool.wait(a, m_half)
            a = pool.mark(lambda e: e.tensor_tensor(rstd[:, lo:hi], rstd[:, lo:hi], halfneg[:, 0:4], ALU.pow))
            yield
            dve.wait(a)
            for i in range(lo, hi):
                tok = dve.mark(lambda e, i=i: e.tensor_scalar(dst_tok[:, i, :], x_tok[:, i, :], mv[:, i, 0:1],
                                                              rstd[:, i:i + 1], ALU.subtract, ALU.mult))
            yield
            bank = bank_for_ln[c % len(bank_for_ln)]
            pe.wait(tok, consts, *bank.free)
            for i in range(4):
                a = pe.mark(lambda e, i=i: e.transpose(bank.ap[:, P * i:P * (i + 1)], dst_tok[:, lo + i, :], ident))
            act.wait(a)
            a = act.mark(lambda e: e.copy(dstT[:, 512 * c:512 * (c + 1)], bank.ap))
            bank.free = [a]
            ln_done[c] = (tok, a)
            yield

        def pick_first_max(src, out_f, out_b, ready):
            def bc(t):
                return t.unsqueeze(2).to_broadcast([P, NT, E])
            dve.wait(ready)
            a = dve.mark(lambda e: e.tensor_reduce(mx[:, :], src, AX.X, ALU.max))
            dve.wait(a)
            a = dve.mark(lambda e: e.tensor_tensor(tmp8[:, :, :], src, bc(mx[:, :]), ALU.is_equal))
            dve.wait(a)
            dw = down.unsqueeze(1).to_broadcast([P, NT, E])
            a = dve.mark(lambda e: e.tensor_tensor(tmp8[:, :, :], tmp8[:, :, :], dw, ALU.mult))
            dve.wait(a)
            a = dve.mark(lambda e: e.tensor_reduce(posf[:, :], tmp8[:, :, :], AX.X, ALU.max))
            dve.wait(a)
            a = dve.mark(lambda e: e.tensor_tensor(out_f, dw, bc(posf[:, :]), ALU.is_equal))
            dve.wait(a)
            return dve.mark(lambda e: e.tensor_copy(out_b, out_f))

        def logits(L, xT, bank):
            pe.wait(small, *(ln_done[c][1] for c in range(4)), *bank.free)
            for i in range(NT):
                a = pe.mark(lambda e, i=i: e.matmul(bank.ap[:, E * i:E * (i + 1)], xT[:, P * i:P * (i + 1)],
                                                    wr[:, L, :], start=True, stop=True))
            return a

        def route0():
            a = logits(0, xnT, bank6)
            dve.wait(a)
            a = dve.mark(lambda e: e.tensor_tensor(lg[:, :, :], bank6.ap[:, 0:NT * E].rearrange("p (t e) -> p t e", e=E),
                                                   rb[:, :].unsqueeze(1).to_broadcast([P, NT, E]), ALU.add))
            bank6.free = [a]
            dve.wait(consts)
            a = pick_first_max(lg[:, :, :], ohf[0][:, :, :], ohb[0][:, 0:NT, :], a)
            pe.wait(a, m_ohz, *bank7.free)
            rk = bank7.ap[:, 0:(NT + 1) * E]
            pe.do(lambda e: e.matmul(rk, before, ohb[0][:, :, :], start=True, stop=False, skip_group_check=True))
            for k in range(1, NT + 1):
                a = pe.mark(lambda e, k=k: e.matmul(rk[:, E * k:], onesb, ohb[0][:, 0:NT + 1 - k, :], start=False,
                                                    stop=k == NT, skip_group_check=True))
            rv = rk.rearrange("p (t e) -> p t e", e=E)
            dve.wait(a)
            a = dve.mark(lambda e: e.tensor_copy(tiles_of[:, 0, :], rv[:, NT, :]))
            dve.wait(a)
            a = dve.mark(lambda e: e.tensor_tensor(cnt[:, :, :], tiles_of[:, 0, :].unsqueeze(2).to_broadcast([P, E, NT]),
                                                   steps.unsqueeze(1).to_broadcast([P, E, NT]), ALU.is_gt))
            dve.wait(a)
            a = dve.mark(lambda e: e.tensor_reduce(tiles_of[:, 0, :], cnt[:, :, :], AX.X, ALU.add))
            dve.wait(a)
            uv = upto.rearrange("p (a b) -> p a b", a=E)
            c8 = cnt[:, :, 0:E]
            a = dve.mark(lambda e: e.tensor_tensor(c8, uv, tiles_of[:, 0, :].unsqueeze(1).to_broadcast([P, E, E]),
                                                   ALU.mult))
            dve.wait(a)
            a = dve.mark(lambda e: e.tensor_reduce(tiles_of[:, 1, :], c8, AX.X, ALU.add))
            dve.wait(a)
            dve.do(lambda e: e.tensor_tensor(endsc[:, :, :], tilenr.unsqueeze(2).to_broadcast([P, MT, E]),
                                             tiles_of[:, 1, :].unsqueeze(1).to_broadcast([P, MT, E]), ALU.is_ge))
            a = dve.mark(lambda e: e.tensor_tensor(tiles_of[:, 0, :], tiles_of[:, 1, :], tiles_of[:, 0, :],
                                                   ALU.subtract))
            dve.wait(a)
            a = dve.mark(lambda e: e.tensor_reduce(tef[:, :], endsc[:, :, :], AX.X, ALU.add))
            a = dve.mark(lambda e: e.tensor_scalar(tiles_of[:, 0, :], tiles_of[:, 0, :], float(P), None, ALU.mult))
            dve.wait(a)
            te_m = dve.mark(lambda e: e.tensor_scalar(tei[:, :], tef[:, :], float(E - 1), None, ALU.min))
            a = dve.mark(lambda e: e.tensor_tensor(rank[:, 0:NT, :], rv[:, 0:NT, :],
                                                   tiles_of[:, 0, :].unsqueeze(1).to_broadcast([P, NT, E]), ALU.add))
            bank7.free = [a]
            dve.wait(a)
            a = dve.mark(lambda e: e.tensor_tensor(rank[:, 0:NT, :], rank[:, 0:NT, :], ohf[0][:, :, :], ALU.mult))
            dve.wait(a)
            a = dve.mark(lambda e: e.tensor_reduce(posf[:, :], rank[:, 0:NT, :], AX.X, ALU.add))
            dve.wait(a)
            a = dve.mark(lambda e: e.tensor_copy(posi[:, :], posf[:, :]))
            g = group("scatter_x")
            pool.wait(a, zeroed, *(ln_done[c][0] for c in range(4)))
            for i in range(NT):
                pool.dma(g, lambda e, i=i: e.indirect_dma_start(
                    Xs, bass.IndirectOffsetOnAxis(ap=posi[:, i:i + 1], axis=0), xn_tok[:, i, :], None))
            return te_m, g.done()

        def experts0(te_m, scattered):
            pe.wait(te_m, w_e0, bias_rows, consts)
            loads, reg = {}, {}

            def load(j):
                if j < MT:
                    g = group(f"ld_xs{j}") if j < 4 else loads[j - 4]
                    sp.wait(scattered, *xs[j % 4].free)
                    sp.dma(g, lambda e: e.dma_start(xs[j % 4].ap, Xs[P * j:P * (j + 1), :]))
                    loads[j] = g
                    loads[j, "done"] = g.done()

            def turn(j):
                t = xsT[j % 2]
                pe.wait(loads[j, "done"], *bankM.free)
                a = pe.mark(lambda e: e.transpose(bankM.ap[:, 0:P], xs[j % 4].ap, ident))
                xs[j % 4].free = [a]
                load(j + 4)
                act.wait(a, *t.free)
                bankM.free = [act.mark(lambda e: e.copy(t.ap, bankM.ap[:, 0:P]))]
                reg[j, "xT"] = bankM.free[0]

            def results(j):
                pe.wait(reg[j, "gT"], *bank7.free)
                for c in range(FC):
                    pe.do(lambda e, c=c: e.matmul(bank7.ap[:, 0:D], gaT[0].ap[:, P * c:P * (c + 1)],
                                                  w2[:, bass.ds(reg[j], 1), c, :], start=c == 0, stop=False))
                a = pe.mark(lambda e: e.matmul(bank7.ap[:, 0:D], onesb[0:3, :], b2r[:, bass.ds(reg[j], 1), :],
                                               start=False, stop=True))
                gaT[0].free = [a]
                y = ysb[j % 2]
                act.wait(a, *y.free)
                a = act.mark(lambda e: e.mul(y.ap, bank7.ap[:, 0:D], 0.5))
                bank7.free = [a]
                sp.wait(a)
                if j < 2:
                    y.group = group(f"st_y{j}")
                sp.dma(y.group, lambda e: e.dma_start(Ys[P * j:P * (j + 1), :], y.ap))
                y.free = [y.group.done()]

            def hidden(j):
                t = xsT[j % 2]

                def expert_of(e):
                    reg[j] = e.value_load(tei[0:1, j:j + 1], min_val=0, max_val=E - 1)
                pe.do(expert_of)
                pe.wait(reg[j, "xT"])
                for half, bank in ((0, bank6), (1, bank7)):
                    pe.wait(*bank.free)
                    pe.do(lambda e, half=half, bank=bank: e.matmul(
                        bank.ap, t.ap, w1[:, bass.ds(reg[j], 1), FF * half:FF * (half + 1)], start=True, stop=False))
                    a = pe.mark(lambda e, half=half, bank=bank: e.matmul(
                        bank.ap, onesb[0:3, :], b1r[:, bass.ds(reg[j], 1), FF * half:FF * (half + 1)],
                        start=False, stop=True))
                t.free = [a]
                act.wait(a, *tg[0].free)
                th = act.mark(lambda e: e.activation(tg[0].ap, bank7.ap, ACT.Tanh, scale=0.5))
                bank7.free = [th]
                dve.wait(a, th, *ga[0].free)
                gm = dve.mark(lambda e: e.scalar_tensor_tensor(ga[0].ap, tg[0].ap, 1.0, bank6.ap, ALU.add, ALU.mult))
                bank6.free, tg[0].free = [gm], [gm]
                reg[j, "g"] = gm

            def turn_hidden(j):
                pe.wait(reg[j, "g"], *bank6.free)
                for c in range(FC):
                    a = pe.mark(lambda e, c=c: e.transpose(bank6.ap[:, P * c:P * (c + 1)],
                                                           ga[0].ap[:, P * c:P * (c + 1)], ident))
                ga[0].free = [a]
                dve.wait(a, *gaT[0].free)
                gt = dve.mark(lambda e: e.tensor_copy(gaT[0].ap, bank6.ap))
                bank6.free = [gt]
                reg[j, "gT"] = gt

            for j in range(4):
                load(j)
            turn(0)
            yield
            for j in range(MT):
                if j:
                    results(j - 1)
                hidden(j)
                yield
                if j + 1 < MT:
                    turn(j + 1)
                turn_hidden(j)
                yield
            results(MT - 1)
            yield
            pool.wait(*ysb[0].free, *ysb[1].free)
            gg = [group(f"gather_y{k}") for k in range(4)]
            for i in range(NT):
                b = ygat[i % 4]
                pool.wait(*b.free)
                pool.dma(gg[i % 4], lambda e, i=i, b=b: e.indirect_dma_start(
                    b.ap, None, Ys, bass.IndirectOffsetOnAxis(ap=posi[:, i:i + 1], axis=0)))
                if i >= 3:
                    add_row(i - 3, gg)
                if i % 2:
                    yield
            for i in range(NT - 3, NT):
                add_row(i, gg)
            sp.wait(x_ready[NT - 1])
            sp.dma(g_e1, lambda e: e.dma_start(wi, d["wi"].rearrange("e p n -> p e n")))
            sp.dma(g_e1, lambda e: e.dma_start(wo, d["wo_e"].rearrange("e (c p) n -> p e c n", p=P)))
            x_ready["experts"] = x_ready[NT - 1]
            yield

        def add_row(i, gg):
            b = ygat[i % 4]
            if i // 4 == (NT - 1) // 4 or True:
                dve.wait(Mark(gg[i % 4].sem, 16 * (i // 4 + 1)), x_ready.get(i))
            a = dve.mark(lambda e: e.tensor_tensor(x_tok[:, i, :], x_tok[:, i, :], b.ap, ALU.add))
            b.free = [a]
            x_ready[i] = a

        x_ready = {}

        def project(L, c, xT, st):
            hd = (HD0, HD1)[L]
            g = group(f"terms{L}_{c}")
            for which, (dst, part_of) in enumerate(((Q6[L], QPART), (K6[L], KPART))):
                pe.wait(small, ln_done[c][1], *bankM.free)
                a = pe.mark(lambda e, which=which: e.matmul(bankM.ap, wsmall[:, 3 * L + which, :],
                                                            xT[:, 512 * c:512 * (c + 1)], start=True, stop=True))
                dve.wait(a, small, *q32.free)
                sc = float(1.0 / np.sqrt(hd)) if which == 0 else 1.0
                if L == 0:
                    qm = dve.mark(lambda e, which=which, sc=sc: e.tensor_scalar(
                        q32.ap[:, :], bankM.ap, bqk[:, which:which + 1], sc, ALU.add, ALU.mult))
                else:
                    qm = dve.mark(lambda e, sc=sc: e.tensor_scalar(q32.ap[:, :], bankM.ap, sc, None, ALU.mult))
                bankM.free = [qm]
                act.wait(qm, *parts.free)
                a = act.mark(lambda e: e.copy(parts.ap[:, 0, :], q32.ap[:, :]))
                yield
                dve.wait(a)
                a = dve.mark(lambda e: e.tensor_tensor(q32.ap[:, :], q32.ap[:, :], parts.ap[:, 0, :], ALU.subtract))
                act.wait(a)
                a = act.mark(lambda e: e.copy(parts.ap[:, 1, :], q32.ap[:, :]))
                yield
                dve.wait(a)
                a = dve.mark(lambda e: e.tensor_tensor(parts.ap[:, 2, :], q32.ap[:, :], parts.ap[:, 1, :],
                                                       ALU.subtract))
                q32.free = [a]
                sp.wait(a)
                for t in range(TERMS):
                    sp.dma(g, lambda e, t=t, dst=dst, part_of=part_of: e.dma_start(
                        dst[2 * c:2 * c + 2, t, :, :].rearrange("b f n -> f b n"),
                        parts.ap[:, part_of[t], :].rearrange("p (b n) -> p b n", b=2)))
                parts.free = [g.done()]
                yield
            pe.wait(*bankM.free)
            for i in range(4):
                a = pe.mark(lambda e, i=i: e.matmul(bankM.ap[:, P * i:P * (i + 1)],
                                                    xT[:, 512 * c + P * i:512 * c + P * (i + 1)],
                                                    wsmall[:, 3 * L + 2, :], start=True, stop=True))
            st["x_read", c] = a
            vo = V[:, 4 * c:4 * c + 4, 0:H * VW].rearrange("p t (h v) -> p t h v", v=VW)
            dve.wait(a, *(V_read.get(b) for b in (2 * c, 2 * c + 1)))
            for i in range(4):
                vi = bankM.ap[:, P * i:P * (i + 1)].rearrange("p (h v) -> p h v", v=HD0)
                if L == 0:
                    a = dve.mark(lambda e, i=i, vi=vi: e.tensor_tensor(
                        vo[:, i, :, 0:HD0], vi, bvb[:, :].rearrange("p (h v) -> p h v", v=HD0), ALU.add))
                else:
                    a = dve.mark(lambda e, i=i, vi=vi: e.tensor_copy(vo[:, i, :, 0:HD0], vi))
            bankM.free = [a]
            st["V", c] = a
            st["terms", c] = g.done()
            yield

        V_read = {}
        stack_ready = [None, None, None]
        count = {"pt": 0, "ot": 0, "o": 0, "m": 0}

        def attention(L, st):
            halves = (1, 2)[L]
            rows = TERMS * (HD0, HD1)[L]
            kA = (66, 50)[L]
            kB = kA + 2
            hpu = (2, 1)[L]
            units = H // hpu
            ups = 4 // hpu
            lead = units + (4, 6)[L]
            hh = halves * H
            due = {}
            made = []
            groups_of = {}

            def after(slot, step):
                due.setdefault(slot, []).append(step)

            def load_stack(b):
                i = (b + 2 * L) % 3
                key = "stack", i
                g = groups_of.get(key) or group(f"stack{L}_{i}")
                groups_of[key] = g
                sp.wait(st["terms", b // 2], *stack_ready[i])
                for src, dst in ((Q6[L], Qst[i]), (K6[L], Kst[i])):
                    for r in range(halves):
                        v = src[b].rearrange("t (d r h) n -> (t d) r h n", r=halves, h=H)[:, r, :, :]
                        sp.dma(g, lambda e, r=r, dst=dst, v=v: e.dma_start(dst[64 * r:64 * r + rows, :, :], v))
                st["stack", b] = g.done()

            def first(n):
                b, u = divmod(n, units)
                i, Q, K = b % 2, Qst[(b + 2 * L) % 3], Kst[(b + 2 * L) % 3]
                mo = mbuf[i][:, :, 0:hh].rearrange("p q (r h) -> p r q h", r=halves)
                pe.wait(st["stack", b], consts, *bankA.free)
                if L == 0:
                    for s in range(hpu):
                        h = hpu * u + s
                        pe.do(lambda e, s=s: e.matmul(bankA.ap[:, s, 0:2 * NX], identb, maskb, start=True,
                                                      stop=False, skip_group_check=True))
                        for q in range(TPB):
                            k0 = q * (SEQ - NX)
                            a = pe.mark(lambda e, s=s, h=h, q=q, k0=k0: e.matmul(
                                bankA.ap[:, s, NX * q:NX * (q + 1)], Q[0:kA, h, P * q:P * (q + 1)],
                                K[0:kA, h, k0:k0 + NX], start=False, stop=q == 1, skip_group_check=True))
                    src = bankA.ap[:, :, 0:2 * NX].rearrange("p s (q n) -> p s q n", q=2)
                    dst = mbuf[i][:, :, 2 * u:2 * u + 2].rearrange("p q s -> p s q")
                else:
                    for q in range(TPB):
                        for r in range(2):
                            a = pe.mark(lambda e, r=r, q=q: e.matmul(
                                bankA.ap[:, r, SEQ * q:SEQ * (q + 1)], Q[64 * r:64 * r + kA, u, P * q:P * (q + 1)],
                                K[64 * r:64 * r + kA, u, :], start=True, stop=True))
                    src = bankA.ap.rearrange("p r (q n) -> p r q n", q=2)
                    dst = mo[:, :, :, u]
                dve.wait(a, *mfree[i])
                a = dve.mark(lambda e: e.tensor_reduce(dst, src, AX.X, ALU.max))
                bankA.free = [a]
                return a

            def split_max(b, ready):
                i = b % 2
                dve.wait(ready)
                a = dve.mark(lambda e: e.tensor_copy(M2[i][:, :, 0, 0:hh], mbuf[i][:, :, 0:hh]))
                dve.wait(a)
                a = dve.mark(lambda e: e.tensor_tensor(M2[i][:, :, 1, 0:hh], mbuf[i][:, :, 0:hh],
                                                       M2[i][:, :, 0, 0:hh], ALU.subtract))
                mfree[i] = [a]
                return a

            def place_max(b, ready):
                i, t = b % 2, MTs[b % 2]
                pe.wait(ready, *bankM.free)
                for k in range(2):
                    for q in range(TPB):
                        a = pe.mark(lambda e, k=k, q=q: e.transpose(
                            bankMb[32 * k:32 * k + hh, P * q:P * (q + 1)], M2[i][:, q, k, 0:hh], identb))
                dve.wait(a, *t.free)
                for k in range(2):
                    a = dve.mark(lambda e, k=k: e.tensor_copy(t.ap[32 * k:32 * k + hh, :],
                                                              bankMb[32 * k:32 * k + hh, 0:SEQ]))
                bankM.free = [a]
                key = "max", i
                g = groups_of.get(key) or group(f"max{L}_{i}")
                groups_of[key] = g
                sp.wait(a)
                for k in range(2):
                    sp.dma(g, lambda e, k=k: e.dma_start(Mx[L][b, k, :, :], t.ap[32 * k:32 * k + hh, :]))
                sp.wait(g.done())
                Q = Qst[(b + 2 * L) % 3]
                for r in range(halves):
                    sp.dma(g, lambda e, r=r: e.dma_start(Q[64 * r + kA:64 * r + kA + 2, :, :],
                                                         Mx[L][b, :, H * r:H * (r + 1), :]))
                t.free = [g.done()]
                st["max", b] = g.done()

            def second(n):
                b, u = divmod(n, units)
                Q, K = Qst[(b + 2 * L) % 3], Kst[(b + 2 * L) % 3]
                pt = PT[count["pt"] % len(PT)]
                count["pt"] += 1
                pe.wait(st["max", b], *bankB.free)
                if L == 0:
                    for s in range(hpu):
                        h = hpu * u + s
                        pe.do(lambda e, s=s: e.matmul(bankB.ap[:, s, 0:2 * NX], identb, maskb, start=True,
                                                      stop=False, skip_group_check=True))
                        for k in range(TPB):
                            q0 = k * (SEQ - NX)
                            a = pe.mark(lambda e, s=s, h=h, k=k, q0=q0: e.matmul(
                                bankB.ap[:, s, NX * k:NX * (k + 1)], K[0:kB, h, P * k:P * (k + 1)],
                                Q[0:kB, h, q0:q0 + NX], start=False, stop=k == 1, skip_group_check=True))
                    src, w = bankB.ap[:, :, 0:2 * NX], 4 * NX
                else:
                    for k in range(TPB):
                        for r in range(2):
                            a = pe.mark(lambda e, r=r, k=k: e.matmul(
                                bankB.ap[:, r, SEQ * k:SEQ * (k + 1)], K[64 * r:64 * r + kB, u, P * k:P * (k + 1)],
                                Q[64 * r:64 * r + kB, u, :], start=True, stop=True))
                    src, w = bankB.ap, 2 * 512
                if u == units - 1:
                    stack_ready[(b + 2 * L) % 3] = [a]
                    st["last", b] = a
                    if b + 3 < NB:
                        load_stack(b + 3)
                act.wait(a, *pt.free)
                a = act.mark(lambda e: e.activation(pt.ap[:, 0:w].rearrange("p (s n) -> p s n", s=2), src, ACT.Exp))
                bankB.free = [a]
                made.append((pt, a))

            def values(b, grp, mine, slot):
                ot = OT[count["ot"] % 2]
                count["ot"] += 1
                width = SEQ * halves
                pe.wait(st["V", b // 2], *bankV.free, *(m for _, m in mine))
                for k in range(TPB):
                    for c in range(4):
                        pt, _ = mine[c // hpu]
                        h = 4 * grp + c
                        if L == 0:
                            q0 = k * (SEQ - NX)
                            at_ = (c % 2) * 2 * NX + NX * k
                            rhs = pt.ap[:, at_:at_ + NX]
                            out = bankV.ap[32 * c:32 * c + 32, q0:q0 + NX]
                        else:
                            rhs = pt.ap[:, :].rearrange("p (r k n) -> p r k n", r=2, k=2)[:, :, k, :]
                            out = bankV.ap[32 * c:32 * c + 32, :]
                        a = pe.mark(lambda e, k=k, h=h, rhs=rhs, out=out: e.matmul(
                            out, V[:, TPB * b + k, VW * h:VW * h + 32], rhs, start=k == 0, stop=k == 1,
                            skip_group_check=True))
                for pt, _ in mine:
                    pt.free = [a]
                if grp == 3:
                    V_read[b] = a
                act.wait(a, *ot.free)
                a = act.mark(lambda e: e.copy(ot.ap[:, 0:width], bankV.ap[:, 0:width]))
                bankV.free = [a]
                after(slot + 1, lambda: turn(b, grp, ot, a, slot + 1))

            def turn(b, grp, ot, ready, slot):
                nblk = halves * TPB
                o = Otok[(b + L * NB) % 2]
                pe.wait(ready, *bankM.free)
                for k in range(nblk):
                    a = pe.mark(lambda e, k=k: e.transpose(bankM.ap[:, P * k:P * (k + 1)],
                                                           ot.ap[:, P * k:P * (k + 1)], ident))
                ot.free = [a]
                act.wait(a, *o.free)
                a = act.mark(lambda e: e.copy(
                    o.ap[:, 0:nblk, 4 * grp:4 * grp + 4, :],
                    bankM.ap[:, 0:P * nblk].rearrange("p (k c v) -> p k c v", k=nblk, c=4)[:, :, :, 0:VW]))
                bankM.free = [a]
                if grp == 3:
                    after(slot + 1, lambda: divide(b, o, a, slot + 1))

            def divide(b, o, ready, slot):
                n = halves * TPB * H
                dve.wait(ready)
                r = dve.mark(lambda e: e.reciprocal(rec[:, 0:n].rearrange("p (k h) -> p k h", h=H),
                                                    o.ap[:, 0:halves * TPB, :, HD0]))
                dve.wait(r)
                num = o.ap[:, 0:halves * TPB, :, 0:HD0].rearrange("p k h v -> p (k h) v")
                rb_ = rec[:, 0:n].unsqueeze(2).to_broadcast([P, n, HD0])
                if L == 0:
                    r = dve.mark(lambda e: e.tensor_tensor(osc[:, 0:SEQ].rearrange("p (k v) -> p k v", v=HD0), num,
                                                           rb_, ALU.mult))
                    o.free = [r]
                    dve.wait(r, *(x_ready.get(TPB * b + t) for t in range(TPB)))
                    xb = x_tok[:, TPB * b:TPB * (b + 1), :].rearrange("p t f -> p (t f)")
                    r = dve.mark(lambda e: e.tensor_tensor(xb, xb, osc[:, 0:SEQ], ALU.add))
                    for t in range(TPB):
                        x_ready[TPB * b + t] = r
                    st["out", b] = r
                    return
                r = dve.mark(lambda e: e.tensor_scalar(rec[:, n // 2:n], rec[:, n // 2:n], lam[:, 13:14], None,
                                                       ALU.mult))
                dve.wait(r)
                m = n // 2 * HD0
                r = dve.mark(lambda e: e.tensor_tensor(osc[:, :].rearrange("p (k v) -> p k v", v=HD0), num, rb_,
                                                       ALU.mult))
                o.free = [r]
                dve.wait(r)
                r = dve.mark(lambda e: e.tensor_tensor(osc[:, 0:m], osc[:, 0:m], osc[:, m:2 * m], ALU.add))
                dve.wait(r)
                r = dve.mark(lambda e: e.tensor_tensor(sq[:, :], osc[:, 0:m], osc[:, 0:m], ALU.mult))
                dve.wait(r)
                r = dve.mark(lambda e: e.tensor_reduce(ms[:, :], sq[:, :].rearrange("p (k v) -> p k v", v=HD0),
                                                       AX.X, ALU.add))
                dve.wait(r)
                r = dve.mark(lambda e: e.tensor_scalar(ms[:, :], ms[:, :], 1.0 / HD0, EPS, ALU.mult, ALU.add))
                pool.wait(r)
                r = pool.mark(lambda e: e.tensor_tensor(ms[:, :], ms[:, :], halfneg[:, :], ALU.pow))
                after(slot + 2, lambda: normed(b, r, slot + 2))

            def normed(b, ready, slot):
                m = TPB * H * HD0
                dve.wait(ready)
                r = dve.mark(lambda e: e.tensor_tensor(
                    sq[:, :].rearrange("p (k v) -> p k v", v=HD0), osc[:, 0:m].rearrange("p (k v) -> p k v", v=HD0),
                    ms[:, :].unsqueeze(2).to_broadcast([P, TPB * H, HD0]), ALU.mult))
                after(slot + 1, lambda: turn_out(b, r))

            def turn_out(b, ready):
                pe.wait(ready, *bankM.free)
                for q in range(TPB):
                    a = pe.mark(lambda e, q=q: e.transpose(bankM.ap[:, P * q:P * (q + 1)],
                                                           sq[:, P * q:P * (q + 1)], ident))
                act.wait(a)
                a = act.mark(lambda e: e.copy(attn_tok[:, TPB * b:TPB * (b + 1), :].rearrange("p t f -> p (t f)"),
                                              bankM.ap[:, 0:SEQ]))
                dve.wait(a)
                bankM.free = [a]
                st["out", b] = a

            n, total = -lead, NB * units
            loaded_to = 0
            while n < total or due:
                while loaded_to < min(3, NB) and ("terms", loaded_to // 2) in st and (
                        stack_ready[(loaded_to + 2 * L) % 3] is not None) and (
                        L == 0 or ("clear", (loaded_to + 2) % 3) in st):
                    load_stack(loaded_to)
                    loaded_to += 1
                    yield
                m = n + lead
                if m < total and ("stack", m // units) not in st:
                    yield
                    continue
                if 0 <= n < total:
                    second(n)
                if m < total:
                    a = first(m)
                    if m % units == units - 1:
                        s_m = split_max(m // units, a)
                        after(n + 1, lambda b=m // units, s_m=s_m: place_max(b, s_m))
                if 0 <= n < total and n % ups == ups - 1:
                    b, u = divmod(n, units)
                    mine = made[:]
                    made.clear()
                    after(n + 1, lambda b=b, u=u, mine=mine, s_=n + 1: values(b, u // ups, mine, s_))
                for step in due.pop(n, []):
                    step()
                n += 1
                yield

        def route1():
            a = logits(1, xnT1, bank6)
            lv = bank6.ap[:, 0:NT * E].rearrange("p (t e) -> p t e", e=E)
            dve.wait(a)
            a = dve.mark(lambda e: e.tensor_copy(lg[:, :, :], lv))
            bank6.free = [a]
            dve.wait(a)
            a = dve.mark(lambda e: e.tensor_reduce(mx[:, :], lg[:, :, :], AX.X, ALU.max))
            dve.wait(a)
            mxb = mx[:, :].unsqueeze(2).to_broadcast([P, NT, E])
            a = dve.mark(lambda e: e.tensor_tensor(pr[:, :, :], lg[:, :, :], mxb, ALU.subtract))
            act.wait(a)
            a = act.mark(lambda e: e.activation(pr[:, :, :], pr[:, :, :], ACT.Exp))
            dve.wait(a)
            a = dve.mark(lambda e: e.tensor_reduce(mx[:, :], pr[:, :, :], AX.X, ALU.add))
            dve.wait(a)
            a = dve.mark(lambda e: e.reciprocal(mx[:, :], mx[:, :]))
            dve.wait(a)
            a = dve.mark(lambda e: e.tensor_tensor(pr[:, :, :], pr[:, :, :], mxb, ALU.mult))
            a = pick_first_max(lg[:, :, :], ohf[0][:, :, :], ohb[0][:, 0:NT, :], a)
            dve.wait(a)
            a = dve.mark(lambda e: e.tensor_scalar(tmp8[:, :, :], ohf[0][:, :, :], -BIG, None, ALU.mult))
            dve.wait(a)
            a = dve.mark(lambda e: e.tensor_tensor(lg[:, :, :], lg[:, :, :], tmp8[:, :, :], ALU.add))
            a = pick_first_max(lg[:, :, :], ohf[1][:, :, :], ohb[1][:, 0:NT, :], a)
            ov = [ohb[k][:, 0:NT, :].rearrange("p (g t) e -> p t g e", t=TPB) for k in range(2)]
            pe.wait(a, *bank7.free)
            queue = [(0, 0), (0, 1), (1, 0), (1, 1)]
            for n, (k, t) in enumerate(queue):
                out = bank7.ap[:, 64 * n:64 * n + 64].rearrange("p (g e) -> p g e", e=E)
                pe.do(lambda e, k=k, t=t, out=out, n=n: e.matmul(out, before, ov[k][:, t, :, :], start=True,
                                                               stop=n == 0, skip_group_check=True))
                for m, (k2, t2) in enumerate(queue[:n]):
                    a = pe.mark(lambda e, k2=k2, t2=t2, out=out, m=m, n=n: e.matmul(
                        out, onesb, ov[k2][:, t2, :, :], start=False, stop=m == n - 1, skip_group_check=True))
            dve.wait(a)
            r4 = bank7.ap[:, 0:256].rearrange("p (k t g e) -> p k g t e", k=2, t=TPB, e=E)
            for k in range(2):
                dst = rank[:, NT * k:NT * (k + 1), :]
                for t in range(TPB):
                    a = dve.mark(lambda e, k=k, t=t, dst=dst: e.tensor_scalar(
                        dst.rearrange("p (g t) e -> p t g e", t=TPB)[:, t, :, :], r4[:, k, :, t, :], 1.0, None, ALU.add))
                dve.wait(a)
                a = dve.mark(lambda e, k=k, dst=dst: e.tensor_tensor(dst, dst, ohf[k][:, :, :], ALU.mult))
            bank7.free = [a]
            dve.wait(a)
            a = dve.mark(lambda e: e.tensor_tensor(posm[:, :, :], rank[:, 0:NT, :], rank[:, NT:2 * NT, :], ALU.add))
            dve.wait(a)
            return dve.mark(lambda e: e.tensor_scalar(posm[:, :, :], posm[:, :, :], -1.0, None, ALU.add))

        Dm = [Buffer(tmpA[:, k, :]) for k in range(2)]
        CT = [Buffer(tmpA[:, 2 + k, :]) for k in range(2)]
        Yg = [Buffer(tmpA[:, 4, :])]
        gq = [Buffer(tmpA[:, 5 + k, :]) for k in range(2)]
        iob = iota.unsqueeze(1).to_broadcast([P, E, CAP])

        def one_hot(i, n, routed):
            b = Dm[n % 2]
            dve.wait(routed, *b.free)
            return b, dve.mark(lambda e, b=b, i=i: e.tensor_tensor(
                b.ap.rearrange("p (e c) -> p e c", e=E), iob,
                posm[:, i, :].unsqueeze(2).to_broadcast([P, E, CAP]), ALU.is_equal))

        def experts1(routed):
            banks = (bank6, bank7)
            n = 0
            for g in range(NB):
                bank = banks[g % 2]
                for t in range(TPB):
                    b, a = one_hot(TPB * g + t, n, routed)
                    n += 1
                    yield
                    pe.wait(a, *bank.free)
                    a = pe.mark(lambda e, g=g, t=t, b=b, bank=bank: e.matmul(
                        bank.ap, xn1_tok[:, TPB * g + t, :], b.ap, start=t == 0, stop=t == 1))
                    b.free = [a]
                act.wait(a)
                ex = act.mark(lambda e, g=g, bank=bank: e.copy(XE[:, g, :, :],
                                                              bank.ap.rearrange("p (e c) -> p e c", e=E)))
                bank.free = [ex]
            last_read = a
            gfree = [[last_read], [st1["x_read", c] for c in range(4)] + [routed]]
            n = 0
            state = {}

            def hidden(e_, f, bank, u):
                pe.wait(ex, w_e1, *bank.free)
                a = pe.mark(lambda e: e.matmul(bank.ap, wi[:, e_, P * f:P * (f + 1)], XE[:, :, e_, :],
                                               start=True, stop=True))
                act.wait(a, *u.free)
                return act.mark(lambda e: e.activation(u.ap, bank.ap, ACT.Square, scale=float(np.sqrt(GELU_A))))

            def inner(bank, u, a):
                dve.wait(a)
                a = dve.mark(lambda e: e.scalar_tensor_tensor(u.ap, u.ap, 1.0, bank.ap, ALU.add, ALU.mult))
                act.wait(a)
                return act.mark(lambda e: e.activation(u.ap, u.ap, ACT.Tanh, scale=GELU_C))

            def outer(e_, f, bank, u, a):
                gb = e_ % 2
                dve.wait(a, *gfree[gb])
                a = dve.mark(lambda e: e.scalar_tensor_tensor(G[:, gb, f, :], u.ap, 1.0, bank.ap, ALU.add, ALU.mult))
                bank.free, u.free = [a], [a]
                state[e_, f] = a

            for e_ in range(E):
                pending = None
                for f in range(FC):
                    bank, u = banks[n % 2], gq[n % 2]
                    n += 1
                    a = hidden(e_, f, bank, u)
                    if pending:
                        outer(*pending)
                    yield
                    a = inner(bank, u, a)
                    pending = (e_, f, bank, u, a)
                bank = banks[n % 2]
                n += 1
                for f in range(FC):
                    if f == 1:
                        outer(*pending)
                    pe.wait(state[e_, f] if f < 3 else state[e_, 3], *(bank.free if f == 0 else []))
                    a = pe.mark(lambda e, e_=e_, f=f, bank=bank: e.matmul(
                        bank.ap, wo[:, e_, f, :], G[:, e_ % 2, f, :], start=f == 0, stop=f == FC - 1))
                    if f < 3:
                        yield
                gfree[e_ % 2] = [a]
                act.wait(a)
                a = act.mark(lambda e, e_=e_, bank=bank: e.mul(XE[:, :, e_, :],
                                                               bank.ap.rearrange("p (g c) -> p g c", g=NB), 0.5))
                bank.free = [a]
                experts1.done = a
                yield

        def combine(b, routed):
            g = b
            y = Yg[0]
            pe.wait(experts1.done, *bank6.free)
            for k in range(4):
                a = pe.mark(lambda e, k=k, g=g: e.transpose(
                    bank6.ap[:, P * k:P * (k + 1)], XE[:, g, 2 * k:2 * k + 2, :].rearrange("p e c -> p (e c)"), ident))
            act.wait(a, *y.free)
            ym = act.mark(lambda e, y=y: e.copy(y.ap, bank6.ap))
            bank6.free = [ym]
            gates = []
            for t in range(TPB):
                i = TPB * b + t
                dm, a = one_hot(i, t, routed)
                dve.wait(a)
                gates.append((dm, dve.mark(lambda e, i=i, dm=dm: e.tensor_tensor(
                    dm.ap.rearrange("p (e c) -> p e c", e=E), dm.ap.rearrange("p (e c) -> p e c", e=E),
                    pr[:, i, :].unsqueeze(2).to_broadcast([P, E, CAP]), ALU.mult))))
                yield
            turned = []
            for t in range(TPB):
                dm, a = gates[t]
                pe.wait(a, *bank7.free)
                for k in range(4):
                    a = pe.mark(lambda e, k=k, dm=dm: e.transpose(bank7.ap[:, P * k:P * (k + 1)],
                                                                  dm.ap[:, P * k:P * (k + 1)], ident))
                dm.free = [a]
                ct = CT[t]
                act.wait(a, *ct.free)
                a = act.mark(lambda e, ct=ct: e.copy(ct.ap, bank7.ap))
                bank7.free = [a]
                turned.append(a)
                yield
            while ("out", b) not in st1:
                yield
            for t in range(TPB):
                i, ct = TPB * b + t, CT[t]
                pe.wait(turned[t], ym, st1["out", b], m_wo, *bank6.free)
                ob = bank6.ap[:, P * t:P * (t + 1)]
                pe.do(lambda e, i=i, ob=ob: e.matmul(ob, attn_tok[:, i, :], wsmall[:, 6, :], start=True, stop=False,
                                                     skip_group_check=True))
                for k in range(4):
                    a = pe.mark(lambda e, k=k, ct=ct, y=y, ob=ob: e.matmul(
                        ob, ct.ap[:, P * k:P * (k + 1)], y.ap[:, P * k:P * (k + 1)], start=False, stop=k == 3,
                        skip_group_check=True))
                ct.free = [a]
                if t == 0:
                    yield
            y.free = [a]
            dve.wait(a)
            xb = x_tok[:, TPB * b:TPB * (b + 1), :]
            a = dve.mark(lambda e, xb=xb: e.tensor_tensor(xb, xb, bank6.ap[:, 0:SEQ].rearrange("p (t f) -> p t f", t=TPB),
                                                          ALU.add))
            bank6.free = [a]
            sp.wait(a)
            sp.dma(g_out, lambda e, b=b, xb=xb: e.dma_start(d["out"][b].rearrange("(t p) c -> p t c", p=P), xb))
            yield

        def run(*tasks):
            live = [[t, n, 0.0] for t, n in tasks]
            while live:
                for entry in list(live):
                    entry[2] += entry[1]
                    while entry[2] >= 1:
                        entry[2] -= 1
                        if next(entry[0], "end") == "end":
                            live.remove(entry)
                            break

        st0, st1 = {}, {}
        g_out = group("store_out")
        stack_ready[0] = stack_ready[1] = [*m_set, m_kset]

        def front0():
            for c in range(4):
                yield from layer_norm(c, [x_in[c]], xn_tok, xnT)
                if c == 0:
                    yield from project(0, 0, xnT, st0)
            te_m, scattered = route0()
            st0["routed"] = te_m, scattered
            yield
            for c in range(1, 4):
                yield from project(0, c, xnT, st0)
            pool.wait(scattered, *(st0["x_read", c] for c in range(4)), st0["routed"][0])
            pool.do(lambda e: e.memset(Qst[2], 0.0))
            stack_ready[2] = [pool.mark(lambda e: e.memset(Kst[2], -1.0))]
            yield

        def layer0_experts():
            while "routed" not in st0:
                yield
            yield from experts0(*st0["routed"])

        def front1():
            while "experts" not in x_ready:
                yield
            for c in range(4):
                while ("out", 2 * c + 1) not in st0:
                    yield
                ready = [x_ready[i] for i in range(4 * c, 4 * c + 4)]
                yield from layer_norm(c, ready, xn1_tok, xnT1)
                yield from project(1, c, xnT1, st1)

        def clear_stacks():
            for b in (5, 6, 7):
                while ("last", b) not in st0:
                    yield
                i = b % 3
                pool.wait(*stack_ready[i])
                pool.do(lambda e, i=i: e.memset(Qst[i], 0.0))
                stack_ready[i] = [pool.mark(lambda e, i=i: e.memset(Kst[i], -1.0))]
                st1["clear", i] = True
                yield

        def layer1_experts():
            while ("terms", 3) not in st1:
                yield
            routed = route1()
            st1["routed"] = routed
            yield
            yield from experts1(routed)
            for b in range(NB):
                yield from combine(b, routed)

        run((front0(), 2), (attention(0, st0), 1), (layer0_experts(), 1), (clear_stacks(), 1), (front1(), 1),
            (attention(1, st1), 1), (layer1_experts(), 1))
        for g in groups:
            sp.wait(g.done())

        block = ctx.enter_context(nc.Block())

        @block.sync
        def _(e):
            sp.play(e)

        @block.gpsimd
        def _(e):
            pool.play(e)

        @block.vector
        def _(e):
            dve.play(e)

        @block.scalar
        def _(e):
            act.play(e)

        @block.tensor
        def _(e):
            pe.play(e)


def kernel(**inputs):
    import concourse.bacc as bacc
    from concourse.bass_utils import run_bass_kernel_spmd

    a = {k: np.asarray(v) for k, v in inputs.items()}
    o0 = np.arange(D).reshape(H, HD0).T.ravel()
    o1 = np.arange(D).reshape(H, 2, HD1).transpose(2, 1, 0).ravel()
    lay = {
        "x": a["L0_attn_hidden_states"],
        "cf": constants_f32(),
        "cb": constants_masks(),
        "wsmall": np.stack([a["L0_attn_Wq"][:, o0], a["L0_attn_Wk"][:, o0], a["L0_attn_Wv"],
                            a["L1_attn_Wq"].T[:, o1], a["L1_attn_Wk"].T[:, o1], a["L1_attn_Wv"].T, a["L1_attn_Wo"].T], axis=1),
        "wr": np.stack([a["L0_ffn_router_w"], a["L1_ffn_w_router"]], axis=1),
        "rb": np.tile(a["L0_ffn_router_b"][None, :], (P, 1)),
        "bqk": np.stack([a["L0_attn_bq"][o0], a["L0_attn_bk"][o0]], axis=1),
        "bvb": np.tile(a["L0_attn_bv"][None, :], (P, 1)),
        "lamv": np.tile(np.stack([a["L1_attn_lambda_q1"], a["L1_attn_lambda_k1"], a["L1_attn_lambda_q2"],
                                  a["L1_attn_lambda_k2"]])[None], (P, 1, 1)),
        "subln": np.tile(a["L1_attn_subln_w"], H)[:, None],
        "bias": np.concatenate([a["L0_ffn_b1"].reshape(P, 64), a["L0_ffn_b2"].reshape(P, 8)], axis=1),
        "w1": a["L0_ffn_w1"], "w2": a["L0_ffn_w2"], "wi": a["L1_ffn_wi"], "wo_e": a["L1_ffn_wo"],
    }
    lay = {k: np.ascontiguousarray(v) for k, v in lay.items()}
    nc = bacc.Bacc("TRN2", target_bir_lowering=False, num_devices=1)
    d = {k: nc.dram_tensor(f"in_{k}", v.shape, mybir.dt.from_np(v.dtype), kind="ExternalInput").ap()
         for k, v in lay.items()}
    d["out"] = nc.dram_tensor("out", (NB, SEQ, D), F32, kind="ExternalOutput").ap()
    build(nc, d)
    r = run_bass_kernel_spmd(nc, [{f"in_{k}": v for k, v in lay.items()}], core_ids=[0])
    return r.results[0]["out"]
```

```python
import numpy as np
import concourse.bass as bass
from concourse import mybir
from contextlib import ExitStack

F32 = mybir.dt.float32
BF16 = mybir.dt.bfloat16
I32 = mybir.dt.int32
ALU = mybir.AluOpType
ACT = mybir.ActivationFunctionType
AX = mybir.AxisListType

P = 128
NB, SEQ, D = 8, 256, 128
NT = NB * SEQ // P
TPB = SEQ // P
H = 16
HD0 = D // H
HD1 = HD0 // 2
WINDOW = 32
NX = P + WINDOW
E, FF = 8, 512
FC = FF // P
CAP = 64
MT = NT + E - 1
EPS = 1e-5
LAMBDA_INIT = float(0.8 - 0.6 * np.exp(-0.3 * 12))
TERMS = 6
QPART = (0, 0, 0, 1, 1, 2)
KPART = (0, 1, 2, 0, 1, 0)
SCORE_ROWS = (66, 50)
TERM_RUNS = ((0, 3), (3, 2), (5, 1))
BIG = 1e30
F0, F1 = 2, 1
A1_PACE = 0.5
E0_PACE, E1_PACE = 0.6, 0.5
E0_DELAY = 20
LATE = 14
GATHER_DELAY = 2
S1 = 1
VW = HD0 + 1
VROW = H * VW + 32 - VW
GELU_C = float(np.sqrt(2.0 / np.pi))
GELU_A = 0.044715


class Mark:

    def __init__(self, sem, value):
        self.sem, self.value = sem, value


class Queue:

    def __init__(self, sem):
        self.sem, self.count, self.steps, self.passed = sem, 0, [], {}

    def wait(self, *marks):
        for m in marks:
            if m is None:
                continue
            key = id(m.sem)
            if self.passed.get(key, 0) < m.value:
                self.passed[key] = m.value
                self.steps.append(lambda e, m=m: e.wait_ge(m.sem, m.value))

    def do(self, step):
        self.steps.append(step)

    def mark(self, step):
        self.count += 1
        self.steps.append(lambda e: step(e).then_inc(self.sem, 1))
        return Mark(self.sem, self.count)

    def dma(self, group, step):
        group.n += 16
        self.steps.append(lambda e: step(e).then_inc(group.sem, 16))

    def play(self, engine):
        for step in self.steps:
            step(engine)


class DmaGroup:

    def __init__(self, sem):
        self.sem, self.n = sem, 0

    def done(self):
        return Mark(self.sem, self.n)


class Buffer:

    def __init__(self, ap):
        self.ap, self.free = ap, []


def constants_f32():
    parts = [np.eye(P), np.tile(np.arange(CAP), (P, 1)), np.tile(np.arange(E, 0, -1), (P, 1)),
             np.tile(np.arange(NT) * P, (P, 1)),
             np.tile((np.arange(E)[None, :] <= np.arange(E)[:, None]).ravel(), (P, 1)),
             np.tile(np.arange(MT), (P, 1))]
    return np.concatenate(parts, axis=1).astype(np.float32)


def constants_masks():
    p = np.arange(P)[:, None]
    c = np.arange(NX)[None, :]
    mask = [np.where(np.abs(c - p) <= WINDOW, 0.0, -BIG), np.where(np.abs(c - WINDOW - p) <= WINDOW, 0.0, -BIG)]
    parts = [np.eye(P), (p < np.arange(P)[None, :]), np.ones((P, P))] + mask
    return np.concatenate(parts, axis=1).astype(np.float32)


def build(nc, d):
    ctx = ExitStack()
    with ctx:
        def sb(name, shape, dt=F32):
            return ctx.enter_context(nc.sbuf_tensor(name, shape, dt))

        def sem(name):
            return ctx.enter_context(nc.semaphore(name))

        groups = []

        def group(name):
            groups.append(DmaGroup(sem(name)))
            return groups[-1]

        pe, act, dve, pool, sp = (Queue(sem(f"done_{n}")) for n in ("pe", "act", "dve", "pool", "sp"))

        cf = sb("cf", [P, P + CAP + E + NT + E * E + MT])
        cb = sb("cb", [P, 3 * P + 2 * NX], BF16)
        at = 0
        names = {}
        for n, w in (("ident", P), ("iota", CAP), ("down", E), ("steps", NT), ("upto", E * E), ("tiles", MT)):
            names[n] = cf[:, at:at + w]
            at += w
        ident, iota, down, steps, upto, tilenr = (names[n] for n in ("ident", "iota", "down", "steps", "upto", "tiles"))
        identb, before, onesb, maskb = cb[:, 0:P], cb[:, P:2 * P], cb[:, 2 * P:3 * P], cb[:, 3 * P:]

        x_tok = sb("x_tok", [P, NT, D])
        xn_tok = sb("xn_tok", [P, NT, D])
        xnT = sb("xnT", [P, NT * P])
        attn_tok = sb("attn_tok", [P, NT, D])
        wsmall = sb("wsmall", [P, 7, D])
        wr = sb("wr", [P, 2, E])
        rb = sb("rb", [P, E])
        bqk = sb("bqk", [P, 2])
        bvb = sb("bvb", [P, D])
        lamv = sb("lamv", [P, 4, HD1])
        subln = sb("subln", [P, 1])
        regA = sb("regA", [P, E * 2 * FF + E * FC * D])
        w1 = regA[:, 0:E * 2 * FF].rearrange("p (e n) -> p e n", e=E)
        w2 = regA[:, E * 2 * FF:].rearrange("p (e c n) -> p e c n", e=E, c=FC)
        XE = regA[:, 0:4096].rearrange("p (g e c) -> p g e c", e=E, g=NB)
        G = regA[:, 4096:8192].rearrange("p (b f n) -> p b f n", b=2, f=FC)
        xn1_tok = regA[:, 4096:6144].rearrange("p (t c) -> p t c", c=D)
        xnT1 = regA[:, 6144:8192]
        tmpA = regA[:, 8192:12288].rearrange("p (k n) -> p k n", k=8)
        regB = sb("regB", [P, 2 * E * FF])
        wi = regB[:, 0:E * FF].rearrange("p (e n) -> p e n", e=E)
        wo = regB[:, E * FF:].rearrange("p (e c n) -> p e c n", e=E, c=FC)
        b1r = regB[0:3, 0:4096].bitcast(BF16).rearrange("p (e n) -> p e n", e=E)
        b2r = regB[0:3, 4096:4608].bitcast(BF16).rearrange("p (e n) -> p e n", e=E)
        xs = [Buffer(regB[:, 4608 + P * i:4608 + P * (i + 1)]) for i in range(4)]
        xsT = [Buffer(regB[:, 5120 + P * i:5120 + P * (i + 1)]) for i in range(2)]
        tg = [Buffer(regB[:, 5376 + 512 * i:5376 + 512 * (i + 1)]) for i in range(1)]
        ga = [Buffer(regB[:, 5888:6400])]
        gaT = [Buffer(regB[:, 6400:6912])]
        ysb = [Buffer(regB[:, 6912 + P * i:6912 + P * (i + 1)]) for i in range(2)]
        ygat = regB[:, 4608:4608 + NT * P].rearrange("p (t c) -> p t c", c=D)
        bias3 = sb("bias3", [P, 3, 72], BF16)
        biasf = regB[:, 7992:7992 + 144].rearrange("p (k n) -> p k n", k=2)

        Qst = [sb(f"Qst{i}", [P, H, SEQ], BF16)[:, :, :] for i in range(2)]
        Kst = [sb(f"Kst{i}", [P, H, SEQ], BF16)[:, :, :] for i in range(2)]
        Qst.append(xnT[:, :].bitcast(BF16).rearrange("p (h n) -> p h n", h=H))
        Kst.append(xn_tok[:, :, :].bitcast(BF16).rearrange("p t c -> p (t c)").rearrange("p (h n) -> p h n", h=H))
        late_tok = attn_tok[:, 6:16, :].rearrange("p t c -> p (t c)")
        q32s = [Buffer(sb("q32", [P, 512])[:, :]), Buffer(late_tok[:, 0:512])]
        partss = [Buffer(sb("parts", [P, 3, 512], BF16)[:, :, :]),
                  Buffer(late_tok[:, 512:1280].bitcast(BF16).rearrange("p (k n) -> p k n", k=3))]
        V = sb("V", [P, NT, VROW])
        PT = [Buffer(sb(f"PT{i}", [P, 1024])) for i in range(5)]
        OT = [Buffer(sb(f"OT{i}", [P, 512])) for i in range(2)]
        Otok = [Buffer(sb(f"Otok{i}", [P, 2 * TPB, H, VW])) for i in range(2)]
        rec = sb("rec", [P, 2 * TPB * H])
        osc = sb("osc", [P, 2 * TPB * H * HD0])
        sq = sb("sq", [P, TPB * H * HD0])
        ms = sb("ms", [P, TPB * H])
        mbuf = [sb(f"mbuf{i}", [P, TPB, 2 * H]) for i in range(2)]
        M2 = [sb(f"M2{i}", [P, TPB, 2, 2 * H], BF16) for i in range(2)]
        MTs = [Buffer(sb(f"MTs{i}", [64, SEQ], BF16)) for i in range(2)]
        mfree = [[], []]
        stats = sb("stats", [P, NT, 6])
        mv = sb("mv", [P, NT, 2])
        rstd = sb("rstd", [P, NT])
        halfneg = sb("halfneg", [P, TPB * H])
        lam = sb("lam", [P, 24])
        lg = sb("lg", [P, NT, E])
        pr = sb("pr", [P, NT, E])
        tmp8 = sb("tmp8", [P, NT, E])
        mx = sb("mx", [P, NT])
        ohf = [sb(f"ohf{k}", [P, NT, E]) for k in range(2)]
        ohb = [sb(f"ohb{k}", [P, NT + 1, E], BF16) for k in range(2)]
        rank = sb("rank", [P, 2 * NT, E])
        cnt = regB[:, 7680:7808].rearrange("p (e t) -> p e t", e=E)
        tiles_of = sb("tiles_of", [P, 2, E])
        posf = sb("posf", [P, NT])
        posi = sb("posi", [P, NT], I32)
        endsc = regB[:, 7808:7808 + MT * E].rearrange("p (t e) -> p t e", e=E)
        tef = sb("tef", [P, MT])
        tei = sb("tei", [P, MT], I32)
        posm = sb("posm", [P, NT, E])

        PS = ctx.enter_context(nc.psum_tensor("PS", [P, 8, 512], F32))
        bankA, bankB = ([Buffer(PS[:, i + k, :]) for k in range(2)] for i in (0, 2))
        bankV, bankM, bank6, bank7 = (Buffer(PS[:, i, :]) for i in (4, 5, 6, 7))
        bank_for_ln = [bank7, bankV, bank7, bankV]
        ln_done = {}

        Q6 = [nc.dram_tensor(f"Q6_{L}", (NB // 2, TERMS, D, 2, SEQ), BF16, kind="Internal").ap() for L in range(2)]
        K6 = [nc.dram_tensor(f"K6_{L}", (NB // 2, TERMS, D, 2, SEQ), BF16, kind="Internal").ap() for L in range(2)]
        Mx = [nc.dram_tensor(f"Mx_{L}", (NB, 2, (1, 2)[L] * H, SEQ), BF16, kind="Internal").ap() for L in range(2)]
        B3 = nc.dram_tensor("B3", (3, P, 72), BF16, kind="Internal").ap()
        empty = SCORE_ROWS[1] - TERMS * HD1
        ZR = -(-empty * H * SEQ // (6 * D * 2))
        Zd = nc.dram_tensor("Zd", (ZR, 6 * D * 2), BF16, kind="Internal").ap()
        Xs = nc.dram_tensor("Xs", (MT * P, D), F32, kind="Internal").ap()
        Ys = nc.dram_tensor("Ys", (MT * P, D), F32, kind="Internal").ap()

        g_c, g_w, g_e0, g_e1 = (group(n) for n in ("ld_const", "ld_small", "ld_exp0", "ld_exp1"))
        w_e1 = Mark(g_e1.sem, 32)
        xin = d["x"].rearrange("b (t p) c -> p (b t) c", p=P)
        x_in = []
        for k in range(4):
            g = group(f"ld_x{k}")
            sp.dma(g, lambda e, k=k: e.dma_start(x_tok[:, 4 * k:4 * k + 4, :], xin[:, 4 * k:4 * k + 4, :]))
            x_in.append(g.done())
        sp.dma(g_c, lambda e: e.dma_start(cf[:, :], d["cf"]))
        sp.dma(g_c, lambda e: e.dma_start(PT[0].ap[:, 0:3 * P + 2 * NX], d["cb"]))
        for dst, name in ((wsmall[:, :, :], "wsmall"), (wr[:, :, :], "wr"), (rb[:, :], "rb"), (bqk[:, :], "bqk"),
                          (bvb[:, :], "bvb"), (lamv[:, :, :], "lamv"), (subln[:, :], "subln"),
                          (biasf[:, 0, :], "bias")):
            sp.dma(g_w, lambda e, dst=dst, name=name: e.dma_start(dst, d[name]))
        w1_d = d["w1"].rearrange("e p n -> p e n")
        w2_d = d["w2"].rearrange("e (c p) n -> p e c n", p=P)
        loaded, small = g_c.done(), g_w.done()

        pool.do(lambda e: e.memset(lam[:, :], 0.0))
        m_zero = pool.mark(lambda e: e.memset(attn_tok[:, 0:6, :], 0.0))
        m_half = dve.mark(lambda e: e.memset(halfneg[:, :], -0.5))
        m_ohz = dve.mark(lambda e: e.memset(ohb[0][:, NT, :], 0.0))
        dve.do(lambda e: e.memset(V[:, :, 0:H * VW].rearrange("p t (h v) -> p t h v", v=VW)[:, :, :, HD0], 1.0))
        m_ones = dve.mark(lambda e: e.memset(V[:, :, H * VW:], 1.0))
        m_set = [m_ones]

        def fill_stacks():
            for i in range(2):
                m_set.append(pool.mark(lambda e, i=i: e.memset(Qst[i][:, :, :], 0.0)))
                m_set.append(pool.mark(lambda e, i=i: e.memset(Kst[i][:, :, :], -1.0)))

        g_z = group("zero_xs")
        sp.wait(m_zero)
        xs_v = Xs.rearrange("(t p) c -> p t c", p=P)
        for k in range(0, MT, 6):
            n = min(6, MT - k)
            sp.dma(g_z, lambda e, k=k, n=n: e.dma_start(xs_v[:, k:k + n, :], attn_tok[:, 0:n, :]))
        sp.dma(g_z, lambda e: e.dma_start(Zd[:, :], attn_tok[0:ZR, 0:6, :].rearrange("p t c -> p (t c)").bitcast(BF16)))
        zeroed = g_z.done()
        act.wait(loaded)
        consts = act.mark(lambda e: e.copy(cb[:, :], PT[0].ap[:, 0:3 * P + 2 * NX]))
        PT[0].free = [consts]
        for e_ in range(0, E, 2):
            sp.dma(g_e0, lambda e, e_=e_: e.dma_start(w1[:, e_:e_ + 2, :], w1_d[:, e_:e_ + 2, :]))
            sp.dma(g_e0, lambda e, e_=e_: e.dma_start(w2[:, e_:e_ + 2, :, :], w2_d[:, e_:e_ + 2, :, :]))
        w_e0 = g_e0.done()
        dve.wait(small)
        b_ready = dve.mark(lambda e: e.tensor_scalar(bqk[:, 0:1], bqk[:, 0:1], float(1.0 / np.sqrt(HD0)), None,
                                                     ALU.mult))
        late = {}

        def set_up_late():
            for _ in range(LATE):
                yield
            dve.wait(small, m_zero)
            a = dve.mark(lambda e: e.tensor_tensor(lam[:, 0:8].rearrange("p (a b) -> p a b", a=2),
                                                   lamv[:, 0::2, :], lamv[:, 1::2, :], ALU.mult))
            dve.wait(a)
            a = dve.mark(lambda e: e.tensor_reduce(lam[:, 8:10], lam[:, 0:8].rearrange("p (a b) -> p a b", a=2),
                                                   AX.X, ALU.add))
            act.wait(a)
            a = act.mark(lambda e: e.activation(lam[:, 10:12], lam[:, 8:10], ACT.Exp))
            dve.wait(a)
            a = dve.mark(lambda e: e.tensor_tensor(lam[:, 12:13], lam[:, 11:12], lam[:, 10:11], ALU.subtract))
            dve.wait(a)
            yield
            dve.do(lambda e: e.tensor_scalar(lam[:, 13:14], lam[:, 12:13], -LAMBDA_INIT, None, ALU.add))
            late["wo"] = dve.mark(lambda e: e.tensor_scalar(wsmall[:, 6, :], wsmall[:, 6, :], subln[:, 0:1], 1.0 - LAMBDA_INIT,
                                                              ALU.mult, ALU.mult))
            yield
            a = dve.mark(lambda e: e.tensor_scalar(biasf[:, 0, 64:72], biasf[:, 0, 64:72], 2.0, None, ALU.mult))
            g_b = group("bias_rows")
            for k in range(3):
                src = k % 2
                dve.wait(a)
                a = dve.mark(lambda e, k=k, src=src: e.tensor_copy(bias3[:, k, :], biasf[:, src, :]))
                if k < 2:
                    dve.wait(a)
                    a = dve.mark(lambda e, k=k, src=src: e.tensor_tensor(biasf[:, 1 - src, :], biasf[:, src, :],
                                                                         bias3[:, k, :], ALU.subtract))
            sp.wait(a)
            sp.dma(g_b, lambda e: e.dma_start(B3.rearrange("k p n -> p k n"), bias3[:, :, :]))
            sp.wait(g_b.done())
            b1v = regB[0:3, 0:4096].bitcast(BF16).rearrange("k (q n) -> k q n", n=64)
            b2v = regB[0:3, 4096:4608].bitcast(BF16).rearrange("k (q n) -> k q n", n=8)
            sp.dma(g_b, lambda e: e.dma_start(b1v, B3[:, :, 0:64]))
            sp.dma(g_b, lambda e: e.dma_start(b2v, B3[:, :, 64:72]))
            late["bias"] = g_b.done()
            yield

        def side_by_side(*tasks):
            live = list(tasks)
            while live:
                for t in list(live):
                    if next(t, "end") == "end":
                        live.remove(t)
                yield

        def layer_norm(c, ready, dst_tok, dstT):
            lo, hi = 4 * c, 4 * c + 4
            dve.wait(*ready)
            for i in range(lo, hi):
                a = dve.mark(lambda e, i=i: e.bn_stats(stats[:, i, :], x_tok[:, i, :]))
            dve.wait(a)
            for i in range(lo, hi):
                a = dve.mark(lambda e, i=i: e.bn_aggr(mv[:, i, :], stats[:, i, :]))
            dve.wait(a)
            a = dve.mark(lambda e: e.tensor_scalar(rstd[:, lo:hi], mv[:, lo:hi, 1], EPS, None, ALU.add))
            pool.wait(a, m_half)
            a = pool.mark(lambda e: e.tensor_tensor(rstd[:, lo:hi], rstd[:, lo:hi], halfneg[:, 0:4], ALU.pow))
            yield
            dve.wait(a)
            for i in range(lo, hi):
                tok = dve.mark(lambda e, i=i: e.tensor_scalar(dst_tok[:, i, :], x_tok[:, i, :], mv[:, i, 0:1],
                                                              rstd[:, i:i + 1], ALU.subtract, ALU.mult))
            yield
            bank = bank_for_ln[c % len(bank_for_ln)]
            pe.wait(tok, consts, *bank.free)
            for i in range(4):
                a = pe.mark(lambda e, i=i: e.transpose(bank.ap[:, P * i:P * (i + 1)], dst_tok[:, lo + i, :], ident))
            act.wait(a)
            a = act.mark(lambda e: e.copy(dstT[:, 512 * c:512 * (c + 1)], bank.ap))
            bank.free = [a]
            ln_done[c] = (tok, a)
            yield

        def pick_first_max(src, out_f, out_b, ready):
            def bc(t):
                return t.unsqueeze(2).to_broadcast([P, NT, E])
            dve.wait(ready)
            a = dve.mark(lambda e: e.tensor_reduce(mx[:, :], src, AX.X, ALU.max))
            dve.wait(a)
            a = dve.mark(lambda e: e.tensor_tensor(tmp8[:, :, :], src, bc(mx[:, :]), ALU.is_equal))
            dve.wait(a)
            dw = down.unsqueeze(1).to_broadcast([P, NT, E])
            yield
            a = dve.mark(lambda e: e.tensor_tensor(tmp8[:, :, :], tmp8[:, :, :], dw, ALU.mult))
            dve.wait(a)
            a = dve.mark(lambda e: e.tensor_reduce(posf[:, :], tmp8[:, :, :], AX.X, ALU.max))
            yield
            dve.wait(a)
            a = dve.mark(lambda e: e.tensor_tensor(out_f, dw, bc(posf[:, :]), ALU.is_equal))
            dve.wait(a)
            a = dve.mark(lambda e: e.tensor_copy(out_b, out_f))
            yield
            return a

        def logits(L, c, xT, bank):
            pe.wait(small, ln_done[c][1], *(bank.free if c == 0 else []))
            for i in range(4 * c, 4 * c + 4):
                a = pe.mark(lambda e, i=i: e.matmul(bank.ap[:, E * i:E * (i + 1)], xT[:, P * i:P * (i + 1)],
                                                    wr[:, L, :], start=True, stop=True))
            return a

        def route0():
            for c in range(4):
                a = logits(0, c, xnT, bank6)
                yield
            dve.wait(a, small)
            a = dve.mark(lambda e: e.tensor_tensor(lg[:, :, :], bank6.ap[:, 0:NT * E].rearrange("p (t e) -> p t e", e=E),
                                                   rb[:, :].unsqueeze(1).to_broadcast([P, NT, E]), ALU.add))
            bank6.free = [a]
            dve.wait(consts)
            a = yield from pick_first_max(lg[:, :, :], ohf[0][:, :, :], ohb[0][:, 0:NT, :], a)
            yield
            pe.wait(a, m_ohz, *bank7.free)
            rk = bank7.ap[:, 0:(NT + 1) * E]
            pe.do(lambda e: e.matmul(rk, before, ohb[0][:, :, :], start=True, stop=False, skip_group_check=True))
            for k in range(1, NT + 1):
                a = pe.mark(lambda e, k=k: e.matmul(rk[:, E * k:], onesb, ohb[0][:, 0:NT + 1 - k, :], start=False,
                                                    stop=k == NT, skip_group_check=True))
            rv = rk.rearrange("p (t e) -> p t e", e=E)
            dve.wait(a)
            a = dve.mark(lambda e: e.tensor_copy(tiles_of[:, 0, :], rv[:, NT, :]))
            dve.wait(a)
            a = dve.mark(lambda e: e.tensor_tensor(cnt[:, :, :], tiles_of[:, 0, :].unsqueeze(2).to_broadcast([P, E, NT]),
                                                   steps.unsqueeze(1).to_broadcast([P, E, NT]), ALU.is_gt))
            dve.wait(a)
            a = dve.mark(lambda e: e.tensor_reduce(tiles_of[:, 0, :], cnt[:, :, :], AX.X, ALU.add))
            dve.wait(a)
            uv = upto.rearrange("p (a b) -> p a b", a=E)
            c8 = cnt[:, :, 0:E]
            a = dve.mark(lambda e: e.tensor_tensor(c8, uv, tiles_of[:, 0, :].unsqueeze(1).to_broadcast([P, E, E]),
                                                   ALU.mult))
            dve.wait(a)
            a = dve.mark(lambda e: e.tensor_reduce(tiles_of[:, 1, :], c8, AX.X, ALU.add))
            dve.wait(a)
            dve.do(lambda e: e.tensor_tensor(endsc[:, :, :], tilenr.unsqueeze(2).to_broadcast([P, MT, E]),
                                             tiles_of[:, 1, :].unsqueeze(1).to_broadcast([P, MT, E]), ALU.is_ge))
            a = dve.mark(lambda e: e.tensor_tensor(tiles_of[:, 0, :], tiles_of[:, 1, :], tiles_of[:, 0, :],
                                                   ALU.subtract))
            dve.wait(a)
            a = dve.mark(lambda e: e.tensor_reduce(tef[:, :], endsc[:, :, :], AX.X, ALU.add))
            a = dve.mark(lambda e: e.tensor_scalar(tiles_of[:, 0, :], tiles_of[:, 0, :], float(P), None, ALU.mult))
            dve.wait(a)
            te_m = dve.mark(lambda e: e.tensor_scalar(tei[:, :], tef[:, :], float(E - 1), None, ALU.min))
            a = dve.mark(lambda e: e.tensor_tensor(rank[:, 0:NT, :], rv[:, 0:NT, :],
                                                   tiles_of[:, 0, :].unsqueeze(1).to_broadcast([P, NT, E]), ALU.add))
            bank7.free = [a]
            dve.wait(a)
            a = dve.mark(lambda e: e.tensor_tensor(rank[:, 0:NT, :], rank[:, 0:NT, :], ohf[0][:, :, :], ALU.mult))
            dve.wait(a)
            a = dve.mark(lambda e: e.tensor_reduce(posf[:, :], rank[:, 0:NT, :], AX.X, ALU.add))
            dve.wait(a)
            a = dve.mark(lambda e: e.tensor_copy(posi[:, :], posf[:, :]))
            g = group("scatter_x")
            pool.wait(a, zeroed, *(ln_done[c][0] for c in range(4)))
            for i in range(NT):
                pool.dma(g, lambda e, i=i: e.indirect_dma_start(
                    Xs, bass.IndirectOffsetOnAxis(ap=posi[:, i:i + 1], axis=0), xn_tok[:, i, :], None))
            st0["routed"] = te_m, g.done()
            yield

        def experts0(te_m, scattered):
            pe.wait(te_m, w_e0, late["bias"], consts)
            loads, reg = {}, {}

            def load(j):
                if j < MT:
                    g = group(f"ld_xs{j}") if j < 4 else loads[j - 4]
                    sp.wait(scattered, *xs[j % 4].free)
                    sp.dma(g, lambda e: e.dma_start(xs[j % 4].ap, Xs[P * j:P * (j + 1), :]))
                    loads[j] = g
                    loads[j, "done"] = g.done()

            def turn(j):
                t = xsT[j % 2]
                pe.wait(loads[j, "done"], *bankM.free)
                a = pe.mark(lambda e: e.transpose(bankM.ap[:, 0:P], xs[j % 4].ap, ident))
                xs[j % 4].free = [a]
                load(j + 4)
                act.wait(a, *t.free)
                bankM.free = [act.mark(lambda e: e.copy(t.ap, bankM.ap[:, 0:P]))]
                reg[j, "xT"] = bankM.free[0]

            def results(j):
                pe.wait(reg[j, "gT"], *bank6.free)
                for c in range(FC):
                    pe.do(lambda e, c=c: e.matmul(bank6.ap[:, 0:D], gaT[0].ap[:, P * c:P * (c + 1)],
                                                  w2[:, bass.ds(reg[j], 1), c, :], start=c == 0, stop=False))
                a = pe.mark(lambda e: e.matmul(bank6.ap[:, 0:D], onesb[0:3, :], b2r[:, bass.ds(reg[j], 1), :],
                                               start=False, stop=True))
                gaT[0].free = [a]
                y = ysb[j % 2]
                act.wait(a, *y.free)
                a = act.mark(lambda e: e.mul(y.ap, bank6.ap[:, 0:D], 0.5))
                bank6.free = [a]
                sp.wait(a)
                if j < 2:
                    y.group = group(f"st_y{j}")
                sp.dma(y.group, lambda e: e.dma_start(Ys[P * j:P * (j + 1), :], y.ap))
                y.free = [y.group.done()]

            def hidden(j):
                t = xsT[j % 2]

                def expert_of(e):
                    reg[j] = e.value_load(tei[0:1, j:j + 1], min_val=0, max_val=E - 1)
                pe.do(expert_of)
                pe.wait(reg[j, "xT"])
                for half, bank in ((1, bank7), (0, bank6)):
                    pe.wait(*bank.free)
                    pe.do(lambda e, half=half, bank=bank: e.matmul(
                        bank.ap, t.ap, w1[:, bass.ds(reg[j], 1), FF * half:FF * (half + 1)], start=True, stop=False))
                    a = pe.mark(lambda e, half=half, bank=bank: e.matmul(
                        bank.ap, onesb[0:3, :], b1r[:, bass.ds(reg[j], 1), FF * half:FF * (half + 1)],
                        start=False, stop=True))
                    if half:
                        gate = a
                t.free = [a]
                act.wait(gate, *tg[0].free)
                th = act.mark(lambda e: e.activation(tg[0].ap, bank7.ap, ACT.Tanh, scale=0.5))
                bank7.free = [th]
                dve.wait(a, th, *ga[0].free)
                gm = dve.mark(lambda e: e.scalar_tensor_tensor(ga[0].ap, tg[0].ap, 1.0, bank6.ap, ALU.add, ALU.mult))
                bank6.free, tg[0].free = [gm], [gm]
                reg[j, "g"] = gm

            def turn_hidden(j):
                pe.wait(reg[j, "g"], *bank7.free)
                for c in range(FC):
                    a = pe.mark(lambda e, c=c: e.transpose(bank7.ap[:, P * c:P * (c + 1)],
                                                           ga[0].ap[:, P * c:P * (c + 1)], ident))
                ga[0].free = [a]
                dve.wait(a, *gaT[0].free)
                gt = dve.mark(lambda e: e.tensor_copy(gaT[0].ap, bank7.ap))
                bank7.free = [gt]
                reg[j, "gT"] = gt

            for j in range(4):
                load(j)
            turn(0)
            yield
            for j in range(MT):
                if j:
                    results(j - 1)
                hidden(j)
                yield
                if j + 1 < MT:
                    turn(j + 1)
                turn_hidden(j)
                yield
            results(MT - 1)
            yield
            pool.wait(*ysb[0].free, *ysb[1].free)
            def add_rows(c):
                rows = slice(4 * c, 4 * c + 4)
                dve.wait(st0["gathered", c], *(x_ready.get(i) for i in range(4 * c, 4 * c + 4)))
                a = dve.mark(lambda e: e.tensor_tensor(x_tok[:, rows, :], x_tok[:, rows, :], ygat[:, rows, :],
                                                       ALU.add))
                for i in range(4 * c, 4 * c + 4):
                    x_ready[i] = a
                st0["added", c] = True

            for c in range(4):
                g = group(f"gather_y{c}")
                for i in range(4 * c, 4 * c + 4):
                    pool.dma(g, lambda e, i=i: e.indirect_dma_start(
                        ygat[:, i, :], None, Ys, bass.IndirectOffsetOnAxis(ap=posi[:, i:i + 1], axis=0)))
                    if i % 2:
                        yield
                st0["gathered", c] = g.done()
                for _ in range(GATHER_DELAY):
                    yield
                if c:
                    add_rows(c - 1)
            for _ in range(GATHER_DELAY):
                yield
            add_rows(3)
            sp.wait(x_ready[NT - 1])
            sp.dma(g_e1, lambda e: e.dma_start(wi, d["wi"].rearrange("e p n -> p e n")))
            sp.dma(g_e1, lambda e: e.dma_start(wo, d["wo_e"].rearrange("e (c p) n -> p e c n", p=P)))
            yield

        x_ready = {}

        def project(L, c, xT, st):
            hd = (HD0, HD1)[L]
            landed = [group(f"terms{L}_{c}_{n}") for n in "qk"]

            def split(which):
                dst, g = (Q6[L], K6[L])[which], landed[which]
                q32, parts = q32s[which], partss[which]
                pe.wait(small, ln_done[c][1], *bankM.free)
                a = pe.mark(lambda e, which=which: e.matmul(bankM.ap, wsmall[:, 3 * L + which, :],
                                                            xT[:, 512 * c:512 * (c + 1)], start=True, stop=True))
                act.wait(a, b_ready, *q32.free)
                sc = float(1.0 / np.sqrt(hd)) if which == 0 else 1.0
                bias = bqk[:, which:which + 1] if L == 0 else 0.0
                qm = act.mark(lambda e: e.activation(q32.ap[:, :], bankM.ap, ACT.Identity, bias=bias, scale=sc))
                bankM.free = [qm]
                act.wait(qm, *parts.free)
                a = act.mark(lambda e: e.copy(parts.ap[:, 0, :], q32.ap[:, :]))
                yield
                rest = pool if L == 1 and which == 1 else dve
                rest.wait(a)
                a = rest.mark(lambda e: e.tensor_tensor(q32.ap[:, :], q32.ap[:, :], parts.ap[:, 0, :], ALU.subtract))
                act.wait(a)
                a = act.mark(lambda e: e.copy(parts.ap[:, 1, :], q32.ap[:, :]))
                yield
                dve.wait(a)
                a = dve.mark(lambda e: e.tensor_tensor(parts.ap[:, 2, :], q32.ap[:, :], parts.ap[:, 1, :],
                                                       ALU.subtract))
                q32.free = [a]
                sp.wait(a)
                for t, n in TERM_RUNS:
                    src = parts.ap[:, QPART[t]:QPART[t] + 1, :].to_broadcast([P, n, 512]) if which == 0 else (
                        parts.ap[:, 0:n, :])
                    sp.dma(g, lambda e, t=t, n=n, dst=dst, src=src: e.dma_start(
                        dst[c, t:t + n, :, :, :].rearrange("t f b n -> f t (b n)"), src))
                parts.free = [g.done()]
                yield

            yield from side_by_side(split(0), split(1))
            pe.wait(*bankM.free)
            for i in range(4):
                a = pe.mark(lambda e, i=i: e.matmul(bankM.ap[:, P * i:P * (i + 1)],
                                                    xT[:, 512 * c + P * i:512 * c + P * (i + 1)],
                                                    wsmall[:, 3 * L + 2, :], start=True, stop=True))
            st["x_read", c] = a
            vo = V[:, 4 * c:4 * c + 4, 0:H * VW].rearrange("p t (h v) -> p t h v", v=VW)
            vi = bankM.ap.rearrange("p (t h v) -> p t h v", t=4, v=HD0)
            if L == 0:
                bv = bvb[:, :].rearrange("p (h v) -> p h v", v=HD0).unsqueeze(1).to_broadcast([P, 4, H, HD0])
                dve.wait(a, small)
                a = dve.mark(lambda e: e.tensor_tensor(vo[:, :, :, 0:HD0], vi, bv, ALU.add))
            else:
                act.wait(a, *(V_read.get(b) for b in (2 * c, 2 * c + 1)))
                a = act.mark(lambda e: e.copy(vo[:, :, :, 0:HD0], vi))
            bankM.free = [a]
            st["V", c] = a
            st["terms", c] = [g.done() for g in landed]
            yield

        V_read = {}
        stack_ready = [None, None, None]
        count = {"pt": 0, "ot": 0, "o": 0, "m": 0}

        def attention(L, st):
            halves = (1, 2)[L]
            rows = TERMS * (HD0, HD1)[L]
            kA = SCORE_ROWS[L]
            kB = kA + 2
            hpu = (2, 1)[L]
            units = H // hpu
            ups = 4 // hpu
            lead = units + (4, 6)[L]
            hh = halves * H
            bankT = (bankM, bankV)[L]
            bankTb = bankT.ap.bitcast(BF16)
            due = {}
            made = []
            groups_of = {}

            def after(slot, step):
                due.setdefault(slot, []).append(step)

            def order(alone):
                return [(r, t) for r in range(2) for t in range(2)] if alone else [
                    (r, t) for t in range(2) for r in range(2)]

            def load_stack(b):
                i = (b + 2 * L) % 3
                key = "stack", i
                g = groups_of.get(key) or group(f"stack{L}_{i}")
                groups_of[key] = g
                sp.wait(zeroed, *st["terms", b // 2], *stack_ready[i])
                for src, dst in ((Q6[L], Qst[i]), (K6[L], Kst[i])):
                    for r in range(halves):
                        v = src[b // 2, :, :, b % 2, :].rearrange("t (d r h) n -> (t d) r h n", r=halves, h=H)[:, r, :, :]
                        sp.dma(g, lambda e, r=r, dst=dst, v=v: e.dma_start(dst[64 * r:64 * r + rows, :, :], v))
                if L == 1 and b < 3:
                    sp.dma(g, lambda e: e.dma_start(
                        Qst[i][rows:kA, :, :],
                        Zd.rearrange("a b -> (a b)")[0:empty * H * SEQ].rearrange("(r h n) -> r h n", r=empty, h=H)))
                st["stack", b] = g.done()

            def first(n, alone):
                b, u = divmod(n, units)
                i, Q, K = b % 2, Qst[(b + 2 * L) % 3], Kst[(b + 2 * L) % 3]
                pe.wait(st["stack", b], consts)
                filled = [None, None]
                if L == 0:
                    for s, bank in enumerate(bankA):
                        h = hpu * u + s
                        pe.wait(*bank.free)
                        pe.do(lambda e, bank=bank: e.matmul(bank.ap[:, 0:2 * NX], identb, maskb, start=True,
                                                            stop=False, skip_group_check=True))
                        for q in range(TPB):
                            k0 = q * (SEQ - NX)
                            filled[s] = pe.mark(lambda e, bank=bank, h=h, q=q, k0=k0: e.matmul(
                                bank.ap[:, NX * q:NX * (q + 1)], Q[0:kA, h, P * q:P * (q + 1)],
                                K[0:kA, h, k0:k0 + NX], start=False, stop=q == 1, skip_group_check=True))
                    w = NX
                else:
                    for r, q in order(alone):
                        bank = bankA[r]
                        pe.wait(*bank.free)
                        filled[r] = pe.mark(lambda e, bank=bank, r=r, q=q: e.matmul(
                            bank.ap[:, SEQ * q:SEQ * (q + 1)], Q[64 * r:64 * r + kA, u, P * q:P * (q + 1)],
                            K[64 * r:64 * r + kA, u, :], start=True, stop=True))
                    w = SEQ
                for s, bank in enumerate(bankA):
                    dst = mbuf[i][:, :, (hpu * u + s, H * s + u)[L]]
                    dve.wait(filled[s], *mfree[i])
                    a = dve.mark(lambda e, bank=bank, dst=dst: e.tensor_reduce(
                        dst, bank.ap[:, 0:2 * w].rearrange("p (q n) -> p q n", q=2), AX.X, ALU.max))
                    bank.free = [a]
                return a

            def split_max(b, ready):
                i = b % 2
                dve.wait(ready)
                a = dve.mark(lambda e: e.tensor_copy(M2[i][:, :, 0, 0:hh], mbuf[i][:, :, 0:hh]))
                dve.wait(a)
                a = dve.mark(lambda e: e.tensor_tensor(M2[i][:, :, 1, 0:hh], mbuf[i][:, :, 0:hh],
                                                       M2[i][:, :, 0, 0:hh], ALU.subtract))
                mfree[i] = [a]
                return a

            def place_max(b, ready):
                i, t = b % 2, MTs[b % 2]
                pe.wait(ready, *bankT.free)
                for k in range(2):
                    for q in range(TPB):
                        a = pe.mark(lambda e, k=k, q=q: e.transpose(
                            bankTb[32 * k:32 * k + hh, P * q:P * (q + 1)], M2[i][:, q, k, 0:hh], identb))
                dve.wait(a, *t.free)
                for k in range(2):
                    a = dve.mark(lambda e, k=k: e.tensor_copy(t.ap[32 * k:32 * k + hh, :],
                                                              bankTb[32 * k:32 * k + hh, 0:SEQ]))
                bankT.free = [a]
                key = "max", i
                g = groups_of.get(key) or group(f"max{L}_{i}")
                groups_of[key] = g
                sp.wait(a)
                for k in range(2):
                    sp.dma(g, lambda e, k=k: e.dma_start(Mx[L][b, k, :, :], t.ap[32 * k:32 * k + hh, :]))
                sp.wait(g.done())
                Q = Qst[(b + 2 * L) % 3]
                for r in range(halves):
                    sp.dma(g, lambda e, r=r: e.dma_start(Q[64 * r + kA:64 * r + kA + 2, :, :],
                                                         Mx[L][b, :, H * r:H * (r + 1), :]))
                t.free = [g.done()]
                st["max", b] = g.done()

            def second(n, alone):
                b, u = divmod(n, units)
                Q, K = Qst[(b + 2 * L) % 3], Kst[(b + 2 * L) % 3]
                pt = PT[count["pt"] % len(PT)]
                count["pt"] += 1
                pe.wait(st["max", b])
                filled = [None, None]
                if L == 0:
                    for s, bank in enumerate(bankB):
                        h = hpu * u + s
                        pe.wait(*bank.free)
                        pe.do(lambda e, bank=bank: e.matmul(bank.ap[:, 0:2 * NX], identb, maskb, start=True,
                                                            stop=False, skip_group_check=True))
                        for k in range(TPB):
                            q0 = k * (SEQ - NX)
                            filled[s] = pe.mark(lambda e, bank=bank, h=h, k=k, q0=q0: e.matmul(
                                bank.ap[:, NX * k:NX * (k + 1)], K[0:kB, h, P * k:P * (k + 1)],
                                Q[0:kB, h, q0:q0 + NX], start=False, stop=k == 1, skip_group_check=True))
                    w = 2 * NX
                else:
                    for r, k in order(alone):
                        bank = bankB[r]
                        pe.wait(*bank.free)
                        filled[r] = pe.mark(lambda e, bank=bank, r=r, k=k: e.matmul(
                            bank.ap[:, SEQ * k:SEQ * (k + 1)], K[64 * r:64 * r + kB, u, P * k:P * (k + 1)],
                            Q[64 * r:64 * r + kB, u, :], start=True, stop=True))
                    w = 2 * SEQ
                if u == units - 1:
                    stack_ready[(b + 2 * L) % 3] = [filled[1]]
                    st["last", b] = filled[1]
                    if b + 3 < NB:
                        load_stack(b + 3)
                act.wait(*pt.free)
                for s, bank in enumerate(bankB):
                    act.wait(filled[s])
                    a = act.mark(lambda e, s=s, bank=bank: e.activation(pt.ap[:, w * s:w * (s + 1)],
                                                                        bank.ap[:, 0:w], ACT.Exp))
                    bank.free = [a]
                made.append((pt, a))

            def values(b, grp, mine, slot):
                ot = OT[count["ot"] % 2]
                count["ot"] += 1
                width = SEQ * halves
                pe.wait(st["V", b // 2], *bankV.free, *(m for _, m in mine))
                for k in range(TPB):
                    for c in range(4):
                        pt, _ = mine[c // hpu]
                        h = 4 * grp + c
                        if L == 0:
                            q0 = k * (SEQ - NX)
                            at_ = (c % 2) * 2 * NX + NX * k
                            rhs = pt.ap[:, at_:at_ + NX]
                            out = bankV.ap[32 * c:32 * c + 32, q0:q0 + NX]
                        else:
                            rhs = pt.ap[:, :].rearrange("p (r k n) -> p r k n", r=2, k=2)[:, :, k, :]
                            out = bankV.ap[32 * c:32 * c + 32, :]
                        a = pe.mark(lambda e, k=k, h=h, rhs=rhs, out=out: e.matmul(
                            out, V[:, TPB * b + k, VW * h:VW * h + 32], rhs, start=k == 0, stop=k == 1,
                            skip_group_check=True))
                for pt, _ in mine:
                    pt.free = [a]
                if grp == 3:
                    V_read[b] = a
                act.wait(a, *ot.free)
                a = act.mark(lambda e: e.copy(ot.ap[:, 0:width], bankV.ap[:, 0:width]))
                bankV.free = [a]
                after(slot + 1, lambda: turn(b, grp, ot, a, slot + 1))

            def turn(b, grp, ot, ready, slot):
                nblk = halves * TPB
                o = Otok[(b + L * NB) % 2]
                pe.wait(ready, *bankT.free)
                for k in range(nblk):
                    a = pe.mark(lambda e, k=k: e.transpose(bankT.ap[:, P * k:P * (k + 1)],
                                                           ot.ap[:, P * k:P * (k + 1)], ident))
                ot.free = [a]
                act.wait(a, *o.free)
                a = act.mark(lambda e: e.copy(
                    o.ap[:, 0:nblk, 4 * grp:4 * grp + 4, :],
                    bankT.ap[:, 0:P * nblk].rearrange("p (k c v) -> p k c v", k=nblk, c=4)[:, :, :, 0:VW]))
                bankT.free = [a]
                if grp == 3:
                    after(slot + 1, lambda: divide(b, o, a, slot + 1))

            def divide(b, o, ready, slot):
                n = halves * TPB * H
                dve.wait(ready)
                r = dve.mark(lambda e: e.reciprocal(rec[:, 0:n].rearrange("p (k h) -> p k h", h=H),
                                                    o.ap[:, 0:halves * TPB, :, HD0]))
                dve.wait(r)
                num = o.ap[:, 0:halves * TPB, :, 0:HD0].rearrange("p k h v -> p (k h) v")
                rb_ = rec[:, 0:n].unsqueeze(2).to_broadcast([P, n, HD0])
                if L == 0:
                    r = dve.mark(lambda e: e.tensor_tensor(osc[:, 0:SEQ].rearrange("p (k v) -> p k v", v=HD0), num,
                                                           rb_, ALU.mult))
                    o.free = [r]
                    dve.wait(r, *(x_ready.get(TPB * b + t) for t in range(TPB)))
                    xb = x_tok[:, TPB * b:TPB * (b + 1), :].rearrange("p t f -> p (t f)")
                    r = dve.mark(lambda e: e.tensor_tensor(xb, xb, osc[:, 0:SEQ], ALU.add))
                    for t in range(TPB):
                        x_ready[TPB * b + t] = r
                    st["out", b] = r
                    return
                r = dve.mark(lambda e: e.tensor_scalar(rec[:, n // 2:n], rec[:, n // 2:n], lam[:, 13:14], None,
                                                       ALU.mult))
                dve.wait(r)
                r = dve.mark(lambda e: e.tensor_tensor(osc[:, :].rearrange("p (k v) -> p k v", v=HD0), num, rb_,
                                                       ALU.mult))
                o.free = [r]
                after(slot + 1, lambda: difference(b, r, slot + 1))

            half = TPB * H * HD0

            def difference(b, ready, slot):
                dve.wait(ready)
                r = dve.mark(lambda e: e.tensor_tensor(osc[:, 0:half], osc[:, 0:half], osc[:, half:2 * half], ALU.add))
                dve.wait(r)
                r = dve.mark(lambda e: e.tensor_tensor(sq[:, :], osc[:, 0:half], osc[:, 0:half], ALU.mult))
                after(slot + 1, lambda: mean_square(b, r, slot + 1))

            def mean_square(b, ready, slot):
                dve.wait(ready)
                r = dve.mark(lambda e: e.tensor_reduce(ms[:, :], sq[:, :].rearrange("p (k v) -> p k v", v=HD0),
                                                       AX.X, ALU.add))
                dve.wait(r)
                r = dve.mark(lambda e: e.tensor_scalar(ms[:, :], ms[:, :], 1.0 / HD0, EPS, ALU.mult, ALU.add))
                pool.wait(r)
                r = pool.mark(lambda e: e.tensor_tensor(ms[:, :], ms[:, :], halfneg[:, :], ALU.pow))
                after(slot + 4, lambda: normed(b, r, slot + 4))

            def normed(b, ready, slot):
                dve.wait(ready)
                r = dve.mark(lambda e: e.tensor_tensor(
                    sq[:, :].rearrange("p (k v) -> p k v", v=HD0), osc[:, 0:half].rearrange("p (k v) -> p k v", v=HD0),
                    ms[:, :].unsqueeze(2).to_broadcast([P, TPB * H, HD0]), ALU.mult))
                after(slot + 1, lambda: turn_out(b, r))

            def turn_out(b, ready):
                pe.wait(ready, *bankT.free)
                for q in range(TPB):
                    a = pe.mark(lambda e, q=q: e.transpose(bankT.ap[:, P * q:P * (q + 1)],
                                                           sq[:, P * q:P * (q + 1)], ident))
                act.wait(a, *q32s[1].free, *partss[1].free)
                a = act.mark(lambda e: e.copy(attn_tok[:, TPB * b:TPB * (b + 1), :].rearrange("p t f -> p (t f)"),
                                              bankT.ap[:, 0:SEQ]))
                dve.wait(a)
                bankT.free = [a]
                st["out", b] = a

            n, total = -lead, NB * units
            loaded_to = 0
            while n < total or due:
                while loaded_to < min(3, NB) and ("terms", loaded_to // 2) in st and (
                        stack_ready[(loaded_to + 2 * L) % 3] is not None) and (
                        L == 0 or ("last", 5 + loaded_to) in st0) and (
                        loaded_to < 2 or n + lead > units + 1):
                    load_stack(loaded_to)
                    loaded_to += 1
                    yield
                m = n + lead
                if L == 1 and n == 0 and "all" not in st0:
                    yield
                    continue
                if m < total and ("stack", m // units) not in st:
                    yield
                    continue
                if 0 <= n < total:
                    second(n, m >= total)
                    if L == 0:
                        yield
                if m < total:
                    a = first(m, n < 0)
                    if m % units == units - 1:
                        s_m = split_max(m // units, a)
                        after(n + 1, lambda b=m // units, s_m=s_m: place_max(b, s_m))
                if 0 <= n < total and n % ups == ups - 1:
                    b, u = divmod(n, units)
                    mine = made[:]
                    made.clear()
                    later = n + 1
                    after(later, lambda b=b, u=u, mine=mine, s_=later: values(b, u // ups, mine, s_))
                for step in due.pop(n, []):
                    step()
                n += 1
                yield
            st["all"] = True

        def route1():
            a = st1["logits", 3]
            lv = bank6.ap[:, 0:NT * E].rearrange("p (t e) -> p t e", e=E)
            dve.wait(a)
            a = dve.mark(lambda e: e.tensor_copy(lg[:, :, :], lv))
            bank6.free = [a]
            dve.wait(a)
            a = dve.mark(lambda e: e.tensor_reduce(mx[:, :], lg[:, :, :], AX.X, ALU.max))
            dve.wait(a)
            mxb = mx[:, :].unsqueeze(2).to_broadcast([P, NT, E])
            a = dve.mark(lambda e: e.tensor_tensor(pr[:, :, :], lg[:, :, :], mxb, ALU.subtract))
            yield
            act.wait(a)
            a = act.mark(lambda e: e.activation(pr[:, :, :], pr[:, :, :], ACT.Exp))
            yield
            dve.wait(a)
            a = dve.mark(lambda e: e.tensor_reduce(mx[:, :], pr[:, :, :], AX.X, ALU.add))
            dve.wait(a)
            a = dve.mark(lambda e: e.reciprocal(mx[:, :], mx[:, :]))
            dve.wait(a)
            a = dve.mark(lambda e: e.tensor_tensor(pr[:, :, :], pr[:, :, :], mxb, ALU.mult))
            a = yield from pick_first_max(lg[:, :, :], ohf[0][:, :, :], ohb[0][:, 0:NT, :], a)
            yield
            dve.wait(a)
            a = dve.mark(lambda e: e.tensor_scalar(tmp8[:, :, :], ohf[0][:, :, :], -BIG, None, ALU.mult))
            dve.wait(a)
            a = dve.mark(lambda e: e.tensor_tensor(lg[:, :, :], lg[:, :, :], tmp8[:, :, :], ALU.add))
            a = yield from pick_first_max(lg[:, :, :], ohf[1][:, :, :], ohb[1][:, 0:NT, :], a)
            ov = [ohb[k][:, 0:NT, :].rearrange("p (g t) e -> p t g e", t=TPB) for k in range(2)]
            pe.wait(a, *bank7.free)
            queue = [(0, 0), (0, 1), (1, 0), (1, 1)]
            for n, (k, t) in enumerate(queue):
                out = bank7.ap[:, 64 * n:64 * n + 64].rearrange("p (g e) -> p g e", e=E)
                pe.do(lambda e, k=k, t=t, out=out, n=n: e.matmul(out, before, ov[k][:, t, :, :], start=True,
                                                               stop=n == 0, skip_group_check=True))
                for m, (k2, t2) in enumerate(queue[:n]):
                    a = pe.mark(lambda e, k2=k2, t2=t2, out=out, m=m, n=n: e.matmul(
                        out, onesb, ov[k2][:, t2, :, :], start=False, stop=m == n - 1, skip_group_check=True))
            yield
            dve.wait(a)
            r4 = bank7.ap[:, 0:256].rearrange("p (k t g e) -> p k g t e", k=2, t=TPB, e=E)
            for k in range(2):
                dst = rank[:, NT * k:NT * (k + 1), :]
                for t in range(TPB):
                    a = dve.mark(lambda e, k=k, t=t, dst=dst: e.tensor_scalar(
                        dst.rearrange("p (g t) e -> p t g e", t=TPB)[:, t, :, :], r4[:, k, :, t, :], 1.0, None, ALU.add))
                dve.wait(a)
                a = dve.mark(lambda e, k=k, dst=dst: e.tensor_tensor(dst, dst, ohf[k][:, :, :], ALU.mult))
            bank7.free = [a]
            yield
            dve.wait(a)
            a = dve.mark(lambda e: e.tensor_tensor(posm[:, :, :], rank[:, 0:NT, :], rank[:, NT:2 * NT, :], ALU.add))
            dve.wait(a)
            a = dve.mark(lambda e: e.tensor_scalar(posm[:, :, :], posm[:, :, :], -1.0, None, ALU.add))
            yield
            return a

        gfree = [[], []]
        Dm = [Buffer(tmpA[:, k, :]) for k in range(2)]
        gq = [Buffer(tmpA[:, 5 + k, :]) for k in range(2)]
        iob = iota.unsqueeze(1).to_broadcast([P, E, CAP])

        def one_hot(i, n, routed):
            b = Dm[n % 2]
            dve.wait(routed, *b.free)
            return b, dve.mark(lambda e, b=b, i=i: e.tensor_tensor(
                b.ap.rearrange("p (e c) -> p e c", e=E), iob,
                posm[:, i, :].unsqueeze(2).to_broadcast([P, E, CAP]), ALU.is_equal))

        def experts1(routed):
            banks = (bank6, bank7)
            n = 0
            for g in range(NB):
                bank = banks[g % 2]
                for t in range(TPB):
                    b, a = one_hot(TPB * g + t, n, routed)
                    n += 1
                    yield
                    pe.wait(a, *bank.free)
                    a = pe.mark(lambda e, g=g, t=t, b=b, bank=bank: e.matmul(
                        bank.ap, xn1_tok[:, TPB * g + t, :], b.ap, start=t == 0, stop=t == 1))
                    b.free = [a]
                act.wait(a)
                ex = act.mark(lambda e, g=g, bank=bank: e.copy(XE[:, g, :, :],
                                                              bank.ap.rearrange("p (e c) -> p e c", e=E)))
                bank.free = [ex]
            last_read = a
            while ("terms", 3) not in st1:
                yield
            gfree[:] = [[last_read], [st1["x_read", c] for c in range(4)] + [routed]]
            n = 0
            state = {}

            def hidden(j):
                (e_, f), bank, u = divmod(j, FC), banks[j % 2], gq[j % 2]
                pe.wait(ex, w_e1, *bank.free)
                a = pe.mark(lambda e: e.matmul(bank.ap, wi[:, e_, P * f:P * (f + 1)], XE[:, :, e_, :],
                                               start=True, stop=True))
                act.wait(a, *u.free)
                state[j] = act.mark(lambda e: e.activation(u.ap, bank.ap, ACT.Square, scale=float(np.sqrt(GELU_A))))

            def inner(j):
                bank, u = banks[j % 2], gq[j % 2]
                dve.wait(state[j])
                state[j] = dve.mark(lambda e: e.scalar_tensor_tensor(u.ap, u.ap, 1.0, bank.ap, ALU.add, ALU.mult))

            def tanh(j):
                u = gq[j % 2]
                act.wait(state[j])
                state[j] = act.mark(lambda e: e.activation(u.ap, u.ap, ACT.Tanh, scale=GELU_C))

            def outer(j):
                (e_, f), bank, u = divmod(j, FC), banks[j % 2], gq[j % 2]
                dve.wait(state[j], *gfree[e_ % 2])
                a = dve.mark(lambda e: e.scalar_tensor_tensor(G[:, e_ % 2, f, :], u.ap, 1.0, bank.ap,
                                                              ALU.add, ALU.mult))
                bank.free, u.free = [a], [a]
                state[j] = a

            def result(j):
                e_, f = divmod(j, FC)
                pe.wait(state[j], *(bankM.free if f == 0 else []))
                a = pe.mark(lambda e: e.matmul(bankM.ap, wo[:, e_, f, :], G[:, e_ % 2, f, :],
                                               start=f == 0, stop=f == FC - 1))
                if f == FC - 1:
                    gfree[e_ % 2] = [a]
                    act.wait(a)
                    a = act.mark(lambda e: e.mul(XE[:, :, e_, :], bankM.ap.rearrange("p (g c) -> p g c", g=NB), 0.5))
                    bankM.free = [a]
                    experts1.done = a

            jobs = E * FC
            for s in range(0, 2 * jobs + 2 * FC + 2, 2):
                j = s // 2
                if 1 <= j <= jobs:
                    tanh(j - 1)
                if j < jobs:
                    hidden(j)
                yield
                if 1 <= j <= jobs:
                    outer(j - 1)
                if j < jobs:
                    inner(j)
                if j >= FC + 1:
                    result(j - FC - 1)
                yield

        gates_T = [[Buffer(tmpA[:, 2 + t, :]) for t in range(TPB)], [Buffer(G[:, 0, t, :]) for t in range(TPB)]]
        Yg = [Buffer(tmpA[:, 4, :]), Buffer(G[:, 0, 2, :])]
        made_ready, stored = {}, {}

        def make_ready(routed):
            for b in range(NB):
                while b >= 2 and b - 2 not in stored:
                    yield
                y = Yg[b % 2]
                pe.wait(experts1.done, *bank6.free)
                for k in range(4):
                    a = pe.mark(lambda e, k=k, b=b: e.transpose(
                        bank6.ap[:, P * k:P * (k + 1)], XE[:, b, 2 * k:2 * k + 2, :].rearrange("p e c -> p (e c)"),
                        ident))
                act.wait(a, *y.free, *gfree[0])
                ym = act.mark(lambda e, y=y: e.copy(y.ap, bank6.ap))
                bank6.free = [ym]
                turned = []
                for t in range(TPB):
                    i = TPB * b + t
                    dm, a = one_hot(i, t, routed)
                    yield
                    dve.wait(a)
                    a = dve.mark(lambda e, i=i, dm=dm: e.tensor_tensor(
                        dm.ap.rearrange("p (e c) -> p e c", e=E), dm.ap.rearrange("p (e c) -> p e c", e=E),
                        pr[:, i, :].unsqueeze(2).to_broadcast([P, E, CAP]), ALU.mult))
                    yield
                    pe.wait(a, *bank7.free)
                    for k in range(4):
                        a = pe.mark(lambda e, k=k, dm=dm: e.transpose(bank7.ap[:, P * k:P * (k + 1)],
                                                                      dm.ap[:, P * k:P * (k + 1)], ident))
                    dm.free = [a]
                    ct = gates_T[b % 2][t]
                    act.wait(a, *ct.free)
                    a = act.mark(lambda e, ct=ct: e.copy(ct.ap, bank7.ap))
                    bank7.free = [a]
                    turned.append(a)
                    yield
                made_ready[b] = turned, ym

        def combine():
            for b in range(NB):
                while b not in made_ready:
                    yield
                turned, ym = made_ready[b]
                y = Yg[b % 2]
                for t in range(TPB):
                    ct, ob = gates_T[b % 2][t], bankM.ap[:, P * t:P * (t + 1)]
                    pe.wait(turned[t], ym, *(bankM.free if t == 0 else []))
                    for k in range(4):
                        a = pe.mark(lambda e, k=k, t=t, ct=ct, y=y, ob=ob: e.matmul(
                            ob, ct.ap[:, P * k:P * (k + 1)], y.ap[:, P * k:P * (k + 1)], start=k == 0 and t == 0,
                            stop=False, skip_group_check=True))
                    ct.free = [a]
                    yield
                y.free = [a]
                while ("out", b) not in st1:
                    yield
                pe.wait(st1["out", b], late["wo"])
                for t in range(TPB):
                    a = pe.mark(lambda e, i=TPB * b + t, t=t: e.matmul(
                        bankM.ap[:, P * t:P * (t + 1)], attn_tok[:, i, :], wsmall[:, 6, :], start=False,
                        stop=t == TPB - 1, skip_group_check=True))
                dve.wait(a)
                xb = x_tok[:, TPB * b:TPB * (b + 1), :]
                a = dve.mark(lambda e, xb=xb: e.tensor_tensor(
                    xb, xb, bankM.ap[:, 0:SEQ].rearrange("p (t f) -> p t f", t=TPB), ALU.add))
                bankM.free = [a]
                stored[b] = True
                sp.wait(a)
                sp.dma(g_out, lambda e, b=b, xb=xb: e.dma_start(d["out"][b].rearrange("(t p) c -> p t c", p=P), xb))
                yield

        def run(*tasks):
            live = [[t, n, 0.0] for t, n in tasks]
            while live:
                for entry in list(live):
                    entry[2] += entry[1]
                    while entry[2] >= 1:
                        entry[2] -= 1
                        if next(entry[0], "end") == "end":
                            live.remove(entry)
                            break

        st0, st1 = {}, {}
        g_out = group("store_out")

        def projections0():
            for c in range(4):
                while c not in ln_done:
                    yield
                yield from project(0, c, xnT, st0)

        def routing0():
            norms = [layer_norm(c, [x_in[c]], xn_tok, xnT) for c in range(4)]
            for t in norms:
                next(t)
            fill_stacks()
            stack_ready[0] = stack_ready[1] = m_set
            yield from side_by_side(*norms)
            yield from route0()

        def front0():
            yield from side_by_side(routing0(), projections0(), set_up_late())
            te_m, scattered = st0["routed"]
            pool.wait(scattered, *(st0["x_read", c] for c in range(4)), te_m)
            pool.do(lambda e: e.memset(Qst[2], 0.0))
            stack_ready[2] = [pool.mark(lambda e: e.memset(Kst[2], -1.0))]
            yield

        def layer0_experts():
            while "routed" not in st0:
                yield
            for _ in range(E0_DELAY):
                yield
            yield from experts0(*st0["routed"])

        def slowly(task, pause):
            while next(task, "end") != "end":
                for _ in range(1 + pause):
                    yield

        def norms1():
            for c in range(4):
                while ("out", 2 * c + 1) not in st0 or ("added", c) not in st0:
                    yield
                ready = [x_ready[i] for i in range(4 * c, 4 * c + 4)]
                yield from slowly(layer_norm(c, ready, xn1_tok, xnT1), S1)
                st1["normed", c] = True
                st1["logits", c] = logits(1, c, xnT1, bank6)
                yield

        def projections1():
            for c in range(4):
                while ("normed", c) not in st1:
                    yield
                yield from slowly(project(1, c, xnT1, st1), S1)

        def front1():
            yield from side_by_side(norms1(), projections1())

        def layer1_experts():
            while ("logits", 3) not in st1:
                yield
            routed = yield from route1()
            yield from experts1(routed)
            yield from side_by_side(make_ready(routed), combine())

        run((front0(), F0), (attention(0, st0), 1), (layer0_experts(), E0_PACE), (front1(), F1),
            (attention(1, st1), A1_PACE), (layer1_experts(), E1_PACE))
        for g in groups:
            sp.wait(g.done())

        block = ctx.enter_context(nc.Block())

        @block.sync
        def _(e):
            sp.play(e)

        @block.gpsimd
        def _(e):
            pool.play(e)

        @block.vector
        def _(e):
            dve.play(e)

        @block.scalar
        def _(e):
            act.play(e)

        @block.tensor
        def _(e):
            pe.play(e)


def kernel(**inputs):
    import concourse.bacc as bacc
    from concourse.bass_utils import run_bass_kernel_spmd

    a = {k: np.asarray(v) for k, v in inputs.items()}
    o0 = np.arange(D).reshape(H, HD0).T.ravel()
    o1 = np.arange(D).reshape(H, 2, HD1).transpose(2, 1, 0).ravel()
    lay = {
        "x": a["L0_attn_hidden_states"],
        "cf": constants_f32(),
        "cb": constants_masks(),
        "wsmall": np.stack([a["L0_attn_Wq"][:, o0], a["L0_attn_Wk"][:, o0], a["L0_attn_Wv"],
                            a["L1_attn_Wq"].T[:, o1], a["L1_attn_Wk"].T[:, o1], a["L1_attn_Wv"].T, a["L1_attn_Wo"].T], axis=1),
        "wr": np.stack([a["L0_ffn_router_w"], a["L1_ffn_w_router"]], axis=1),
        "rb": np.tile(a["L0_ffn_router_b"][None, :], (P, 1)),
        "bqk": np.stack([a["L0_attn_bq"][o0], a["L0_attn_bk"][o0]], axis=1),
        "bvb": np.tile(a["L0_attn_bv"][None, :], (P, 1)),
        "lamv": np.tile(np.stack([a["L1_attn_lambda_q1"], a["L1_attn_lambda_k1"], a["L1_attn_lambda_q2"],
                                  a["L1_attn_lambda_k2"]])[None], (P, 1, 1)),
        "subln": np.tile(a["L1_attn_subln_w"], H)[:, None],
        "bias": np.concatenate([a["L0_ffn_b1"].reshape(P, 64), a["L0_ffn_b2"].reshape(P, 8)], axis=1),
        "w1": a["L0_ffn_w1"], "w2": a["L0_ffn_w2"], "wi": a["L1_ffn_wi"], "wo_e": a["L1_ffn_wo"],
    }
    lay = {k: np.ascontiguousarray(v) for k, v in lay.items()}
    nc = bacc.Bacc("TRN2", target_bir_lowering=False, num_devices=1)
    d = {k: nc.dram_tensor(f"in_{k}", v.shape, mybir.dt.from_np(v.dtype), kind="ExternalInput").ap()
         for k, v in lay.items()}
    d["out"] = nc.dram_tensor("out", (NB, SEQ, D), F32, kind="ExternalOutput").ap()
    build(nc, d)
    r = run_bass_kernel_spmd(nc, [{f"in_{k}": v for k, v in lay.items()}], core_ids=[0])
    return r.results[0]["out"]
```
